# Optimizing a Trainium2 kernel written in Bass

```python
import numpy as np
import jax
import jax.numpy as jnp

def _softmax(x, axis=-1):
    return jax.nn.softmax(x, axis=axis)

def _gelu(x):
    return jax.nn.gelu(x, approximate=True)

def _silu(x):
    return jax.nn.silu(x)

def _sigmoid(x):
    return jax.nn.sigmoid(x)

def _layernorm(x, axis=-1, eps=1e-05):
    m = jnp.mean(x, axis=axis, keepdims=True)
    v = jnp.var(x, axis=axis, keepdims=True)
    return (x - m) / jnp.sqrt(v + eps)

def _scatter_add(tgt, idx, src, axis=0):
    return tgt.at[idx].add(src)

def _segment_sum(src, seg, n):
    return jax.ops.segment_sum(src, seg, n)
kernel_name = 'mk_conv_attn_hybrid_d2_conv_nchw256_r2_5fb6e2'

def setup_inputs(seed: int=0):
    np.random.seed(seed)
    _w = jnp.asarray

    def _rec_inputs():
        import jax
        import jax.numpy as jnp
        _gk = jax.random.key(seed)
        x = -0.0005207 + 1.001 * jax.random.normal(jax.random.fold_in(_gk, 1), (8, 128, 32, 32), jnp.float32)
        return x
    x = _rec_inputs()

    def _L0_conv_setup():
        import jax, jax.numpy as jnp
        import numpy as np
        B, C, H, W = (8, 128, 32, 32)
        N_HEAD = 4
        EPS = 1e-05
        key = jax.random.key(seed)
        ks = jax.random.split(key, 8)
        return {'input': jax.random.normal(ks[0], (B, C, H, W), dtype=jnp.float32), 'bn_gamma': jnp.ones((C,), dtype=jnp.float32), 'bn_beta': jnp.zeros((C,), dtype=jnp.float32), 'bn_mean': jax.random.normal(ks[1], (C,), dtype=jnp.float32) * 0.1, 'bn_var': jax.random.uniform(ks[2], (C,), dtype=jnp.float32, minval=0.5, maxval=1.5), 'dw_w': jax.random.normal(ks[3], (C,), dtype=jnp.float32) * (1.0 / np.sqrt(C)), 'pw_w': jax.random.normal(ks[4], (3 * C, C), dtype=jnp.float32) * (1.0 / np.sqrt(C)), 'out_w': jax.random.normal(ks[5], (C, C), dtype=jnp.float32) * (1.0 / np.sqrt(C)), 'out_b': jnp.zeros((C,), dtype=jnp.float32)}
    _L0_conv_all = _L0_conv_setup()
    _L0_conv_in = {k: v for k, v in _L0_conv_all.items() if k in ('bn_gamma', 'bn_beta', 'bn_mean', 'bn_var', 'dw_w', 'pw_w', 'out_w', 'out_b')}
    del _L0_conv_all

    def _L1_attn_setup():
        import jax, jax.numpy as jnp
        import numpy as np
        EPS = 1e-06

        def _rmsnorm(x, w):
            xf = x.astype(jnp.float32)
            y = xf * jax.lax.rsqrt(jnp.mean(xf * xf, axis=-1, keepdims=True) + EPS)
            return y.astype(x.dtype) * w
        key = jax.random.key(seed)
        k0, k1, k2 = jax.random.split(key, 3)
        B, T, C = (2, 512, 128)
        x = jax.random.normal(k0, (B, T, C), jnp.float32)
        w_qkv = jax.random.normal(k1, (3 * C, C), jnp.float32) / np.float32(np.sqrt(C))
        w_proj = jax.random.normal(k2, (C, C), jnp.float32) / np.float32(np.sqrt(C))
        qn_w = jnp.ones((2,), jnp.float32)
        kn_w = jnp.ones((2,), jnp.float32)
        return {'x': x, 'w_qkv': w_qkv, 'w_proj': w_proj, 'qn_w': qn_w, 'kn_w': kn_w}
    _L1_attn_all = _L1_attn_setup()
    _L1_attn_in = {k: v for k, v in _L1_attn_all.items() if k in ('w_qkv', 'w_proj', 'qn_w', 'kn_w')}
    del _L1_attn_all

    def _L1_ffn_setup():
        import jax, jax.numpy as jnp
        import numpy as np
        BN_EPS = 0.001

        def _bn(h, g, b, m, v):
            return g * (h - m) * jax.lax.rsqrt(v + BN_EPS) + b
        key = jax.random.key(seed)
        ks = jax.random.split(key, 8)
        B, F, Df = (128, 32, 128)
        E, H, D = (8, 128, 128)
        s1 = 1.0 / np.sqrt(Df)
        s2 = 1.0 / np.sqrt(H)
        return {'x': jax.random.normal(ks[0], (B, F, Df), jnp.float32), 'Wr': jax.random.normal(ks[1], (Df, E), jnp.float32) * s1, 'br': jnp.zeros((E,), jnp.float32), 'W1': jax.random.normal(ks[2], (E, Df, H), jnp.float32) * s1, 'b1': jnp.zeros((E, H), jnp.float32), 'g1': jnp.ones((E, H), jnp.float32), 'be1': jnp.zeros((E, H), jnp.float32), 'm1': jnp.zeros((E, H), jnp.float32), 'v1': jnp.ones((E, H), jnp.float32), 'W2': jax.random.normal(ks[3], (E, H, H), jnp.float32) * s2, 'b2': jnp.zeros((E, H), jnp.float32), 'g2': jnp.ones((E, H), jnp.float32), 'be2': jnp.zeros((E, H), jnp.float32), 'm2': jnp.zeros((E, H), jnp.float32), 'v2': jnp.ones((E, H), jnp.float32), 'Wo': jax.random.normal(ks[4], (E, H, D), jnp.float32) * s2, 'bo': jnp.zeros((E, D), jnp.float32)}
    _L1_ffn_all = _L1_ffn_setup()
    _L1_ffn_in = {k: v for k, v in _L1_ffn_all.items() if k in ('Wr', 'br', 'W1', 'b1', 'g1', 'be1', 'm1', 'v1', 'W2', 'b2', 'g2', 'be2', 'm2', 'v2', 'Wo', 'bo')}
    del _L1_ffn_all
    return {'x': x, 'L0_conv_bn_gamma': _L0_conv_in['bn_gamma'], 'L0_conv_bn_beta': _L0_conv_in['bn_beta'], 'L0_conv_bn_mean': _L0_conv_in['bn_mean'], 'L0_conv_bn_var': _L0_conv_in['bn_var'], 'L0_conv_dw_w': _L0_conv_in['dw_w'], 'L0_conv_pw_w': _L0_conv_in['pw_w'], 'L0_conv_out_w': _L0_conv_in['out_w'], 'L0_conv_out_b': _L0_conv_in['out_b'], 'L1_attn_w_qkv': _L1_attn_in['w_qkv'], 'L1_attn_w_proj': _L1_attn_in['w_proj'], 'L1_attn_qn_w': _L1_attn_in['qn_w'], 'L1_attn_kn_w': _L1_attn_in['kn_w'], 'L1_ffn_Wr': _L1_ffn_in['Wr'], 'L1_ffn_br': _L1_ffn_in['br'], 'L1_ffn_W1': _L1_ffn_in['W1'], 'L1_ffn_b1': _L1_ffn_in['b1'], 'L1_ffn_g1': _L1_ffn_in['g1'], 'L1_ffn_be1': _L1_ffn_in['be1'], 'L1_ffn_m1': _L1_ffn_in['m1'], 'L1_ffn_v1': _L1_ffn_in['v1'], 'L1_ffn_W2': _L1_ffn_in['W2'], 'L1_ffn_b2': _L1_ffn_in['b2'], 'L1_ffn_g2': _L1_ffn_in['g2'], 'L1_ffn_be2': _L1_ffn_in['be2'], 'L1_ffn_m2': _L1_ffn_in['m2'], 'L1_ffn_v2': _L1_ffn_in['v2'], 'L1_ffn_Wo': _L1_ffn_in['Wo'], 'L1_ffn_bo': _L1_ffn_in['bo']}

def reference(x, L0_conv_bn_gamma, L0_conv_bn_beta, L0_conv_bn_mean, L0_conv_bn_var, L0_conv_dw_w, L0_conv_pw_w, L0_conv_out_w, L0_conv_out_b, L1_attn_w_qkv, L1_attn_w_proj, L1_attn_qn_w, L1_attn_kn_w, L1_ffn_Wr, L1_ffn_br, L1_ffn_W1, L1_ffn_b1, L1_ffn_g1, L1_ffn_be1, L1_ffn_m1, L1_ffn_v1, L1_ffn_W2, L1_ffn_b2, L1_ffn_g2, L1_ffn_be2, L1_ffn_m2, L1_ffn_v2, L1_ffn_Wo, L1_ffn_bo):
    import jax
    import jax.numpy as jnp

    def _L0_conv_ref(input, bn_gamma, bn_beta, bn_mean, bn_var, dw_w, pw_w, out_w, out_b):
        import jax, jax.numpy as jnp
        import numpy as np
        B, C, H, W = (8, 128, 32, 32)
        N_HEAD = 4
        EPS = 1e-05
        b, c, h, w = input.shape
        n_head = N_HEAD
        head_dim = c // n_head
        scale = (bn_gamma * jax.lax.rsqrt(bn_var + EPS) * dw_w)[None, :, None, None]
        shift = (bn_beta * dw_w)[None, :, None, None]
        mean = bn_mean[None, :, None, None]
        x = (input - mean) * scale + shift
        qkv = jnp.einsum('oc,bchw->bohw', pw_w, x)
        qkv = qkv.reshape(b, n_head, head_dim * 3, h, w)
        q, k, v = jnp.split(qkv, 3, axis=2)
        attn = jnp.einsum('bnchw,bncyx->bnhwyx', q, k) * (1.0 / np.sqrt(head_dim))
        attn = jax.nn.softmax(attn, axis=-1)
        out = jnp.einsum('bnhwyx,bncyx->bnchw', attn, v).reshape(b, c, h, w)
        out = jnp.einsum('oc,bchw->bohw', out_w, out) + out_b[None, :, None, None]
        return out + input

    def _L1_attn_ref(x, w_qkv, w_proj, qn_w, kn_w):
        import jax, jax.numpy as jnp
        import numpy as np
        EPS = 1e-06

        def _rmsnorm(x, w):
            xf = x.astype(jnp.float32)
            y = xf * jax.lax.rsqrt(jnp.mean(xf * xf, axis=-1, keepdims=True) + EPS)
            return y.astype(x.dtype) * w
        B, T, C = x.shape
        HD = 2
        H = C // HD
        qkv = x @ w_qkv.T
        q, k, v = jnp.split(qkv, 3, axis=-1)
        heads = lambda t: t.reshape(B, T, H, HD).transpose(0, 2, 1, 3)
        q = _rmsnorm(heads(q), qn_w)
        k = _rmsnorm(heads(k), kn_w)
        v = heads(v)
        scale = np.float32(1.0 / np.sqrt(HD))
        att = jnp.einsum('bhtd,bhsd->bhts', q, k) * scale
        causal = jnp.tril(jnp.ones((T, T), bool))
        att = jnp.where(causal, att, jnp.float32(-1e+30))
        att = jax.nn.softmax(att, axis=-1)
        y = jnp.einsum('bhts,bhsd->bhtd', att, v)
        y = y.transpose(0, 2, 1, 3).reshape(B, T, C)
        return y @ w_proj.T

    def _L1_ffn_ref(x, Wr, br, W1, b1, g1, be1, m1, v1, W2, b2, g2, be2, m2, v2, Wo, bo):
        import jax, jax.numpy as jnp
        import numpy as np
        BN_EPS = 0.001

        def _bn(h, g, b, m, v):
            return g * (h - m) * jax.lax.rsqrt(v + BN_EPS) + b
        feat = jnp.mean(x, axis=0)
        w = jax.nn.softmax(feat @ Wr + br, axis=-1)
        h = jnp.einsum('bfd,edh->bfeh', x, W1) + b1
        h = jax.nn.relu(_bn(h, g1, be1, m1, v1))
        h = jnp.einsum('bfeh,ehk->bfek', h, W2) + b2
        h = jax.nn.relu(_bn(h, g2, be2, m2, v2))
        y = jnp.einsum('bfeh,ehd->bfed', h, Wo) + bo
        return jnp.einsum('bfed,fe->bfd', y, w)

    def _gn(v, G=32, eps=1e-05):
        B_, C_, H_, W_ = v.shape
        g = v.reshape(B_, G, C_ // G, H_, W_)
        m = jnp.mean(g, axis=(2, 3, 4), keepdims=True)
        s = jnp.var(g, axis=(2, 3, 4), keepdims=True)
        return ((g - m) / jnp.sqrt(s + eps)).reshape(v.shape)

    def _ln_c(v, eps=1e-06):
        m = jnp.mean(v, axis=1, keepdims=True)
        s = jnp.var(v, axis=1, keepdims=True)
        return (v - m) / jnp.sqrt(s + eps)

    def _ln_t(v, eps=1e-05):
        m = jnp.mean(v, axis=-1, keepdims=True)
        s = jnp.var(v, axis=-1, keepdims=True)
        return (v - m) / jnp.sqrt(s + eps)

    def _to_tokens(v):
        B_, C_, H_, W_ = v.shape
        return v.reshape(B_, C_, H_ * W_).transpose(0, 2, 1)

    def _from_tokens(t, like):
        B_, C_, H_, W_ = like.shape
        return t.transpose(0, 2, 1).reshape(B_, C_, H_, W_)
    x = _L0_conv_ref(x, L0_conv_bn_gamma, L0_conv_bn_beta, L0_conv_bn_mean, L0_conv_bn_var, L0_conv_dw_w, L0_conv_pw_w, L0_conv_out_w, L0_conv_out_b)
    t = _to_tokens(x)
    t = t + _L1_attn_ref(_ln_t(t), L1_attn_w_qkv, L1_attn_w_proj, L1_attn_qn_w, L1_attn_kn_w)
    t = t + _L1_ffn_ref(_ln_t(t), L1_ffn_Wr, L1_ffn_br, L1_ffn_W1, L1_ffn_b1, L1_ffn_g1, L1_ffn_be1, L1_ffn_m1, L1_ffn_v1, L1_ffn_W2, L1_ffn_b2, L1_ffn_g2, L1_ffn_be2, L1_ffn_m2, L1_ffn_v2, L1_ffn_Wo, L1_ffn_bo)
    x = _from_tokens(t, x)
    return x

_drawn_inputs = setup_inputs


def setup_inputs(seed=0):
    import zlib

    import numpy as np

    out = dict(_drawn_inputs(seed))
    spreads = {'L0_conv_bn_gamma': (1.0, 0.2),
     'L0_conv_bn_beta': (0.0, 0.1),
     'L0_conv_out_b': (0.0, 0.1),
     'L1_attn_qn_w': (1.0, 0.6),
     'L1_attn_kn_w': (1.0, 0.6),
     'L1_ffn_br': (0.0, 0.624),
     'L1_ffn_b1': (0.0, 0.381),
     'L1_ffn_g1': (1.0, 0.2),
     'L1_ffn_be1': (0.0, 0.455),
     'L1_ffn_m1': (0.0, 0.443),
     'L1_ffn_v1': (1.0, 0.6),
     'L1_ffn_b2': (0.0, 0.318),
     'L1_ffn_g2': (1.0, 0.2),
     'L1_ffn_be2': (0.0, 0.326),
     'L1_ffn_m2': (0.0, 0.315),
     'L1_ffn_v2': (1.0, 0.6),
     'L1_ffn_bo': (0.0, 0.1)}
    factors = {}
    for name, (base, spread) in spreads.items():
        noise = np.random.default_rng([zlib.crc32(name.encode()), seed]).standard_normal(out[name].shape)
        drawn = base * np.exp(spread * noise) if base else spread * noise
        out[name] = jnp.asarray(drawn.astype(out[name].dtype))
    for name, factor in factors.items():
        out[name] = (out[name] * factor).astype(out[name].dtype)
    return out
```

```python
from contextlib import ExitStack

import concourse.bass as bass
from concourse import mybir

F32 = mybir.dt.float32
BF16 = mybir.dt.bfloat16
ACT = mybir.ActivationFunctionType
ALU = mybir.AluOpType
AX_X = mybir.AxisListType.X
ds = bass.ds

P = 128
B = 8
H = W = 32
T = H * W
HALF = T // 2
NT = T // P
NH0 = 4
D0 = P // NH0
NH1 = P // 2
NHB = B * NH1
NE = 8
HG = 4
NG = NHB // HG
BN_EPS0 = 1e-5
LN_EPS = 1e-5
RMS_EPS = 1e-6
BN_EPS = 1e-3
SCALE0 = D0 ** -0.5
SCALE1 = 2 ** -0.5
GUARD = 60.0
BIG = 3.0e38

INC = 16

QS = 256
STEPS = T // QS
SUB = 8
TURN = 2 * STEPS * SUB
GK = W
RB = P // GK
L_MOVE = NH0
L_EXP = 9
L_SUM = 10
L_NORM = 23
L_PV = 24
L_OUT = L_PV + SUB
TAIL = L_OUT

STACK = 12
QROWS, KROWS = STACK + 3, STACK

UNITS = [(j, t) for j in range(NT) for t in range(j, NT)]
UPC = 3
CHUNKS = [UNITS[i:i + UPC] for i in range(0, len(UNITS), UPC)]
NC = len(CHUNKS)
CW = UPC * HG * P
PRING = 6
VW = 44


def runs(chunk, split_half):
    out = []
    for i, (j, t) in enumerate(chunk):
        if out and out[-1][1] == j and out[-1][2] + out[-1][3] == t and not (
                split_half and t == NT // 2):
            out[-1][3] += 1
        else:
            out.append([i, j, t, 1])
    return out


CHUNK_A = max(c for c, ch in enumerate(CHUNKS) if any(t < NT // 2 for _, t in ch))

PARAMS = ["L1_ffn_b1", "L1_ffn_g1", "L1_ffn_be1", "L1_ffn_m1", "L1_ffn_v1",
          "L1_ffn_b2", "L1_ffn_g2", "L1_ffn_be2", "L1_ffn_m2", "L1_ffn_v2"]
VECTORS = ["L0_conv_bn_gamma", "L0_conv_bn_beta", "L0_conv_bn_mean", "L0_conv_bn_var",
           "L0_conv_dw_w", "L0_conv_out_b"]
NPR = NE * len(PARAMS) + len(VECTORS)


def hybrid_kernel(nc, a, out):
    x_v = a["x"].rearrange("b c h w -> c b (h w)")
    out_v = out.rearrange("b c h w -> c b (h w)")

    parts0 = nc.dram_tensor("parts0", (B, 6, P, T), BF16, kind="Internal").ap()
    values0 = nc.dram_tensor("values0", (B, P, T), F32, kind="Internal").ap()
    qstack = nc.dram_tensor("qstack", (QROWS, NHB, T), BF16, kind="Internal").ap()
    kstack = nc.dram_tensor("kstack", (KROWS, NHB, T), BF16, kind="Internal").ap()
    attn1 = nc.dram_tensor("attn1", (NHB, 3, T), F32, kind="Internal").ap()

    with ExitStack() as ctx:
        def sb(name, shape, dt=F32):
            return ctx.enter_context(nc.sbuf_tensor(name, shape, dt))

        def sem(name):
            return ctx.enter_context(nc.semaphore(name))

        X = sb("X", [P, B, T])
        WT = sb("WT", [P, 8 * P])
        ident = sb("ident", [P, P])
        mean_w = sb("mean_w", [P, P])
        causal = sb("causal", [P, P])
        PT = sb("PT", [P, NPR])
        CV = sb("CV", [P, 64])
        qkw = sb("qkw", [P, 4])
        br_b = sb("br_b", [P, NE])
        Wr = sb("Wr", [P, NE])
        bo = sb("bo", [NE, P])
        eps_c = sb("eps_c", [P, 5])
        Yall = sb("Yall", [P, B, T])
        arena_bytes = 136 * 1024
        arena = sb("arena", [P, arena_bytes // 4])

        class Cut:
            def __init__(self, at=0):
                self.at = at

            def __call__(self, shape, dt=F32):
                n = 1
                for s in shape:
                    n *= s
                size = 2 if dt == BF16 else 4
                words = (n * size + 3) // 4
                start = self.at // 4
                self.at += words * 4
                assert self.at <= arena_bytes, self.at
                ap = arena[:, start:start + words]
                if dt != F32:
                    ap = ap.bitcast(dt)
                names = [f"d{i}" for i in range(len(shape))]
                if len(shape) > 1:
                    ap = ap.rearrange("p (" + " ".join(names) + ") -> p " + " ".join(names),
                                      **dict(zip(names[1:], shape[1:])))
                return ap

        cut = Cut()
        WR = cut([8, P])
        PRr = cut([P])
        cut = Cut(8 * 1024)
        xbn = [cut([T]) for _ in range(2)]
        parts = [cut([6, T], BF16) for _ in range(2)]
        rest0 = [cut([T]) for _ in range(2)]
        v_out = [cut([T]) for _ in range(2)]
        cut = Cut()
        E0 = [cut([NT, NH0, QS]) for _ in range(2)]
        K1, K2 = [[cut([NH0, T], BF16) for _ in range(2)] for _ in range(2)]
        Q1, Q2 = [[cut([NH0, HALF], BF16) for _ in range(2)] for _ in range(2)]
        V0 = [cut([T]) for _ in range(2)]
        RS = [cut([NH0, QS], BF16) for _ in range(2)]
        sums = cut([QS])
        rec = cut([QS])
        rec_rest = cut([QS])
        rec_parts = cut([3, QS], BF16)
        maxima = cut([2 * NH0, GK], BF16)
        spread = cut([NT, P], BF16)
        window = cut([2 * GK - RB])
        identb = cut([P], BF16)
        cut = Cut()
        V1 = cut([NT, NHB * 3])
        in_c = cut.at
        xc = [cut([T]) for _ in range(2)]
        sq = [cut([T]) for _ in range(2)]
        xn = [cut([T]) for _ in range(2)]
        ss = [cut([HALF]) for _ in range(2)]
        sqa = [cut([HALF]) for _ in range(2)]
        nrm = [cut([HALF]) for _ in range(5)]
        rst = [cut([HALF]) for _ in range(5)]
        tmp = [cut([HALF]) for _ in range(3)]
        planes = cut([15, HALF], BF16)
        cut = Cut(in_c)
        Qs = [cut([HG, T], BF16) for _ in range(2)]
        Ks = [cut([HG, T], BF16) for _ in range(2)]
        PR1 = [cut([CW]) for _ in range(PRING)]
        Vg = [cut([NT, VW]) for _ in range(2)]
        Oe = [Yall[:, 0, :], Yall[:, 1, :]]
        cut = Cut()
        exc = [cut([T]) for _ in range(2)]
        esq = [cut([T]) for _ in range(2)]
        num = [cut([T]) for _ in range(2)]
        den = cut([T])
        rden = cut([T])
        expand = cut([2, P])
        xsum = cut([T])
        cut = Cut(cut.at)
        W1, W2, Wo = [cut([NE, P]) for _ in range(3)]
        wB = cut([NE, T])
        sel = cut([NE, P])
        wT = cut([T])
        lg = cut([NT, NE])
        lw = cut([NT, NE])
        lm = cut([NT])
        h1 = [cut([HALF]) for _ in range(2)]
        h2 = [cut([HALF]) for _ in range(2)]
        h2w = [cut([HALF]) for _ in range(2)]
        res = [cut([HALF]) for _ in range(2)]

        ps = ctx.enter_context(nc.psum_tensor("ps", [P, 8 * HALF], F32))

        def bank(k, n=1):
            return ps[:, k * HALF:(k + n) * HALF]

        c_scale0, c_bias0, c_wq, c_ck, c_t = 0, 1, 2, 4, 6
        c_A1, c_B1, c_A2, c_B2, c_sd = 8, 16, 24, 32, 40

        def cv(c, n=1):
            return CV[:, c:c + n]

        def param(name):
            if name in PARAMS:
                k = NE * PARAMS.index(name)
                return PT[:, k:k + NE]
            k = NE * len(PARAMS) + VECTORS.index(name)
            return PT[:, k:k + 1]

        def wt(what):
            k, n = {"q0": (0, P), "k0": (P, P), "v0": (2 * P, P), "out": (3 * P, P),
                    "qk1": (4 * P, 2 * P), "v1": (6 * P, P), "proj": (7 * P, P)}[what]
            return WT[:, k:k + n]

        w_loaded, ffn_w_loaded = sem("w_loaded"), sem("ffn_w_loaded")
        x_loaded_first, x_loaded_rest = sem("x_loaded_first"), sem("x_loaded_rest")
        ident_set, eps_set = sem("ident_set"), sem("eps_set")
        w_turned, w_copied = sem("w_turned"), sem("w_copied")
        param_step, param_sd = sem("param_step"), sem("param_sd")
        a_bn, a_mm, a_hi, a_rest, a_lo = [sem(n) for n in ("a_bn", "a_mm", "a_hi", "a_rest", "a_lo")]
        a_stored = [sem("a_stored_even"), sem("a_stored_odd")]
        k_loaded = [sem("k_loaded_even"), sem("k_loaded_odd")]
        v_loaded = [sem("v_loaded_even"), sem("v_loaded_odd")]
        q_loaded = [sem("q_loaded_low"), sem("q_loaded_high")]
        b_const = sem("b_constants")
        b_raw, b_max, b_moved, b_guard = [sem(n) for n in ("b_raw_scores", "b_max", "b_max_turned", "b_guard")]
        b_qk, b_exp, b_sum, b_summed = [sem(n) for n in ("b_scores", "b_exp", "b_sum", "b_sum_copied")]
        b_rec, b_rhi, b_rrest, b_rmid, b_rlo = [sem(n) for n in (
            "b_rec", "b_rec_hi", "b_rec_rest", "b_rec_mid", "b_rec_lo")]
        rs_loaded = [sem("rs_loaded_even"), sem("rs_loaded_odd")]
        b_spread, b_norm, b_pv, b_out = [sem(n) for n in ("b_spread", "b_norm", "b_pv", "b_out")]
        c_pe, c_dve, c_act, c_pool = [sem(n) for n in ("c_pe", "c_dve", "c_act", "c_pool")]
        c_stored, ones_set = sem("c_stored"), sem("ones_set")
        e_pe, e_dve, e_act, e_pool = [sem(n) for n in ("e_pe", "e_dve", "e_act", "e_pool")]
        e_loaded, e_set = sem("e_loaded"), sem("e_set")
        d_init, d_vinit = sem("d_slots_set"), sem("d_value_slots_set")
        d_loaded = [sem("d_loaded_even"), sem("d_loaded_odd")]
        d_qk, d_exp, d_mask, d_pv = [sem(n) for n in ("d_scores", "d_exp", "d_mask", "d_pv")]
        d_v, d_ev = sem("d_values"), sem("d_copied_out")
        d_stored = [sem("d_stored_even"), sem("d_stored_odd")]
        f_mm, f_dve, f_exp, f_set = [sem(n) for n in ("f_mm", "f_dve", "f_exp", "f_set")]
        f_wbps, f_wbA, f_wbV = sem("f_wb_product"), sem("f_wb_copied_act"), sem("f_wb_copied_dve")
        g_h1, g_r1, g_h2, g_r2 = [sem(n) for n in ("g_h1", "g_relu1", "g_h2", "g_relu2")]
        g_w, g_y3, g_y, g_res = [sem(n) for n in ("g_weighted", "g_third", "g_sum", "g_res")]
        out_stored = [sem("out_stored_low"), sem("out_stored_high")]

        W_LOADS = 4 + len(PARAMS) + len(VECTORS) + 3
        FFN_LOADS = 5
        K_LOADS, Q_LOADS = 6, 6
        RS_LOADS = 3 * NH0
        NSTEP = B * STEPS
        C_STORES = 13
        MASKS = [2 * sum(j == t for j, t in ch) for ch in CHUNKS]

        def wait(eng, s, v):
            if isinstance(v, int) and v <= 0:
                return
            eng.wait_ge(s, v)

        def peeled(eng, n, body):
            body(0)
            with eng.Fori(1, n) as i:
                body(i)

        def turns(eng, body):
            body(0, range(TURN))
            with eng.Fori(1, B // 2) as i:
                body(i, range(TURN))
            body(B // 2, range(TAIL + 1))

        def in_range(i, k, lag):
            if not isinstance(i, int):
                return True
            return 0 <= i * TURN + k - lag < B // 2 * TURN

        def wait_moved(eng, i, st):
            if isinstance(i, int) and i * 2 * STEPS + st < 0:
                return
            eng.wait_ge(rs_loaded[st % 2], i * (STEPS * RS_LOADS * INC) + (st // 2 + 1) * (RS_LOADS * INC))

        class Steps:
            def __init__(self, s, names):
                self.s, self.names = s, names

            def after(self, eng, i, name):
                wait(eng, self.s, i * len(self.names) + self.names.index(name) + 1)

        two = (0, 1)
        five = range(5)
        CP = Steps(c_pe, [f"{n}{p}" for n in ("z", "mean", "var", "val") for p in two] + ["qk0", "qk1"])
        CD = Steps(c_dve, [f"{n}{p}" for n in ("x", "xc", "rec") for p in two]
                   + [f"{n}/{th}" for th in two for n in
                      ["rq", "rk", "n0", "n1", "n2", "n3"] + [f"g{k}" for k in range(8)]
                      + [f"rest{k}" for k in five]])
        CA = Steps(c_act, [f"{n}{p}" for n in ("sq", "sd", "cv") for p in two]
                   + [f"{n}/{th}" for th in two for n in ["s0", "s1", "s2", "s3", "sd0", "sd1"]
                      + [f"hi{k}" for k in five] + [f"mid{k}" for k in five]])
        CG = Steps(c_pool, ["xn0", "xn1"] + [f"{n}/{th}" for th in two for n in
                                             ["ss0", "ss1"] + [f"lo{k}" for k in five]])
        EP = Steps(e_pe, [f"{n}{p}" for n in ("den", "z", "mean", "var") for p in two])
        ED = Steps(e_dve, ["rden"] + [f"{n}{p}" for n in ("y", "x", "xc", "rec", "sum") for p in two])
        EA = Steps(e_act, [f"{n}{p}" for n in ("sq", "sd") for p in two])
        EG = Steps(e_pool, ["xn0", "xn1"])

        def before(i, th):
            return (i, 0) if th else (i - 1, 1)

        def hi_plane(k):
            return 3 * k

        def half(ap, th):
            return ap[:, th * HALF:(th + 1) * HALF]

        def flat(ap):
            return ap.rearrange("p n t -> p (n t)")

        block = ctx.enter_context(nc.Block())

        @block.sync
        def _(sp):
            sp.dma_start(X[:, 0:2, :], x_v[:, 0:2, :]).then_inc(x_loaded_first, INC)
            sp.dma_start(WR[:, 0:3, :], a["L0_conv_pw_w"].rearrange("(k p) c -> p k c", p=P)).then_inc(w_loaded, INC)
            sp.dma_start(WR[:, 3, :], a["L0_conv_out_w"]).then_inc(w_loaded, INC)
            sp.dma_start(WR[:, 4:7, :], a["L1_attn_w_qkv"].rearrange("(k p) c -> p k c", p=P)).then_inc(w_loaded, INC)
            sp.dma_start(WR[:, 7, :], a["L1_attn_w_proj"]).then_inc(w_loaded, INC)
            for k, name in enumerate(PARAMS):
                sp.dma_start(PRr[NE * k:NE * (k + 1), :], a[name]).then_inc(w_loaded, INC)
            for k, name in enumerate(VECTORS):
                r = NE * len(PARAMS) + k
                sp.dma_start(PRr[r:r + 1, :], a[name].rearrange("(o c) -> o c", o=1)).then_inc(w_loaded, INC)
            for k, name in enumerate(["L1_attn_qn_w", "L1_attn_kn_w"]):
                sp.dma_start(qkw[:, 2 * k:2 * k + 2],
                             a[name].rearrange("(o c) -> o c", o=1).to_broadcast([P, 2])).then_inc(w_loaded, INC)
            sp.dma_start(br_b[:, :],
                         a["L1_ffn_br"].rearrange("(o c) -> o c", o=1).to_broadcast([P, NE])).then_inc(w_loaded, INC)
            sp.dma_start(X[:, 2:B, :], x_v[:, 2:B, :]).then_inc(x_loaded_rest, INC)
            sp.dma_start(Wr[:, :], a["L1_ffn_Wr"]).then_inc(ffn_w_loaded, INC)
            sp.dma_start(bo[:, :], a["L1_ffn_bo"]).then_inc(ffn_w_loaded, INC)

            with sp.Fori(0, B // 2) as i:
                for par in range(2):
                    b = i * 2 + par
                    sp.wait_ge(a_lo, b * 2 + 2)
                    sp.dma_start(parts0[ds(b, 1)].rearrange("o k p t -> p (o k) t"), parts[par])\
                        .then_inc(a_stored[par], INC)
                    sp.dma_start(values0[ds(b, 1)].rearrange("o p t -> p (o t)"), v_out[par])\
                        .then_inc(a_stored[par], INC)

            for par in range(2):
                sp.wait_ge(a_stored[par], B * INC)

            def load_k(b, par):
                for tile, kinds in ((K1, (3, 4, 3)), (K2, (5, 3, 4))):
                    for r, kind in enumerate(kinds):
                        src = parts0[ds(b, 1), kind].rearrange("o (n i) t -> i (o n) t", n=NH0)
                        sp.dma_start(tile[par][D0 * r:D0 * (r + 1), :, :], src).then_inc(k_loaded[par], INC)

            def load_q(b, th):
                for tile, kinds in ((Q1, (0, 0, 1)), (Q2, (0, 2, 1))):
                    for r, kind in reversed(list(enumerate(kinds))):
                        src = parts0[ds(b, 1), kind, :, th * HALF:(th + 1) * HALF]\
                            .rearrange("o (n i) t -> i (o n) t", n=NH0)
                        sp.dma_start(tile[th][D0 * r:D0 * (r + 1), :, :], src).then_inc(q_loaded[th], INC)

            def load_v(b, par):
                sp.dma_start(V0[par], values0[ds(b, 1)].rearrange("o p t -> p (o t)")).then_inc(v_loaded[par], INC)

            def feed(i, last=False):
                for st in range(2 * STEPS):
                    g = i * (2 * STEPS) + st
                    sp.wait_ge(b_rlo, g + 1)
                    for r in range(3):
                        for n in range(NH0):
                            sp.dma_start(RS[st % 2][GK * r:GK * (r + 1), n, :], rec_parts[GK * n:GK * (n + 1), r, :])\
                                .then_inc(rs_loaded[st % 2], INC)
                    par, q = st // STEPS, st % STEPS
                    b, sub = i * 2 + par, i * TURN + par * (TURN // 2)
                    if not (last and par == 1) and q in (1, 2):
                        sp.wait_ge(b_qk, sub * 2 + 2 * SUB * (STEPS // 2) * q)
                        load_q(b + 1, q - 1)
                    if not last and q == 3:
                        sp.wait_ge(b_qk, sub * 2 + TURN)
                        load_k(b + 2, par)
                    first_image = isinstance(i, int) and i == 0 and par == 0
                    if q == 0 and not first_image and not (last and par == 1):
                        sp.wait_ge(b_pv, sub)
                        load_v(b + 1, 1 - par)

            load_k(0, 0)
            for th in range(2):
                load_q(0, th)
            load_v(0, 0)
            load_k(1, 1)
            load_v(1, 1)
            feed(0)
            with sp.Fori(1, B // 2 - 1) as i:
                feed(i)
            feed(B // 2 - 1, last=True)

            with sp.Fori(0, B // 2) as i:
                for th in range(2):
                    CG.after(sp, i, f"lo4/{th}")

                    def rows(dram, r, k):
                        return dram[r:r + k, ds(i * P, P), th * HALF:(th + 1) * HALF].rearrange("r h t -> h r t")
                    for d in range(2):
                        q, k, r = hi_plane(d), hi_plane(2 + d), 6 * d
                        sp.dma_start(rows(qstack, r, 3), planes[:, q:q + 1, :].to_broadcast([P, 3, HALF]))\
                            .then_inc(c_stored, INC)
                        sp.dma_start(rows(qstack, r + 3, 2), planes[:, q + 1:q + 2, :].to_broadcast([P, 2, HALF]))\
                            .then_inc(c_stored, INC)
                        sp.dma_start(rows(qstack, r + 5, 1), planes[:, q + 2:q + 3, :]).then_inc(c_stored, INC)
                        sp.dma_start(rows(kstack, r, 3), planes[:, k:k + 3, :]).then_inc(c_stored, INC)
                        sp.dma_start(rows(kstack, r + 3, 2), planes[:, k:k + 2, :]).then_inc(c_stored, INC)
                        sp.dma_start(rows(kstack, r + 5, 1), planes[:, k:k + 1, :]).then_inc(c_stored, INC)
                    g = hi_plane(4)
                    sp.dma_start(rows(qstack, STACK, 3), planes[:, g:g + 3, :]).then_inc(c_stored, INC)

            sp.wait_ge(c_stored, B * C_STORES * INC)
            sp.wait_ge(d_init, 4)

            def load_group(g, par):
                sp.dma_start(Qs[par][0:QROWS, :, :], qstack[:, ds(g * HG, HG), :]).then_inc(d_loaded[par], INC)
                sp.dma_start(Ks[par][0:KROWS, :, :], kstack[:, ds(g * HG, HG), :]).then_inc(d_loaded[par], INC)

            def store_group(g, par):
                sp.wait_ge(d_ev, g * 2 + 2)
                for j in range(HG):
                    sp.dma_start(attn1[ds(g * HG + j, 1)].rearrange("o r t -> (o r) t"),
                                 Oe[par][32 * j:32 * j + 3, :]).then_inc(d_stored[par], INC)

            for par in range(2):
                load_group(par, par)
            with sp.Fori(0, NG // 2 - 1) as i:
                for par in range(2):
                    g = i * 2 + par
                    sp.wait_ge(d_qk, g * NC + NC)
                    load_group(g + 2, par)
                    store_group(g, par)
            for par in range(2):
                store_group(NG - 2 + par, par)

            for par in range(2):
                sp.wait_ge(d_stored[par], NG // 2 * HG * INC)
            sp.wait_ge(d_pv, NG * NC)
            for w, name in ((W1, "L1_ffn_W1"), (W2, "L1_ffn_W2"), (Wo, "L1_ffn_Wo")):
                sp.dma_start(w, a[name].rearrange("e d h -> d e h")).then_inc(ffn_w_loaded, INC)

            def load_pair(i):
                EP.after(sp, i - 1, "z1")
                for par in range(2):
                    for d in range(2):
                        sp.dma_start(num[par][d:P:2, :], attn1[ds((i * 2 + par) * NH1, NH1), d, :])\
                            .then_inc(e_loaded, INC)
                sp.dma_start(den, attn1[ds(i * P, P), 2, :]).then_inc(e_loaded, INC)
            peeled(sp, B // 2, load_pair)

            with sp.Fori(0, B) as i:
                for th in range(2):
                    sp.wait_ge(g_res, i * 2 + th + 1)
                    sp.dma_start(out_v[:, ds(i, 1), th * HALF:(th + 1) * HALF].rearrange("p o t -> p (o t)"),
                                 res[th]).then_inc(out_stored[th], INC)
            for th in range(2):
                sp.wait_ge(out_stored[th], B * INC)

        @block.gpsimd
        def _(pool):
            pool.memset(ident[:, :], 0.0).then_inc(ident_set, 1)
            pool.memset(causal[:, :], BIG).then_inc(ident_set, 1)
            pool.memset(mean_w[:, :], 1.0 / P).then_inc(eps_set, 1)
            pool.memset(eps_c[:, 0:1], LN_EPS).then_inc(eps_set, 1)
            pool.memset(eps_c[:, 1:2], RMS_EPS).then_inc(eps_set, 1)
            pool.memset(eps_c[:, 2:3], 0.0).then_inc(eps_set, 1)
            pool.wait_ge(ident_set, 2)
            pool.affine_select(out=ident[:, :], in_=ident[:, :], compare_op=ALU.not_equal, fill=1.0, base=0,
                               pattern=[[-1, P]], channel_multiplier=1).then_inc(ident_set, 1)
            pool.affine_select(out=causal[:, :], in_=causal[:, :], compare_op=ALU.is_ge, fill=0.0, base=0,
                               pattern=[[1, P]], channel_multiplier=-1).then_inc(ident_set, 1)

            pool.wait_ge(ident_set, 4)
            made = [0]

            def constant(ins):
                made[0] += 1
                ins.then_inc(b_const, 1)
                pool.wait_ge(b_const, made[0])
            constant(pool.tensor_copy(identb, ident[:, :]))
            constant(pool.memset(spread[0:3 * GK], 0.0))
            constant(pool.memset(window, 0.0))
            for par in range(2):
                constant(pool.memset(K2[par][3 * GK:P], 0.0))
            for r in range(3):
                v = flat(spread[GK * r:GK * (r + 1)]).rearrange("p (y x) -> p y x", x=GK)
                constant(pool.affine_select(out=v, in_=v, compare_op=ALU.not_equal, fill=1.0, base=0,
                                            pattern=[[-1, H], [0, GK]], channel_multiplier=1))
            for j in range(RB):
                at = GK - RB + j
                constant(pool.memset(window[GK * j:GK * (j + 1), at:at + 1], 1.0))
            for par in range(2):
                v = K2[par][3 * GK:P].rearrange("p n (y x) -> p n y x", x=GK)
                constant(pool.affine_select(out=v, in_=v, compare_op=ALU.not_equal, fill=-1.0, base=0,
                                            pattern=[[0, NH0], [-1, H], [0, GK]], channel_multiplier=1))

            with pool.Fori(0, B // 2) as i:
                for par in range(2):
                    b = i * 2 + par
                    for k in range(2):
                        pool.wait_ge(a_hi, b * 5 + 4 + k)
                        pool.tensor_tensor(parts[par][:, 3 * k + 2, :], rest0[k], parts[par][:, 3 * k + 1, :],
                                           ALU.subtract).then_inc(a_lo, 1)

            def pool_b(i):
                for par in range(2):
                    g = i * 2 + par
                    pool.wait_ge(b_rmid, g + 1)
                    if par:
                        pool.wait_ge(rs_loaded[0], i * (RS_LOADS * INC) + RS_LOADS * INC)
                    else:
                        wait(pool, rs_loaded[1], i * (RS_LOADS * INC))
                    pool.tensor_tensor(rec_parts[:, 2, :], rec_rest, rec_parts[:, 1, :], ALU.subtract).then_inc(b_rlo, 1)
            peeled(pool, NSTEP // 2, pool_b)

            pool.wait_ge(b_out, NSTEP)
            pool.memset(V1, 1.0).then_inc(ones_set, 1)

            def pool_c(i):
                for par in range(2):
                    CD.after(pool, i, f"rec{par}")
                    CP.after(pool, i - 1, "qk1")
                    pool.tensor_tensor(xn[par], xc[par], sq[par], ALU.mult).then_inc(c_pool, 1)
                for th in range(2):
                    for k in range(2):
                        CA.after(pool, i, f"s{2 * k + 1}/{th}")
                        pool.tensor_tensor(ss[k], ss[k], sqa[k], ALU.add).then_inc(c_pool, 1)
                    for k in range(5):
                        CA.after(pool, i, f"mid{k}/{th}")
                        r = hi_plane(k)
                        pool.tensor_tensor(planes[:, r + 2, :], rst[k], planes[:, r + 1, :],
                                           ALU.subtract).then_inc(c_pool, 1)
            peeled(pool, B // 2, pool_c)

            pool.wait_ge(c_stored, B * C_STORES * INC)
            CP.after(pool, B // 2 - 1, "qk1")
            CD.after(pool, B // 2 - 1, "rest4/1")
            for s in range(2):
                pool.memset(Qs[s], 0.0).then_inc(d_init, 1)
                pool.memset(Ks[s], 1.0).then_inc(d_init, 1)
            for s in range(2):
                pool.memset(Vg[s], 0.0).then_inc(d_vinit, 1)
            CA.after(pool, B // 2 - 1, "cv1")
            pool.wait_ge(d_vinit, 2)

            def group_values(g, par):
                pool.tensor_copy(Vg[par][:, :, 0:3 * HG], V1[:, :, ds(g * (3 * HG), 3 * HG)]).then_inc(d_v, 1)

            def pool_d(i):
                for par in range(2):
                    g = i * 2 + par
                    wait(pool, d_pv, g * NC - NC)
                    group_values(g, par)
            peeled(pool, NG // 2, pool_d)

            pool.wait_ge(d_pv, NG * NC)
            pool.memset(expand, 0.0).then_inc(e_set, 1)
            pool.memset(xsum, 0.0).then_inc(e_set, 1)
            pool.wait_ge(e_set, 2)
            for par in range(2):
                e_v = expand[:, par, :].rearrange("p (h d) -> p h d", d=2)
                pool.affine_select(out=e_v, in_=e_v, compare_op=ALU.not_equal, fill=1.0, base=-NH1 * par,
                                   pattern=[[-1, NH1], [0, 2]], channel_multiplier=1).then_inc(e_set, 1)
            pool.memset(sel[0:NE, :, :], 0.0).then_inc(f_set, 1)
            pool.wait_ge(f_set, 1)
            pool.affine_select(out=sel[0:NE, :, :], in_=sel[0:NE, :, :], compare_op=ALU.not_equal, fill=1.0,
                               base=0, pattern=[[-1, NE], [0, P]], channel_multiplier=1).then_inc(f_set, 1)

            with pool.Fori(0, B // 2) as i:
                for par in range(2):
                    ED.after(pool, i, f"rec{par}")
                    pool.tensor_tensor(Yall[:, ds(i * 2 + par, 1), :].rearrange("p o t -> p (o t)"),
                                       exc[par], esq[par], ALU.mult).then_inc(e_pool, 1)

        @block.scalar
        def _(act):
            act.wait_ge(w_turned, 1)
            w = bank(0, 2)
            act.activation(WT[:, 0:3 * P].rearrange("p (s n i) -> p n s i", s=3, n=NH0),
                           w[:, 0:3 * P].rearrange("p (n s i) -> p n s i", s=3, n=NH0), ACT.Copy).then_inc(w_copied, 1)
            act.activation(wt("out"), w[:, 3 * P:4 * P], ACT.Copy).then_inc(w_copied, 1)
            act.activation(wt("qk1").rearrange("p (s d h) -> p s h d", s=2, d=2),
                           w[:, 4 * P:6 * P].rearrange("p (s h d) -> p s h d", s=2, d=2), ACT.Copy).then_inc(w_copied, 1)
            act.activation(WT[:, 6 * P:8 * P], w[:, 6 * P:8 * P], ACT.Copy).then_inc(w_copied, 1)
            act.wait_ge(param_step, 3)
            act.activation(cv(c_sd, 17), cv(c_sd, 17), ACT.Sqrt).then_inc(param_sd, 1)

            def act_a(i):
                for par in range(2):
                    b = i * 2 + par
                    wait(act, a_stored[par], i * (2 * INC))
                    for k in range(2):
                        act.wait_ge(a_mm, b * 3 + k + 1)
                        act.activation(parts[par][:, 3 * k, :], bank(2 * k, 2), ACT.Copy).then_inc(a_hi, 1)
                    act.wait_ge(a_mm, b * 3 + 3)
                    act.activation(v_out[par], bank(4, 2), ACT.Copy).then_inc(a_hi, 1)
                    for k in range(2):
                        act.wait_ge(a_rest, b * 2 + k + 1)
                        act.activation(parts[par][:, 3 * k + 1, :], rest0[k], ACT.Copy).then_inc(a_hi, 1)
            peeled(act, B // 2, act_a)

            act.wait_ge(eps_set, 4)
            act.activation(eps_c[:, 3:4], eps_c[:, 2:3], ACT.Exp)

            def act_b(i, subs):
                for k in subs:
                    K = i * TURN + k
                    if k % NH0 == 0 and in_range(i, k, L_MOVE):
                        c = (k - L_MOVE) % TURN
                        q = c // SUB % STEPS
                        at = (q % 2) * QS + c // NH0 % 2 * P
                        act.wait_ge(b_moved, i * (TURN // NH0) + k // NH0)
                        act.activation(Q2[q // 2][3 * GK:P, :, at:at + P],
                                       bank(2)[3 * GK:P].rearrange("p (n q) -> p n q", n=NH0),
                                       ACT.Copy).then_inc(b_guard, 1)
                    if k % SUB == 2 and in_range(i, k, L_SUM + SUB):
                        g = i * (2 * STEPS) + (k - L_SUM - SUB) // SUB
                        act.wait_ge(b_sum, g * SUB + SUB)
                        wait(act, b_rec, g)
                        act.activation(sums, bank(7)[:, 0:QS], ACT.Copy).then_inc(b_summed, 1)
                    if k % SUB == 3 and in_range(i, k, L_SUM + SUB + 1):
                        st = (k - L_SUM - SUB - 1) // SUB
                        act.wait_ge(b_rec, i * (2 * STEPS) + st + 1)
                        wait_moved(act, i, st - 1)
                        act.activation(rec_parts[:, 0, :], rec, ACT.Copy).then_inc(b_rhi, 1)
                    if k % SUB == 4 and in_range(i, k, L_SUM + SUB + 2):
                        g = i * (2 * STEPS) + (k - L_SUM - SUB - 2) // SUB
                        act.wait_ge(b_rrest, g + 1)
                        act.activation(rec_parts[:, 1, :], rec_rest, ACT.Copy).then_inc(b_rmid, 1)
                    if in_range(i, k, L_EXP):
                        c = (k - L_EXP) % TURN
                        for hp in range(2):
                            act.wait_ge(b_qk, K * 2 + (hp + 1 - 2 * L_EXP))
                            wait(act, b_pv, K + (1 - L_EXP - 2 * SUB))
                            act.activation(E0[c // SUB % 2][:, c % SUB, 2 * hp:2 * hp + 2, :].rearrange("p n q -> p (n q)"),
                                           bank(2 + hp), ACT.Exp, scale=SCALE0).then_inc(b_exp, 1)
                    if k % SUB == L_OUT % SUB and in_range(i, k, L_OUT):
                        g0 = (k - L_OUT) // SUB
                        act.wait_ge(b_pv, i * TURN + (g0 + 1) * SUB)
                        act.activation(Yall[:, ds(i * 2 + g0 // STEPS, 1), (g0 % STEPS) * QS:(g0 % STEPS + 1) * QS]
                                       .rearrange("p o t -> p (o t)"), bank(6)[:, 0:QS], ACT.Copy).then_inc(b_out, 1)
            turns(act, act_b)

            def act_c(i):
                for par in range(2):
                    CD.after(act, i, f"xc{par}")
                    act.activation(sq[par], xc[par], ACT.Square).then_inc(c_act, 1)
                for par in range(2):
                    CP.after(act, i, f"var{par}")
                    act.activation(sq[par], bank(2 * par, 2), ACT.Sqrt, bias=eps_c[:, 0:1]).then_inc(c_act, 1)
                for par in range(2):
                    CP.after(act, i, f"val{par}")
                    act.wait_ge(ones_set, 1)
                    dst = V1[:, :, ds((i * 2 + par) * (3 * NH1), 3 * NH1)].rearrange("p s (h e) -> p s h e", e=3)
                    act.activation(dst[:, :, :, 0:2],
                                   bank(4 + 2 * par, 2).rearrange("p (s h d) -> p s h d", s=NT, d=2),
                                   ACT.Copy).then_inc(c_act, 1)
                for th in range(2):
                    pi, pth = before(i, th)
                    CP.after(act, i, f"qk{th}")
                    CD.after(act, pi, f"n3/{pth}")
                    for k in range(4):
                        act.activation((ss, sqa)[k % 2][k // 2], bank(4 * th + k), ACT.Square).then_inc(c_act, 1)
                    for k in range(2):
                        CG.after(act, i, f"ss{k}/{th}")
                        act.activation(ss[k], ss[k], ACT.Sqrt, bias=eps_c[:, 1:2], scale=0.5).then_inc(c_act, 1)
                    wait(act, c_stored, i * (2 * C_STORES * INC) + th * (C_STORES * INC))
                    for k in range(5):
                        CD.after(act, i, f"n{k}/{th}" if k < 4 else f"g7/{th}")
                        act.activation(planes[:, hi_plane(k), :], nrm[k], ACT.Copy).then_inc(c_act, 1)
                    for k in range(5):
                        CD.after(act, i, f"rest{k}/{th}")
                        act.activation(planes[:, hi_plane(k) + 1, :], rst[k], ACT.Copy).then_inc(c_act, 1)
            peeled(act, B // 2, act_c)

            act.wait_ge(d_init, 4)
            act.activation(eps_c[:, 4:5], eps_c[:, 2:3], ACT.Exp)

            def act_d(i):
                for par in range(2):
                    for c in range(NC):
                        k = i * (2 * NC) + (par * NC + c)
                        s = (par * NC + c) % 2
                        act.wait_ge(d_qk, k + 1)
                        wait(act, d_pv, k - (PRING - 1))
                        act.activation(PR1[(par * NC + c) % PRING], bank(UPC * s, UPC), ACT.Exp).then_inc(d_exp, 1)
            peeled(act, NG // 2, act_d)

            with act.Fori(0, B // 2) as i:
                for par in range(2):
                    ED.after(act, i, f"xc{par}")
                    act.activation(esq[par], exc[par], ACT.Square).then_inc(e_act, 1)
                for par in range(2):
                    EP.after(act, i, f"var{par}")
                    act.activation(esq[par], bank(2 * par, 2), ACT.Sqrt, bias=eps_c[:, 0:1]).then_inc(e_act, 1)

            act.wait_ge(f_dve, 3)
            act.activation(lw, lg, ACT.Exp).then_inc(f_exp, 1)
            for e in range(0, NE, 2):
                act.wait_ge(f_wbps, e + 1)
                act.activation(wB[:, e, :], bank(4, 2), ACT.Copy).then_inc(f_wbA, 1)

            def act_f(i):
                def relu2(k):
                    n, e = i * (2 * NE) + k, k % NE
                    act.wait_ge(g_h2, n + 1)
                    wait(act, g_w, n - 1)
                    act.activation(h2[k % 2], bank(2 + k % 2), ACT.Relu, bias=cv(c_B2 + e),
                                   scale=cv(c_A2 + e)).then_inc(g_r2, 1)
                for k in range(2 * NE):
                    n, e = i * (2 * NE) + k, k % NE
                    act.wait_ge(g_h1, n + 1)
                    wait(act, g_h2, n - 1)
                    act.activation(h1[k % 2], bank(k % 2), ACT.Relu, bias=cv(c_B1 + e),
                                   scale=cv(c_A1 + e)).then_inc(g_r1, 1)
                    if k:
                        relu2(k - 1)
                relu2(2 * NE - 1)
            peeled(act, B, act_f)

        @block.tensor
        def _(pe):
            pe.wait_ge(ident_set, 4)
            pe.wait_ge(w_loaded, W_LOADS * INC)
            for k in range(8):
                mm = pe.transpose(ps[:, k * P:(k + 1) * P], WR[:, k, :], ident[:, :])
            mm.then_inc(w_turned, 1)
            pe.transpose(bank(2)[:, 0:NPR], PRr[0:NPR, :], ident[0:NPR, 0:NPR]).then_inc(w_turned, 1)

            pe.wait_ge(w_copied, 4)

            def pe_a(i):
                for par in range(2):
                    b = i * 2 + par
                    pe.wait_ge(a_bn, b + 1)
                    for k, w in enumerate(("q0", "k0")):
                        wait(pe, a_rest, b * 2 + (k - 1))
                        for th in range(2):
                            mm = pe.matmul(bank(2 * k + th), wt(w), half(xbn[par], th), start=True, stop=True)
                        mm.then_inc(a_mm, 1)
                    wait(pe, a_hi, b * 5 - 2)
                    for t in range(NT):
                        mm = pe.matmul(bank(4, 2)[:, t * P:(t + 1) * P], xbn[par][:, t * P:(t + 1) * P], wt("v0"),
                                       start=True, stop=True)
                    mm.then_inc(a_mm, 1)
            peeled(pe, B // 2, pe_a)

            pe.wait_ge(a_hi, B * 5)
            pe.wait_ge(a_rest, B * 2)

            pe.wait_ge(b_const, 14)

            def pe_b(i, subs):
                for k in subs:
                    K = i * TURN + k
                    if k % NH0 == 0 and in_range(i, k, L_MOVE):
                        pe.wait_ge(b_max, K)
                        wait(pe, b_guard, i * (TURN // NH0) + (k // NH0 - 1))
                        wait(pe, b_exp, K * 2 + (-1 - 2 * L_EXP))
                        for n in range(NH0):
                            mm = pe.matmul(bank(2)[3 * GK:P, n * P:(n + 1) * P],
                                           maxima[:, (k + n - L_MOVE) % SUB, :], identb, start=True, stop=True)
                        mm.then_inc(b_moved, 1)
                    if in_range(i, k, 0):
                        par, q, qb, n = k // (TURN // 2), k // SUB % STEPS, k // NH0 % 2, k % NH0
                        if k % (TURN // 2) == 0:
                            pe.wait_ge(k_loaded[par], i * (K_LOADS * INC) + K_LOADS * INC)
                        if q % 2 == 0 and k % SUB == 0:
                            pe.wait_ge(q_loaded[q // 2], (i * 2 + (par + 1)) * (Q_LOADS * INC))
                        wait(pe, b_max, K)
                        at = (q % 2) * QS + qb * P
                        for th in range(2):
                            mm = pe.matmul(bank(th), Q1[q // 2][0:3 * D0, n, at:at + P],
                                           half(K1[par][0:3 * D0, n, :], th), start=True, stop=True)
                        mm.then_inc(b_raw, 1)
                    for hp in range(2):
                        if in_range(i, k, L_EXP):
                            c = (k - L_EXP) % TURN
                            par, q, kb = c // (TURN // 2), c // SUB % STEPS, c % SUB
                            at = (q % 2) * QS
                            if k % NH0 == 0 and hp == 0 and in_range(i, k, L_MOVE):
                                wait(pe, b_guard, i * (TURN // NH0) + k // NH0)
                            if kb == 0 and hp == 0:
                                pe.wait_ge(b_guard, (i * (TURN // SUB) + ((k - L_EXP) // SUB + 1)) * (SUB // NH0))
                            wait(pe, b_exp, K * 2 + (hp - 1 - 2 * L_EXP))
                            for n in (2 * hp, 2 * hp + 1):
                                o = bank(2 + hp)[:, (n % 2) * QS:(n % 2 + 1) * QS]
                                pe.matmul(o, K1[par][0:3 * D0, n, kb * P:(kb + 1) * P],
                                          Q1[q // 2][0:3 * D0, n, at:at + QS], start=True, stop=False)
                                mm = pe.matmul(o, K2[par][:, n, kb * P:(kb + 1) * P],
                                               Q2[q // 2][:, n, at:at + QS], start=False, stop=True)
                            mm.then_inc(b_qk, 1)
                        if in_range(i, k, L_NORM):
                            c = (k - L_NORM) % TURN
                            if c % SUB == 0 and hp == 0:
                                wait_moved(pe, i, (k - L_NORM) // SUB)
                            wait(pe, b_norm, K * 2 + (hp - 1 - 2 * L_NORM))
                            pe.matmul(bank(4 + hp), spread[0:3 * GK, c % SUB, :],
                                      RS[c // SUB % 2][0:3 * GK, 2 * hp:2 * hp + 2, :].rearrange("p n q -> p (n q)"),
                                      start=True, stop=True).then_inc(b_spread, 1)
                    if in_range(i, k, L_SUM):
                        c = (k - L_SUM) % TURN
                        kb, sl = c % SUB, c // SUB % 2
                        if kb == 0:
                            wait(pe, b_summed, i * (2 * STEPS) + (k - L_SUM) // SUB)
                        pe.wait_ge(b_exp, K * 2 + (2 - 2 * L_SUM))
                        for n in range(NH0):
                            mm = pe.matmul(bank(7)[GK * n:GK * (n + 1), 0:QS],
                                           window[:, GK - RB - RB * kb:2 * GK - RB - RB * kb], E0[sl][:, kb, n, :],
                                           start=kb == 0, stop=kb == SUB - 1, skip_group_check=True)
                        mm.then_inc(b_sum, 1)
                    if in_range(i, k, L_PV):
                        c = (k - L_PV) % TURN
                        par, kb, sl = c // (TURN // 2), c % SUB, c // SUB % 2
                        if c % (TURN // 2) == 0:
                            pe.wait_ge(v_loaded[par], (i + (k - L_PV) // TURN) * INC + INC)
                        if kb == 0:
                            wait(pe, b_out, i * (2 * STEPS) + (k - L_PV) // SUB)
                        pe.wait_ge(b_norm, K * 2 + (2 - 2 * L_PV))
                        for n in range(NH0):
                            v = kb * P + D0 * n
                            mm = pe.matmul(bank(6)[D0 * n:D0 * (n + 1), 0:QS], V0[par][:, v:v + D0], E0[sl][:, kb, n, :],
                                           start=kb == 0, stop=kb == SUB - 1, skip_group_check=True)
                        mm.then_inc(b_pv, 1)
            turns(pe, pe_b)

            def pe_c(i):
                def image(ap, par, th):
                    return ap[:, ds(i * 2 + par, 1), th * HALF:(th + 1) * HALF].rearrange("p o t -> p (o t)")
                for par in range(2):
                    CD.after(pe, i - 1, "n3/0")
                    CA.after(pe, i - 1, "s3/0")
                    for th in range(2):
                        mm = pe.matmul(bank(2 * par + th), wt("out"), image(Yall, par, th), start=True, stop=True)
                    mm.then_inc(c_pe, 1)
                for par in range(2):
                    CD.after(pe, i - 1, "n3/1")
                    CD.after(pe, i, f"x{par}")
                    for th in range(2):
                        mm = pe.matmul(bank(4 + 2 * par + th), mean_w[:, :], image(X, par, th), start=True, stop=True)
                    mm.then_inc(c_pe, 1)
                for par in range(2):
                    CA.after(pe, i, f"sq{par}")
                    for th in range(2):
                        mm = pe.matmul(bank(2 * par + th), mean_w[:, :], half(sq[par], th), start=True, stop=True)
                    mm.then_inc(c_pe, 1)
                for par in range(2):
                    CG.after(pe, i, f"xn{par}")
                    for t in range(NT):
                        mm = pe.matmul(bank(4 + 2 * par, 2)[:, t * P:(t + 1) * P], xn[par][:, t * P:(t + 1) * P],
                                       wt("v1"), start=True, stop=True)
                    mm.then_inc(c_pe, 1)
                for th in range(2):
                    if th:
                        CA.after(pe, i, "cv1")
                    for k in range(4):
                        for par in range(2):
                            mm = pe.matmul(bank(4 * th + k)[NH1 * par:NH1 * (par + 1), :],
                                           wt("qk1")[:, NH1 * k:NH1 * (k + 1)], half(xn[par], th),
                                           start=True, stop=True)
                    mm.then_inc(c_pe, 1)
            pe.wait_ge(b_out, NSTEP)
            peeled(pe, B // 2, pe_c)

            CD.after(pe, B // 2 - 1, "n3/1")

            def scores1(i, par, c):
                if c == 0:
                    pe.wait_ge(d_loaded[par], i * (2 * INC) + 2 * INC)
                wait(pe, d_exp, i * (2 * NC) + (par * NC + c - 1))
                at = UPC * ((par * NC + c) % 2)
                for h in range(HG - 1):
                    for s, j, t, n in runs(CHUNKS[c], False):
                        pe.matmul(bank(at + h)[:, s * P:(s + n) * P], Ks[par][:, h, j * P:(j + 1) * P],
                                  Qs[par][:, h, t * P:(t + n) * P], start=True, stop=True)
                h = HG - 1
                for s, (j, t) in enumerate(CHUNKS[c]):
                    mm = pe.matmul(bank(at + s)[:, UPC * P:HG * P], Ks[par][:, h, j * P:(j + 1) * P],
                                   Qs[par][:, h, t * P:(t + 1) * P], start=True, stop=True)
                mm.then_inc(d_qk, 1)

            def values1(i, par, c):
                g = i * 2 + par
                if MASKS[c]:
                    pe.wait_ge(d_mask, g * sum(MASKS) + sum(MASKS[:c + 1]))
                else:
                    pe.wait_ge(d_exp, g * NC + (c + 1))
                if c == 0:
                    pe.wait_ge(d_v, g + 1)
                    wait(pe, d_ev, g * 2 - 1)
                if c == 1:
                    wait(pe, d_ev, g * 2)
                pr = PR1[(par * NC + c) % PRING]
                for s, j, t, n in runs(CHUNKS[c], True):
                    high = t >= NT // 2
                    first = j == 0 and t in (0, NT // 2)
                    last = (j, t + n) in ((NT // 2 - 1, NT // 2), (NT - 1, NT))
                    o = bank(7 if high else 6)[:, (t - high * NT // 2) * P:(t + n - high * NT // 2) * P]
                    for h in range(HG):
                        if h < HG - 1:
                            rhs = pr[:, h * HALF + s * P:h * HALF + (s + n) * P]
                        else:
                            rhs = pr.rearrange("p (u c) -> p u c", u=UPC)[:, s:s + n, UPC * P:HG * P]
                        mm = pe.matmul(o[32 * h:32 * (h + 1), :], Vg[par][:, j, 3 * h:3 * h + 32], rhs,
                                       start=first, stop=last, skip_group_check=True)
                mm.then_inc(d_pv, 1)

            def pe_d(i, first=False, last=False):
                for k in range(2 * NC):
                    nk = k + 2
                    if nk < 2 * NC:
                        scores1(i, nk // NC, nk % NC)
                    elif not last:
                        scores1(i + 1, 0, nk - 2 * NC)
                    if k:
                        values1(i, (k - 1) // NC, (k - 1) % NC)
                    elif not first:
                        values1(i - 1, 1, NC - 1)

            scores1(0, 0, 0)
            scores1(0, 0, 1)
            pe_d(0, first=True)
            with pe.Fori(1, NG // 2 - 1) as i:
                pe_d(i)
            pe_d(NG // 2 - 1, last=True)
            values1(NG // 2 - 1, 1, NC - 1)

            pe.wait_ge(d_exp, NG * NC)
            pe.wait_ge(d_ev, 2 * NG)
            pe.wait_ge(e_set, 4)

            def pe_e(i):
                def image(ap, par, th):
                    return ap[:, ds(i * 2 + par, 1), th * HALF:(th + 1) * HALF].rearrange("p o t -> p (o t)")
                for par in range(2):
                    ED.after(pe, i, "rden")
                    ED.after(pe, i - 1, f"xc{par}")
                    for th in range(2):
                        mm = pe.matmul(bank(4 + 2 * par + th), expand[:, par, :], half(rden, th), start=True, stop=True)
                    mm.then_inc(e_pe, 1)
                for par in range(2):
                    ED.after(pe, i, f"y{par}")
                    EA.after(pe, i - 1, f"sd{par}")
                    for th in range(2):
                        mm = pe.matmul(bank(2 * par + th), wt("proj"), half(num[par], th), start=True, stop=True)
                    mm.then_inc(e_pe, 1)
                for par in range(2):
                    ED.after(pe, i, f"x{par}")
                    for th in range(2):
                        mm = pe.matmul(bank(4 + 2 * par + th), mean_w[:, :], image(X, par, th), start=True, stop=True)
                    mm.then_inc(e_pe, 1)
                for par in range(2):
                    EA.after(pe, i, f"sq{par}")
                    for th in range(2):
                        mm = pe.matmul(bank(2 * par + th), mean_w[:, :], half(esq[par], th), start=True, stop=True)
                    mm.then_inc(e_pe, 1)
            peeled(pe, B // 2, pe_e)

            pe.wait_ge(ffn_w_loaded, FFN_LOADS * INC)
            ED.after(pe, B // 2 - 1, "sum1")
            for t in range(NT):
                mm = pe.matmul(bank(0)[:, t * NE:(t + 1) * NE], xsum[:, t * P:(t + 1) * P], Wr[:, :],
                               start=True, stop=True)
            mm.then_inc(f_mm, 1)
            pe.wait_ge(f_dve, 6)
            for t in range(NT):
                mm = pe.transpose(bank(2, 2)[0:NE, t * P:(t + 1) * P], lw[:, t, :], ident[:, :])
            mm.then_inc(f_mm, 1)
            pe.wait_ge(f_dve, 7)
            pe.wait_ge(f_set, 2)
            for e in range(NE):
                wait(pe, f_wbA if e % 2 == 0 else f_wbV, e // 2)
                for th in range(2):
                    mm = pe.matmul(bank(4 + 2 * (e % 2) + th), sel[0:NE, e, :], wT[0:NE, th * HALF:(th + 1) * HALF],
                                   start=True, stop=True)
                mm.then_inc(f_wbps, 1)
            pe.wait_ge(f_wbA, NE // 2)
            pe.wait_ge(f_wbV, NE // 2)

            def pe_f(i):
                def second(k):
                    n = i * (2 * NE) + k
                    pe.wait_ge(g_r1, n + 1)
                    wait(pe, g_r2, n - 1)
                    pe.matmul(bank(2 + k % 2), W2[:, k % NE, :], h1[k % 2], start=True, stop=True).then_inc(g_h2, 1)

                def third(k):
                    n, th, e = i * (2 * NE) + k, k // NE, k % NE
                    pe.wait_ge(g_w, n + 1)
                    if e == 0:
                        wait(pe, g_res, i * 2 + (th - 1))
                    pe.matmul(bank(4 + th), Wo[:, e, :], h2w[k % 2], start=e == 0, stop=False).then_inc(g_y3, 1)
                    if e == NE - 1:
                        pe.matmul(bank(4 + th), bo[:, :], wT[0:NE, th * HALF:(th + 1) * HALF],
                                  start=False, stop=True).then_inc(g_y, 1)
                for k in range(2 * NE):
                    n = i * (2 * NE) + k
                    wait(pe, g_r1, n - 1)
                    th = k // NE
                    pe.matmul(bank(k % 2), W1[:, k % NE, :],
                              Yall[:, ds(i, 1), th * HALF:(th + 1) * HALF].rearrange("p o t -> p (o t)"),
                              start=True, stop=True).then_inc(g_h1, 1)
                    if k >= 1:
                        second(k - 1)
                    if k >= 2:
                        third(k - 2)
                second(2 * NE - 1)
                third(2 * NE - 2)
                third(2 * NE - 1)
            peeled(pe, B, pe_f)

        @block.vector
        def _(dve):
            dve.wait_ge(w_turned, 2)
            dve.tensor_copy(PT[:, :], bank(2)[:, 0:NPR]).then_inc(param_step, 1)
            dve.wait_ge(param_step, 1)
            dve.tensor_scalar(cv(c_sd, NE), param("L1_ffn_v1"), BN_EPS, None, ALU.add).then_inc(param_step, 1)
            dve.tensor_scalar(cv(c_sd + NE, NE), param("L1_ffn_v2"), BN_EPS, None, ALU.add)
            dve.tensor_scalar(cv(c_sd + 2 * NE), param("L0_conv_bn_var"), BN_EPS0, None, ALU.add)\
                .then_inc(param_step, 1)
            step = [3]

            def chain(ins):
                step[0] += 1
                ins.then_inc(param_step, 1)
                dve.wait_ge(param_step, step[0])

            dve.wait_ge(param_sd, 1)
            dve.wait_ge(param_step, 3)
            chain(dve.reciprocal(cv(c_sd, 17), cv(c_sd, 17)))
            for c_A, c_B, k in ((c_A1, c_B1, "1"), (c_A2, c_B2, "2")):
                at = c_sd + NE * (k == "2")
                chain(dve.tensor_tensor(cv(c_A, NE), param("L1_ffn_g" + k), cv(at, NE), ALU.mult))
                chain(dve.tensor_tensor(cv(c_B, NE), param("L1_ffn_b" + k), param("L1_ffn_m" + k), ALU.subtract))
                chain(dve.tensor_tensor(cv(c_B, NE), cv(c_B, NE), cv(c_A, NE), ALU.mult))
                chain(dve.tensor_tensor(cv(c_B, NE), cv(c_B, NE), param("L1_ffn_be" + k), ALU.add))
            chain(dve.tensor_tensor(cv(c_scale0), param("L0_conv_bn_gamma"), cv(c_sd + 2 * NE), ALU.mult))
            chain(dve.tensor_tensor(cv(c_scale0), cv(c_scale0), param("L0_conv_dw_w"), ALU.mult))
            chain(dve.tensor_tensor(cv(c_bias0), param("L0_conv_bn_beta"), param("L0_conv_dw_w"), ALU.mult))
            chain(dve.tensor_tensor(cv(c_t), param("L0_conv_bn_mean"), cv(c_scale0), ALU.mult))
            chain(dve.tensor_tensor(cv(c_bias0), cv(c_bias0), cv(c_t), ALU.subtract))
            chain(dve.tensor_scalar(cv(c_wq, 2), qkw[:, 0:2], SCALE1, None, ALU.mult))
            chain(dve.scalar_tensor_tensor(cv(c_ck, 2), qkw[:, 2:4], -1.0, qkw[:, 2:4], ALU.mult, ALU.max))
            chain(dve.tensor_scalar(cv(c_ck, 2), cv(c_ck, 2), -(2.0 ** 0.5), None, ALU.mult))

            def dve_a(i):
                for par in range(2):
                    b = i * 2 + par
                    wait(dve, a_mm, b * 3 - 3)
                    dve.tensor_scalar(xbn[par], X[:, ds(b, 1), :].rearrange("p o t -> p (o t)"), cv(c_scale0),
                                      cv(c_bias0), ALU.mult, ALU.add).then_inc(a_bn, 1)
                    for k in range(2):
                        dve.wait_ge(a_hi, b * 5 + (k + 1))
                        wait(dve, a_lo, b * 2 + (k - 1))
                        dve.tensor_tensor(rest0[k], bank(2 * k, 2), parts[par][:, 3 * k, :],
                                          ALU.subtract).then_inc(a_rest, 1)
            dve.wait_ge(x_loaded_first, INC)
            dve_a(0)
            dve.wait_ge(x_loaded_rest, INC)
            with dve.Fori(1, B // 2) as i:
                dve_a(i)

            def dve_b(i, subs):
                for k in subs:
                    K = i * TURN + k
                    if in_range(i, k, 0):
                        dve.wait_ge(b_raw, K + 1)
                        wait(dve, b_moved, i * (TURN // NH0) + (k // NH0 - 1))
                        dve.reduce_max(maxima[:, k % SUB, :], bank(0, 2).rearrange("p (y x) -> p y x", x=GK), AX_X)\
                            .then_inc(b_max, 1)
                    if in_range(i, k, L_NORM):
                        c = (k - L_NORM) % TURN
                        for hp in range(2):
                            e = E0[c // SUB % 2][:, c % SUB, 2 * hp:2 * hp + 2, :].rearrange("p n q -> p (n q)")
                            dve.wait_ge(b_spread, K * 2 + (hp + 1 - 2 * L_NORM))
                            dve.tensor_tensor(e, e, bank(4 + hp), ALU.mult).then_inc(b_norm, 1)
                    if k % SUB == 2 and in_range(i, k, L_SUM + SUB):
                        g = i * (2 * STEPS) + (k - L_SUM - SUB) // SUB
                        dve.wait_ge(b_summed, g + 1)
                        wait(dve, b_rrest, g)
                        dve.reciprocal(rec, sums).then_inc(b_rec, 1)
                    if k % SUB == 3 and in_range(i, k, L_SUM + SUB + 1):
                        g = i * (2 * STEPS) + (k - L_SUM - SUB - 1) // SUB
                        dve.wait_ge(b_rhi, g + 1)
                        wait(dve, b_rlo, g)
                        dve.tensor_tensor(rec_rest, rec, rec_parts[:, 0, :], ALU.subtract).then_inc(b_rrest, 1)
            turns(dve, dve_b)

            dve.wait_ge(b_out, NSTEP)

            def dve_c(i):
                for par in range(2):
                    xi = X[:, ds(i * 2 + par, 1), :].rearrange("p o t -> p (o t)")
                    CP.after(dve, i, f"z{par}")
                    dve.scalar_tensor_tensor(xi, bank(2 * par, 2), param("L0_conv_out_b"), xi,
                                             ALU.add, ALU.add).then_inc(c_dve, 1)
                for par in range(2):
                    xi = X[:, ds(i * 2 + par, 1), :].rearrange("p o t -> p (o t)")
                    CP.after(dve, i, f"mean{par}")
                    CG.after(dve, i - 1, f"xn{par}")
                    dve.tensor_tensor(xc[par], xi, bank(4 + 2 * par, 2), ALU.subtract).then_inc(c_dve, 1)
                for par in range(2):
                    CA.after(dve, i, f"sd{par}")
                    dve.reciprocal(sq[par], sq[par]).then_inc(c_dve, 1)
                for th in range(2):
                    pi, pth = before(i, th)
                    for k in range(2):
                        CA.after(dve, i, f"sd{k}/{th}")
                        dve.reciprocal(ss[k], ss[k]).then_inc(c_dve, 1)
                    CA.after(dve, pi, f"hi4/{pth}")
                    wait_rest(dve, pi, pth)
                    for k in range(4):
                        CD.after(dve, i, ("rq", "rk")[k // 2] + f"/{th}")
                        w = cv(c_wq + k) if k < 2 else qkw[:, k:k + 1]
                        dve.scalar_tensor_tensor(nrm[k], bank(4 * th + k), w, ss[k // 2], ALU.mult, ALU.mult)\
                            .then_inc(c_dve, 1)
                    q0, q1, k0, k1, guard = nrm
                    t0, t1, t2 = tmp

                    def g(n, ins):
                        ins.then_inc(c_dve, 1)

                    CD.after(dve, i, f"n3/{th}")
                    g(0, dve.scalar_tensor_tensor(t0, q0, -1.0, q0, ALU.mult, ALU.max))
                    g(1, dve.scalar_tensor_tensor(t1, q1, -1.0, q1, ALU.mult, ALU.max))
                    CD.after(dve, i, f"g0/{th}")
                    g(2, dve.tensor_scalar(t0, t0, cv(c_ck), None, ALU.mult))
                    CD.after(dve, i, f"g2/{th}")
                    g(3, dve.scalar_tensor_tensor(t1, t1, cv(c_ck + 1), t0, ALU.mult, ALU.add))
                    g(4, dve.scalar_tensor_tensor(t2, q0, -1.0, k0, ALU.mult, ALU.mult))
                    CD.after(dve, i, f"g3/{th}")
                    g(5, dve.scalar_tensor_tensor(t0, q1, -1.0, k1, ALU.mult, ALU.mult))
                    CD.after(dve, i, f"g5/{th}")
                    g(6, dve.tensor_tensor(t2, t2, t0, ALU.add))
                    CD.after(dve, i, f"g6/{th}")
                    g(7, dve.scalar_tensor_tensor(guard, t2, -GUARD, t1, ALU.add, ALU.max))
                    for k in range(5):
                        CA.after(dve, i, f"hi{k}/{th}")
                        CG.after(dve, pi, f"lo{k}/{pth}")
                        dve.tensor_tensor(rst[k], nrm[k], planes[:, hi_plane(k), :], ALU.subtract).then_inc(c_dve, 1)

            def wait_rest(eng, i, th):
                CD.after(eng, i, f"rest4/{th}")

            peeled(dve, B // 2, dve_c)

            def copy_out(i, par, hh):
                g = i * 2 + par
                if hh == 0:
                    wait(dve, d_stored[par], i * (HG * INC))
                    dve.wait_ge(d_pv, g * NC + (CHUNK_A + 1))
                else:
                    dve.wait_ge(d_pv, g * NC + NC)
                dve.tensor_copy(half(Oe[par], hh), bank(6 + hh)).then_inc(d_ev, 1)

            def dve_d(i):
                for par in range(2):
                    for c in range(NC):
                        if MASKS[c]:
                            dve.wait_ge(d_exp, i * (2 * NC) + (par * NC + c + 1))
                            pr = PR1[(par * NC + c) % PRING]
                            for s, (j, t) in enumerate(CHUNKS[c]):
                                if j == t:
                                    v = pr.rearrange("p (h c) -> p h c", h=UPC)[:, :, s * P:(s + 1) * P]
                                    m3 = causal[:, :].rearrange("p (o t) -> p o t", o=1).to_broadcast([P, UPC, P])
                                    dve.tensor_tensor(v, v, m3, ALU.min).then_inc(d_mask, 1)
                                    v = pr[:, s * HALF + UPC * P:(s + 1) * HALF]
                                    dve.tensor_tensor(v, v, causal[:, :], ALU.min).then_inc(d_mask, 1)
                        if c == 0:
                            if par == 1:
                                copy_out(i, 0, 1)
                            elif not (isinstance(i, int) and i == 0):
                                copy_out(i - 1, 1, 1)
                        if c == CHUNK_A + 2:
                            copy_out(i, par, 0)
            dve.wait_ge(d_init, 4)
            peeled(dve, NG // 2, dve_d)
            copy_out(NG // 2 - 1, 1, 1)

            def dve_e(i):
                dve.wait_ge(e_loaded, i * (5 * INC) + 5 * INC)
                EP.after(dve, i - 1, "den1")
                dve.reciprocal(rden, den).then_inc(e_dve, 1)
                for par in range(2):
                    EP.after(dve, i, f"den{par}")
                    dve.tensor_tensor(num[par], num[par], bank(4 + 2 * par, 2), ALU.mult).then_inc(e_dve, 1)
                for par in range(2):
                    xi = X[:, ds(i * 2 + par, 1), :].rearrange("p o t -> p (o t)")
                    EP.after(dve, i, f"z{par}")
                    dve.tensor_tensor(xi, xi, bank(2 * par, 2), ALU.add).then_inc(e_dve, 1)
                for par in range(2):
                    xi = X[:, ds(i * 2 + par, 1), :].rearrange("p o t -> p (o t)")
                    EP.after(dve, i, f"mean{par}")
                    EG.after(dve, i - 1, f"xn{par}")
                    dve.tensor_tensor(exc[par], xi, bank(4 + 2 * par, 2), ALU.subtract).then_inc(e_dve, 1)
                for par in range(2):
                    EA.after(dve, i, f"sd{par}")
                    dve.reciprocal(esq[par], esq[par]).then_inc(e_dve, 1)
                for par in range(2):
                    EG.after(dve, i, f"xn{par}")
                    if par:
                        ED.after(dve, i, "sum0")
                    else:
                        ED.after(dve, i - 1, "sum1")
                    dve.tensor_tensor(xsum, xsum, Yall[:, ds(i * 2 + par, 1), :].rearrange("p o t -> p (o t)"),
                                      ALU.add).then_inc(e_dve, 1)
            dve.wait_ge(e_set, 2)
            peeled(dve, B // 2, dve_e)

            def per_token(ap):
                return ap.rearrange("p (t o) -> p t o", o=1).to_broadcast([P, NT, NE])
            dve.wait_ge(f_mm, 1)
            dve.scalar_tensor_tensor(lg, bank(0)[:, 0:NT * NE].rearrange("p (t e) -> p t e", e=NE), 1.0 / B,
                                     br_b[:, :].rearrange("p (o e) -> p o e", o=1).to_broadcast([P, NT, NE]),
                                     ALU.mult, ALU.add).then_inc(f_dve, 1)
            dve.wait_ge(f_dve, 1)
            dve.reduce_max(lm, lg, AX_X).then_inc(f_dve, 1)
            dve.wait_ge(f_dve, 2)
            dve.tensor_tensor(lg, lg, per_token(lm), ALU.subtract).then_inc(f_dve, 1)
            dve.wait_ge(f_exp, 1)
            dve.reduce_sum(lm, lw, AX_X).then_inc(f_dve, 1)
            dve.wait_ge(f_dve, 4)
            dve.reciprocal(lm, lm).then_inc(f_dve, 1)
            dve.wait_ge(f_dve, 5)
            dve.tensor_tensor(lw, lw, per_token(lm), ALU.mult).then_inc(f_dve, 1)
            dve.wait_ge(f_mm, 2)
            dve.tensor_copy(wT[0:NE, :], bank(2, 2)[0:NE, :]).then_inc(f_dve, 1)
            for e in range(1, NE, 2):
                dve.wait_ge(f_wbps, e + 1)
                dve.tensor_copy(wB[:, e, :], bank(6, 2)).then_inc(f_wbV, 1)

            def dve_f(i):
                def result(th):
                    dve.wait_ge(g_y, i * 2 + (th + 1))
                    wait(dve, out_stored[th], i * INC)
                    dve.tensor_tensor(res[th], bank(4 + th),
                                      X[:, ds(i, 1), th * HALF:(th + 1) * HALF].rearrange("p o t -> p (o t)"),
                                      ALU.add).then_inc(g_res, 1)
                for k in range(2 * NE):
                    n, th, e = i * (2 * NE) + k, k // NE, k % NE
                    dve.wait_ge(g_r2, n + 1)
                    wait(dve, g_y3, n - 1)
                    dve.tensor_tensor(h2w[k % 2], h2[k % 2], half(wB[:, e, :], th), ALU.mult).then_inc(g_w, 1)
                    if k == NE + 2:
                        result(0)
                result(1)
            dve.wait_ge(f_wbA, NE // 2)
            dve.wait_ge(f_wbV, NE // 2)
            peeled(dve, B, dve_f)


_INS = ["x"] + VECTORS[:5] + ["L0_conv_pw_w", "L0_conv_out_w", "L0_conv_out_b", "L1_attn_w_qkv", "L1_attn_w_proj",
        "L1_attn_qn_w", "L1_attn_kn_w", "L1_ffn_Wr", "L1_ffn_br", "L1_ffn_W1", "L1_ffn_W2", "L1_ffn_Wo",
        "L1_ffn_bo"] + PARAMS


def kernel(**inputs):
    import numpy as _np
    import concourse.bacc as _bacc
    from concourse import mybir as _mybir
    from concourse.bass_utils import run_bass_kernel_spmd as _run

    nc = _bacc.Bacc("TRN2", target_bir_lowering=False, num_devices=1)
    arrays, aps = {}, {}
    for name in _INS:
        a = _np.ascontiguousarray(inputs[name])
        arrays[f"in_{name}"] = a
        aps[name] = nc.dram_tensor(f"in_{name}", a.shape, _mybir.dt.from_np(a.dtype), kind="ExternalInput").ap()
    out = nc.dram_tensor("out_0", (B, P, H, W), _mybir.dt.float32, kind="ExternalOutput").ap()
    hybrid_kernel(nc, aps, out)
    r = _run(nc, [arrays], core_ids=[0])
    return r.results[0]["out_0"]
```

```python
from contextlib import ExitStack

import concourse.bass as bass
from concourse import mybir

F32 = mybir.dt.float32
BF16 = mybir.dt.bfloat16
ACT = mybir.ActivationFunctionType
ALU = mybir.AluOpType
AX_X = mybir.AxisListType.X
ds = bass.ds

P = 128
B = 8
H = W = 32
T = H * W
HALF = T // 2
NT = T // P
NH0 = 4
D0 = P // NH0
NH1 = P // 2
NHB = B * NH1
NE = 8
HG = 4
NG = NHB // HG
BN_EPS0 = 1e-5
LN_EPS = 1e-5
RMS_EPS = 1e-6
BN_EPS = 1e-3
SCALE0 = D0 ** -0.5
SCALE1 = 2 ** -0.5
GUARD = 60.0
BIG = 3.0e38

INC = 16

QS = 256
STEPS = T // QS
SUB = 8
TURN = 2 * STEPS * SUB
GK = W
RB = P // GK
L_MOVE = NH0
L_EXP = 9
L_SUM = 10
L_NORM = 23
L_PV = 24
L_OUT = L_PV + SUB
TAIL = L_OUT

STACK = 12
QROWS, KROWS = STACK + 3, STACK

UNITS = [(j, t) for j in range(NT) for t in range(j, NT)]
UPC = 3
CHUNKS = [UNITS[i:i + UPC] for i in range(0, len(UNITS), UPC)]
NC = len(CHUNKS)
CW = UPC * HG * P
PRING = 6
VW = 44


def runs(chunk, split_half):
    out = []
    for i, (j, t) in enumerate(chunk):
        if out and out[-1][1] == j and out[-1][2] + out[-1][3] == t and not (
                split_half and t == NT // 2):
            out[-1][3] += 1
        else:
            out.append([i, j, t, 1])
    return out


CHUNK_A = max(c for c, ch in enumerate(CHUNKS) if any(t < NT // 2 for _, t in ch))

PARAMS = ["L1_ffn_b1", "L1_ffn_g1", "L1_ffn_be1", "L1_ffn_m1", "L1_ffn_v1",
          "L1_ffn_b2", "L1_ffn_g2", "L1_ffn_be2", "L1_ffn_m2", "L1_ffn_v2"]
VECTORS = ["L0_conv_bn_gamma", "L0_conv_bn_beta", "L0_conv_bn_mean", "L0_conv_bn_var",
           "L0_conv_dw_w", "L0_conv_out_b"]
NPR = NE * len(PARAMS) + len(VECTORS)


def hybrid_kernel(nc, a, out):
    x_v = a["x"].rearrange("b c h w -> c b (h w)")
    out_v = out.rearrange("b c h w -> c b (h w)")

    parts0 = nc.dram_tensor("parts0", (B, 6, P, T), BF16, kind="Internal").ap()
    values0 = nc.dram_tensor("values0", (B, P, T), F32, kind="Internal").ap()
    qstack = nc.dram_tensor("qstack", (QROWS, NHB, T), BF16, kind="Internal").ap()
    kstack = nc.dram_tensor("kstack", (KROWS, NHB, T), BF16, kind="Internal").ap()
    attn1 = nc.dram_tensor("attn1", (NHB, 3, T), F32, kind="Internal").ap()

    with ExitStack() as ctx:
        def sb(name, shape, dt=F32):
            return ctx.enter_context(nc.sbuf_tensor(name, shape, dt))

        def sem(name):
            return ctx.enter_context(nc.semaphore(name))

        X = sb("X", [P, B, T])
        WT = sb("WT", [P, 8 * P])
        ident = sb("ident", [P, P])
        mean_w = sb("mean_w", [P, P])
        causal = sb("causal", [P, P])
        PT = sb("PT", [P, NPR])
        CV = sb("CV", [P, 64])
        qkw = sb("qkw", [P, 4])
        br_b = sb("br_b", [P, NE])
        Wr = sb("Wr", [P, NE])
        bo = sb("bo", [NE, P])
        eps_c = sb("eps_c", [P, 5])
        Yall = sb("Yall", [P, B, T])
        arena_bytes = 136 * 1024
        arena = sb("arena", [P, arena_bytes // 4])

        class Cut:
            def __init__(self, at=0):
                self.at = at

            def __call__(self, shape, dt=F32):
                n = 1
                for s in shape:
                    n *= s
                size = 2 if dt == BF16 else 4
                words = (n * size + 3) // 4
                start = self.at // 4
                self.at += words * 4
                assert self.at <= arena_bytes, self.at
                ap = arena[:, start:start + words]
                if dt != F32:
                    ap = ap.bitcast(dt)
                names = [f"d{i}" for i in range(len(shape))]
                if len(shape) > 1:
                    ap = ap.rearrange("p (" + " ".join(names) + ") -> p " + " ".join(names),
                                      **dict(zip(names[1:], shape[1:])))
                return ap

        cut = Cut()
        WR = cut([8, P])
        PRr = cut([P])
        cut = Cut(8 * 1024)
        xbn = [cut([T]) for _ in range(2)]
        parts = [cut([6, T], BF16) for _ in range(2)]
        rest0 = [cut([T]) for _ in range(2)]
        v_out = [cut([T]) for _ in range(2)]
        cut = Cut()
        E0 = [cut([NT, NH0, QS]) for _ in range(2)]
        K1, K2 = [[cut([NH0, T], BF16) for _ in range(2)] for _ in range(2)]
        Q1, Q2 = [[cut([NH0, HALF], BF16) for _ in range(2)] for _ in range(2)]
        V0 = [cut([T]) for _ in range(2)]
        RS = [cut([NH0, QS], BF16) for _ in range(2)]
        sums = cut([QS])
        rec = cut([QS])
        rec_rest = cut([QS])
        rec_parts = cut([3, QS], BF16)
        maxima = cut([2 * NH0, GK], BF16)
        spread = cut([NT, P], BF16)
        window = cut([2 * GK - RB])
        identb = cut([P], BF16)
        cut = Cut()
        V1 = cut([NT, NHB * 3])
        in_c = cut.at
        xc = [cut([T]) for _ in range(2)]
        sq = [cut([T]) for _ in range(2)]
        xn = [cut([T]) for _ in range(2)]
        xn_high = cut([HALF])
        ss = [cut([HALF]) for _ in range(2)]
        nrm = [cut([HALF]) for _ in range(5)]
        rst = [cut([HALF]) for _ in range(5)]
        tmp = [cut([HALF]) for _ in range(4)]
        sqa = tmp[2:4]
        planes = [cut([15, HALF], BF16) for _ in range(2)]
        cut = Cut(in_c)
        Qs = [cut([HG, T], BF16) for _ in range(2)]
        Ks = [cut([HG, T], BF16) for _ in range(2)]
        PR1 = [cut([CW]) for _ in range(PRING)]
        Vg = [cut([NT, VW]) for _ in range(2)]
        Oe = [Yall[:, 0, :], Yall[:, 1, :]]
        cut = Cut()
        exc = [cut([T]) for _ in range(2)]
        esq = [cut([T]) for _ in range(2)]
        num = [cut([T]) for _ in range(2)]
        den = cut([T])
        rden = cut([T])
        expand = cut([2, P])
        xsum = cut([T])
        cut = Cut(cut.at)
        W1, W2, Wo = [cut([NE, P]) for _ in range(3)]
        wB = cut([NE, T])
        sel = cut([NE, P])
        wT = cut([T])
        lg = cut([NT, NE])
        lw = cut([NT, NE])
        lm = cut([NT])
        h1 = [cut([HALF]) for _ in range(2)]
        h2 = [cut([HALF]) for _ in range(2)]
        h2w = [cut([HALF]) for _ in range(2)]
        res = [cut([HALF]) for _ in range(2)]

        ps = ctx.enter_context(nc.psum_tensor("ps", [P, 8 * HALF], F32))

        def bank(k, n=1):
            return ps[:, k * HALF:(k + n) * HALF]

        c_scale0, c_bias0, c_wq, c_ck, c_t = 0, 1, 2, 4, 6
        c_A1, c_B1, c_A2, c_B2, c_sd = 8, 16, 24, 32, 40

        def cv(c, n=1):
            return CV[:, c:c + n]

        def param(name):
            if name in PARAMS:
                k = NE * PARAMS.index(name)
                return PT[:, k:k + NE]
            k = NE * len(PARAMS) + VECTORS.index(name)
            return PT[:, k:k + 1]

        def wt(what):
            k, n = {"q0": (0, P), "k0": (P, P), "v0": (2 * P, P), "out": (3 * P, P),
                    "qk1": (4 * P, 2 * P), "v1": (6 * P, P), "proj": (7 * P, P)}[what]
            return WT[:, k:k + n]

        w_loaded, ffn_w_loaded = sem("w_loaded"), sem("ffn_w_loaded")
        x_loaded_first, x_loaded_rest = sem("x_loaded_first"), sem("x_loaded_rest")
        ident_set, eps_set = sem("ident_set"), sem("eps_set")
        w_turned, w_copied = sem("w_turned"), sem("w_copied")
        param_step, param_sd = sem("param_step"), sem("param_sd")
        a_bn, a_mm, a_hi, a_rest, a_lo = [sem(n) for n in ("a_bn", "a_mm", "a_hi", "a_rest", "a_lo")]
        a_stored = [sem("a_stored_even"), sem("a_stored_odd")]
        k_loaded = [sem("k_loaded_even"), sem("k_loaded_odd")]
        v_loaded = [sem("v_loaded_even"), sem("v_loaded_odd")]
        q_loaded = [sem("q_loaded_low"), sem("q_loaded_high")]
        b_const = sem("b_constants")
        b_raw, b_max, b_moved, b_guard = [sem(n) for n in ("b_raw_scores", "b_max", "b_max_turned", "b_guard")]
        b_qk, b_exp, b_sum, b_summed = [sem(n) for n in ("b_scores", "b_exp", "b_sum", "b_sum_copied")]
        b_rec, b_rhi, b_rrest, b_rmid, b_rlo = [sem(n) for n in (
            "b_rec", "b_rec_hi", "b_rec_rest", "b_rec_mid", "b_rec_lo")]
        rs_loaded = [sem("rs_loaded_even"), sem("rs_loaded_odd")]
        b_spread, b_norm, b_pv, b_out = [sem(n) for n in ("b_spread", "b_norm", "b_pv", "b_out")]
        c_pe, c_dve, c_act, c_pool = [sem(n) for n in ("c_pe", "c_dve", "c_act", "c_pool")]
        r_pe, r_dve, r_act, r_pool = [sem(n) for n in ("r_pe", "r_dve", "r_act", "r_pool")]
        c_stored = [sem("c_stored_low"), sem("c_stored_high")]
        ones_set, c_kept = sem("ones_set"), sem("c_kept")
        e_pe, e_dve, e_act, e_pool = [sem(n) for n in ("e_pe", "e_dve", "e_act", "e_pool")]
        e_loaded, e_set = sem("e_loaded"), sem("e_set")
        d_init, d_vinit = sem("d_slots_set"), sem("d_value_slots_set")
        d_loaded = [sem("d_loaded_even"), sem("d_loaded_odd")]
        d_qk, d_exp, d_mask, d_pv = [sem(n) for n in ("d_scores", "d_exp", "d_mask", "d_pv")]
        d_v, d_ev = sem("d_values"), sem("d_copied_out")
        d_stored = [sem("d_stored_even"), sem("d_stored_odd")]
        f_mm, f_dve, f_exp, f_set = [sem(n) for n in ("f_mm", "f_dve", "f_exp", "f_set")]
        f_wbps, f_wbA, f_wbV = sem("f_wb_product"), sem("f_wb_copied_act"), sem("f_wb_copied_dve")
        g_h1, g_r1, g_h2, g_r2 = [sem(n) for n in ("g_h1", "g_relu1", "g_h2", "g_relu2")]
        g_w, g_y3, g_y, g_res = [sem(n) for n in ("g_weighted", "g_third", "g_sum", "g_res")]
        out_stored = [sem("out_stored_low"), sem("out_stored_high")]

        W_LOADS = 4 + len(PARAMS) + len(VECTORS) + 3
        FFN_LOADS = 5
        K_LOADS, Q_LOADS = 6, 6
        RS_LOADS = 3 * NH0
        NSTEP = B * STEPS
        C_STORES = 13
        MASKS = [2 * sum(j == t for j, t in ch) for ch in CHUNKS]

        def wait(eng, s, v):
            if isinstance(v, int) and v <= 0:
                return
            eng.wait_ge(s, v)

        def peeled(eng, n, body):
            body(0)
            with eng.Fori(1, n) as i:
                body(i)

        def turns(eng, body):
            body(0, range(TURN))
            with eng.Fori(1, B // 2) as i:
                body(i, range(TURN))
            body(B // 2, range(TAIL + 1))

        def in_range(i, k, lag):
            if not isinstance(i, int):
                return True
            return 0 <= i * TURN + k - lag < B // 2 * TURN

        def wait_moved(eng, i, st):
            if isinstance(i, int) and i * 2 * STEPS + st < 0:
                return
            eng.wait_ge(rs_loaded[st % 2], i * (STEPS * RS_LOADS * INC) + (st // 2 + 1) * (RS_LOADS * INC))

        class Steps:
            def __init__(self, s, names):
                self.s, self.names = s, names

            def after(self, eng, i, name):
                wait(eng, self.s, i * len(self.names) + self.names.index(name) + 1)

        def turn_parts(i):
            known = isinstance(i, int)
            return not (known and i == B // 2), not (known and i == 0)

        def turns_c(eng, body):
            body(0)
            body(1)
            with eng.Fori(2, B // 2) as i:
                body(i)
            body(B // 2)

        two = (0, 1)
        five = range(5)
        CP = Steps(c_pe, ["z", "mean", "var", "val"])
        CD = Steps(c_dve, ["x", "xc", "rec"])
        CA = Steps(c_act, ["sq", "sd", "cv"])
        CG = Steps(c_pool, ["xn"])
        RP = Steps(r_pe, ["qk"])
        RD = Steps(r_dve, ["rq", "rk", "n0", "n1", "n2", "n3", "rest0", "rest1", "rest2", "rest3", "guard", "rest4"])
        RA = Steps(r_act, [f"s{k}" for k in range(4)] + ["sd0", "sd1", "abs0", "abs1"]
                   + [f"{n}{k}" for n in ("hi", "mid") for k in range(4)] + ["hi4", "mid4"])
        RG = Steps(r_pool, ["ss0", "ss1", "p0", "p1", "bound", "own"] + [f"lo{k}" for k in five])
        EP = Steps(e_pe, [f"{n}{p}" for n in ("den", "z", "mean", "var") for p in two])
        ED = Steps(e_dve, ["rden"] + [f"{n}{p}" for n in ("y", "x", "xc", "rec", "sum") for p in two])
        EA = Steps(e_act, [f"{n}{p}" for n in ("sq", "sd") for p in two])
        EG = Steps(e_pool, ["xn0", "xn1"])

        def hi_plane(k):
            return 3 * k

        def half(ap, th):
            return ap[:, th * HALF:(th + 1) * HALF]

        def flat(ap):
            return ap.rearrange("p n t -> p (n t)")

        block = ctx.enter_context(nc.Block())

        @block.sync
        def _(sp):
            sp.dma_start(X[:, 0:2, :], x_v[:, 0:2, :]).then_inc(x_loaded_first, INC)
            sp.dma_start(WR[:, 0:3, :], a["L0_conv_pw_w"].rearrange("(k p) c -> p k c", p=P)).then_inc(w_loaded, INC)
            sp.dma_start(WR[:, 3, :], a["L0_conv_out_w"]).then_inc(w_loaded, INC)
            sp.dma_start(WR[:, 4:7, :], a["L1_attn_w_qkv"].rearrange("(k p) c -> p k c", p=P)).then_inc(w_loaded, INC)
            sp.dma_start(WR[:, 7, :], a["L1_attn_w_proj"]).then_inc(w_loaded, INC)
            for k, name in enumerate(PARAMS):
                sp.dma_start(PRr[NE * k:NE * (k + 1), :], a[name]).then_inc(w_loaded, INC)
            for k, name in enumerate(VECTORS):
                r = NE * len(PARAMS) + k
                sp.dma_start(PRr[r:r + 1, :], a[name].rearrange("(o c) -> o c", o=1)).then_inc(w_loaded, INC)
            for k, name in enumerate(["L1_attn_qn_w", "L1_attn_kn_w"]):
                sp.dma_start(qkw[:, 2 * k:2 * k + 2],
                             a[name].rearrange("(o c) -> o c", o=1).to_broadcast([P, 2])).then_inc(w_loaded, INC)
            sp.dma_start(br_b[:, :],
                         a["L1_ffn_br"].rearrange("(o c) -> o c", o=1).to_broadcast([P, NE])).then_inc(w_loaded, INC)
            sp.dma_start(X[:, 2:B, :], x_v[:, 2:B, :]).then_inc(x_loaded_rest, INC)
            sp.dma_start(Wr[:, :], a["L1_ffn_Wr"]).then_inc(ffn_w_loaded, INC)
            sp.dma_start(bo[:, :], a["L1_ffn_bo"]).then_inc(ffn_w_loaded, INC)

            with sp.Fori(0, B // 2) as i:
                for par in range(2):
                    b = i * 2 + par
                    sp.wait_ge(a_lo, b * 2 + 2)
                    sp.dma_start(parts0[ds(b, 1)].rearrange("o k p t -> p (o k) t"), parts[par])\
                        .then_inc(a_stored[par], INC)
                    sp.dma_start(values0[ds(b, 1)].rearrange("o p t -> p (o t)"), v_out[par])\
                        .then_inc(a_stored[par], INC)

            for par in range(2):
                sp.wait_ge(a_stored[par], B * INC)

            def load_k(b, par):
                for tile, kinds in ((K1, (3, 4, 3)), (K2, (5, 3, 4))):
                    for r, kind in enumerate(kinds):
                        src = parts0[ds(b, 1), kind].rearrange("o (n i) t -> i (o n) t", n=NH0)
                        sp.dma_start(tile[par][D0 * r:D0 * (r + 1), :, :], src).then_inc(k_loaded[par], INC)

            def load_q(b, th):
                for tile, kinds in ((Q1, (0, 0, 1)), (Q2, (0, 2, 1))):
                    for r, kind in reversed(list(enumerate(kinds))):
                        src = parts0[ds(b, 1), kind, :, th * HALF:(th + 1) * HALF]\
                            .rearrange("o (n i) t -> i (o n) t", n=NH0)
                        sp.dma_start(tile[th][D0 * r:D0 * (r + 1), :, :], src).then_inc(q_loaded[th], INC)

            def load_v(b, par):
                sp.dma_start(V0[par], values0[ds(b, 1)].rearrange("o p t -> p (o t)")).then_inc(v_loaded[par], INC)

            def feed(i, last=False):
                for st in range(2 * STEPS):
                    g = i * (2 * STEPS) + st
                    for r, part_made in enumerate((b_rhi, b_rmid, b_rlo)):
                        sp.wait_ge(part_made, g + 1)
                        for n in range(NH0):
                            sp.dma_start(RS[st % 2][GK * r:GK * (r + 1), n, :], rec_parts[GK * n:GK * (n + 1), r, :])\
                                .then_inc(rs_loaded[st % 2], INC)
                    par, q = st // STEPS, st % STEPS
                    b, sub = i * 2 + par, i * TURN + par * (TURN // 2)
                    if not (last and par == 1) and q in (1, 2):
                        sp.wait_ge(b_qk, sub * 2 + 2 * SUB * (STEPS // 2) * q)
                        load_q(b + 1, q - 1)
                    if not last and q == 3:
                        sp.wait_ge(b_qk, sub * 2 + TURN)
                        load_k(b + 2, par)
                    first_image = isinstance(i, int) and i == 0 and par == 0
                    if q == 0 and not first_image and not (last and par == 1):
                        sp.wait_ge(b_pv, sub)
                        load_v(b + 1, 1 - par)

            load_k(0, 0)
            for th in range(2):
                load_q(0, th)
            load_v(0, 0)
            load_k(1, 1)
            load_v(1, 1)
            feed(0)
            with sp.Fori(1, B // 2 - 1) as i:
                feed(i)
            feed(B // 2 - 1, last=True)

            with sp.Fori(0, B // 2) as i:
                for th in range(2):
                    RG.after(sp, i * 2 + th, "lo4")
                    pl = planes[th]

                    def rows(dram, r, k):
                        return dram[r:r + k, ds(i * P, P), th * HALF:(th + 1) * HALF].rearrange("r h t -> h r t")
                    for d in range(2):
                        q, k, r = hi_plane(d), hi_plane(2 + d), 6 * d
                        sp.dma_start(rows(qstack, r, 3), pl[:, q:q + 1, :].to_broadcast([P, 3, HALF]))\
                            .then_inc(c_stored[th], INC)
                        sp.dma_start(rows(qstack, r + 3, 2), pl[:, q + 1:q + 2, :].to_broadcast([P, 2, HALF]))\
                            .then_inc(c_stored[th], INC)
                        sp.dma_start(rows(qstack, r + 5, 1), pl[:, q + 2:q + 3, :]).then_inc(c_stored[th], INC)
                        sp.dma_start(rows(kstack, r, 3), pl[:, k:k + 3, :]).then_inc(c_stored[th], INC)
                        sp.dma_start(rows(kstack, r + 3, 2), pl[:, k:k + 2, :]).then_inc(c_stored[th], INC)
                        sp.dma_start(rows(kstack, r + 5, 1), pl[:, k:k + 1, :]).then_inc(c_stored[th], INC)
                    g = hi_plane(4)
                    sp.dma_start(rows(qstack, STACK, 3), pl[:, g:g + 3, :]).then_inc(c_stored[th], INC)

            for th in range(2):
                sp.wait_ge(c_stored[th], B // 2 * C_STORES * INC)
            sp.wait_ge(d_init, 4)

            def load_group(g, par):
                sp.dma_start(Qs[par][0:QROWS, :, :], qstack[:, ds(g * HG, HG), :]).then_inc(d_loaded[par], INC)
                sp.dma_start(Ks[par][0:KROWS, :, :], kstack[:, ds(g * HG, HG), :]).then_inc(d_loaded[par], INC)

            def store_group(g, par):
                sp.wait_ge(d_ev, g * 2 + 2)
                for j in range(HG):
                    sp.dma_start(attn1[ds(g * HG + j, 1)].rearrange("o r t -> (o r) t"),
                                 Oe[par][32 * j:32 * j + 3, :]).then_inc(d_stored[par], INC)

            for par in range(2):
                load_group(par, par)
            with sp.Fori(0, NG // 2 - 1) as i:
                for par in range(2):
                    g = i * 2 + par
                    sp.wait_ge(d_qk, g * NC + NC)
                    load_group(g + 2, par)
                    store_group(g, par)
            for par in range(2):
                store_group(NG - 2 + par, par)

            for par in range(2):
                sp.wait_ge(d_stored[par], NG // 2 * HG * INC)
            sp.wait_ge(d_pv, NG * NC)
            for w, name in ((W1, "L1_ffn_W1"), (W2, "L1_ffn_W2"), (Wo, "L1_ffn_Wo")):
                sp.dma_start(w, a[name].rearrange("e d h -> d e h")).then_inc(ffn_w_loaded, INC)

            def load_pair(i):
                EP.after(sp, i - 1, "z1")
                for par in range(2):
                    for d in range(2):
                        sp.dma_start(num[par][d:P:2, :], attn1[ds((i * 2 + par) * NH1, NH1), d, :])\
                            .then_inc(e_loaded, INC)
                sp.dma_start(den, attn1[ds(i * P, P), 2, :]).then_inc(e_loaded, INC)
            peeled(sp, B // 2, load_pair)

            with sp.Fori(0, B) as i:
                for th in range(2):
                    sp.wait_ge(g_res, i * 2 + th + 1)
                    sp.dma_start(out_v[:, ds(i, 1), th * HALF:(th + 1) * HALF].rearrange("p o t -> p (o t)"),
                                 res[th]).then_inc(out_stored[th], INC)
            for th in range(2):
                sp.wait_ge(out_stored[th], B * INC)

        @block.gpsimd
        def _(pool):
            pool.memset(ident[:, :], 0.0).then_inc(ident_set, 1)
            pool.memset(causal[:, :], BIG).then_inc(ident_set, 1)
            pool.memset(mean_w[:, :], 1.0 / P).then_inc(eps_set, 1)
            pool.memset(eps_c[:, 0:1], LN_EPS).then_inc(eps_set, 1)
            pool.memset(eps_c[:, 1:2], RMS_EPS).then_inc(eps_set, 1)
            pool.memset(eps_c[:, 2:3], 0.0).then_inc(eps_set, 1)
            pool.wait_ge(ident_set, 2)
            pool.affine_select(out=ident[:, :], in_=ident[:, :], compare_op=ALU.not_equal, fill=1.0, base=0,
                               pattern=[[-1, P]], channel_multiplier=1).then_inc(ident_set, 1)
            pool.affine_select(out=causal[:, :], in_=causal[:, :], compare_op=ALU.is_ge, fill=0.0, base=0,
                               pattern=[[1, P]], channel_multiplier=-1).then_inc(ident_set, 1)

            pool.wait_ge(ident_set, 4)
            made = [0]

            def constant(ins):
                made[0] += 1
                ins.then_inc(b_const, 1)
                pool.wait_ge(b_const, made[0])
            constant(pool.tensor_copy(identb, ident[:, :]))
            constant(pool.memset(spread[0:3 * GK], 0.0))
            constant(pool.memset(window, 0.0))
            for par in range(2):
                constant(pool.memset(K2[par][3 * GK:P], 0.0))
            for r in range(3):
                v = flat(spread[GK * r:GK * (r + 1)]).rearrange("p (y x) -> p y x", x=GK)
                constant(pool.affine_select(out=v, in_=v, compare_op=ALU.not_equal, fill=1.0, base=0,
                                            pattern=[[-1, H], [0, GK]], channel_multiplier=1))
            for j in range(RB):
                at = GK - RB + j
                constant(pool.memset(window[GK * j:GK * (j + 1), at:at + 1], 1.0))
            for par in range(2):
                v = K2[par][3 * GK:P].rearrange("p n (y x) -> p n y x", x=GK)
                constant(pool.affine_select(out=v, in_=v, compare_op=ALU.not_equal, fill=-1.0, base=0,
                                            pattern=[[0, NH0], [-1, H], [0, GK]], channel_multiplier=1))

            with pool.Fori(0, B // 2) as i:
                for par in range(2):
                    b = i * 2 + par
                    for k in range(2):
                        pool.wait_ge(a_hi, b * 5 + 4 + k)
                        pool.tensor_tensor(parts[par][:, 3 * k + 2, :], rest0[k], parts[par][:, 3 * k + 1, :],
                                           ALU.subtract).then_inc(a_lo, 1)

            def pool_b(i):
                for par in range(2):
                    g = i * 2 + par
                    pool.wait_ge(b_rmid, g + 1)
                    if par:
                        pool.wait_ge(rs_loaded[0], i * (RS_LOADS * INC) + RS_LOADS * INC)
                    else:
                        wait(pool, rs_loaded[1], i * (RS_LOADS * INC))
                    pool.tensor_tensor(rec_parts[:, 2, :], rec_rest, rec_parts[:, 1, :], ALU.subtract).then_inc(b_rlo, 1)
            peeled(pool, NSTEP // 2, pool_b)

            pool.wait_ge(b_out, NSTEP)
            pool.memset(V1, 1.0).then_inc(ones_set, 1)

            def pool_c(i):
                for par in range(2):
                    n, m = i * 2 + par, i * 2 + (par - 2)
                    front, back = turn_parts(i)
                    q0, q1, k0, k1, _ = nrm
                    if back:
                        for k in range(2):
                            RA.after(pool, m, f"s{2 * k + 1}")
                            pool.tensor_tensor(ss[k], ss[k], sqa[k], ALU.add).then_inc(r_pool, 1)
                        RD.after(pool, m, "n3")
                        pool.tensor_tensor(tmp[2], q0, k0, ALU.mult).then_inc(r_pool, 1)
                        pool.tensor_tensor(tmp[3], q1, k1, ALU.mult).then_inc(r_pool, 1)
                        RA.after(pool, m, "abs1")
                        pool.tensor_tensor(tmp[0], tmp[0], tmp[1], ALU.add).then_inc(r_pool, 1)
                        RG.after(pool, m, "p1")
                        pool.tensor_tensor(tmp[2], tmp[2], tmp[3], ALU.add).then_inc(r_pool, 1)
                    if front:
                        CD.after(pool, n, "rec")
                        RP.after(pool, m, "qk")
                        if par == 0:
                            wait(pool, c_kept, i)
                        pool.tensor_tensor(xn[par], xc[par], sq[par], ALU.mult).then_inc(c_pool, 1)
                    if back:
                        for k in range(5):
                            RA.after(pool, m, f"mid{k}")
                            r = hi_plane(k)
                            pool.tensor_tensor(planes[par][:, r + 2, :], rst[k], planes[par][:, r + 1, :],
                                               ALU.subtract).then_inc(r_pool, 1)
            turns_c(pool, pool_c)

            for th in range(2):
                pool.wait_ge(c_stored[th], B // 2 * C_STORES * INC)
            RP.after(pool, B - 1, "qk")
            RD.after(pool, B - 1, "rest4")
            for s in range(2):
                pool.memset(Qs[s], 0.0).then_inc(d_init, 1)
                pool.memset(Ks[s], -1.0).then_inc(d_init, 1)
            for s in range(2):
                pool.memset(Vg[s], 0.0).then_inc(d_vinit, 1)
            CA.after(pool, B - 1, "cv")
            pool.wait_ge(d_vinit, 2)

            def group_values(g, par):
                pool.tensor_copy(Vg[par][:, :, 0:3 * HG], V1[:, :, ds(g * (3 * HG), 3 * HG)]).then_inc(d_v, 1)

            def pool_d(i):
                for par in range(2):
                    g = i * 2 + par
                    wait(pool, d_pv, g * NC - NC)
                    group_values(g, par)
            peeled(pool, NG // 2, pool_d)

            pool.wait_ge(d_pv, NG * NC)
            pool.memset(expand, 0.0).then_inc(e_set, 1)
            pool.memset(xsum, 0.0).then_inc(e_set, 1)
            pool.wait_ge(e_set, 2)
            for par in range(2):
                e_v = expand[:, par, :].rearrange("p (h d) -> p h d", d=2)
                pool.affine_select(out=e_v, in_=e_v, compare_op=ALU.not_equal, fill=1.0, base=-NH1 * par,
                                   pattern=[[-1, NH1], [0, 2]], channel_multiplier=1).then_inc(e_set, 1)
            pool.memset(sel[0:NE, :, :], 0.0).then_inc(f_set, 1)
            pool.wait_ge(f_set, 1)
            pool.affine_select(out=sel[0:NE, :, :], in_=sel[0:NE, :, :], compare_op=ALU.not_equal, fill=1.0,
                               base=0, pattern=[[-1, NE], [0, P]], channel_multiplier=1).then_inc(f_set, 1)

            with pool.Fori(0, B // 2) as i:
                for par in range(2):
                    ED.after(pool, i, f"rec{par}")
                    pool.tensor_tensor(Yall[:, ds(i * 2 + par, 1), :].rearrange("p o t -> p (o t)"),
                                       exc[par], esq[par], ALU.mult).then_inc(e_pool, 1)

        @block.scalar
        def _(act):
            act.wait_ge(w_turned, 1)
            w = bank(0, 2)
            act.activation(WT[:, 0:3 * P].rearrange("p (s n i) -> p n s i", s=3, n=NH0),
                           w[:, 0:3 * P].rearrange("p (n s i) -> p n s i", s=3, n=NH0), ACT.Copy).then_inc(w_copied, 1)
            act.activation(wt("out"), w[:, 3 * P:4 * P], ACT.Copy).then_inc(w_copied, 1)
            act.activation(wt("qk1").rearrange("p (s d h) -> p s h d", s=2, d=2),
                           w[:, 4 * P:6 * P].rearrange("p (s h d) -> p s h d", s=2, d=2), ACT.Copy).then_inc(w_copied, 1)
            act.activation(WT[:, 6 * P:8 * P], w[:, 6 * P:8 * P], ACT.Copy).then_inc(w_copied, 1)
            act.wait_ge(param_step, 3)
            act.activation(cv(c_sd, 17), cv(c_sd, 17), ACT.Sqrt).then_inc(param_sd, 1)

            def act_a(i):
                for par in range(2):
                    b = i * 2 + par
                    wait(act, a_stored[par], i * (2 * INC))
                    for k in range(2):
                        act.wait_ge(a_mm, b * 3 + k + 1)
                        act.activation(parts[par][:, 3 * k, :], bank(2 * k, 2), ACT.Copy).then_inc(a_hi, 1)
                    act.wait_ge(a_mm, b * 3 + 3)
                    act.activation(v_out[par], bank(4, 2), ACT.Copy).then_inc(a_hi, 1)
                    for k in range(2):
                        act.wait_ge(a_rest, b * 2 + k + 1)
                        act.activation(parts[par][:, 3 * k + 1, :], rest0[k], ACT.Copy).then_inc(a_hi, 1)
            peeled(act, B // 2, act_a)

            act.wait_ge(eps_set, 4)
            act.activation(eps_c[:, 3:4], eps_c[:, 2:3], ACT.Exp)

            def act_b(i, subs):
                for k in subs:
                    K = i * TURN + k
                    if k % NH0 == 0 and in_range(i, k, L_MOVE):
                        c = (k - L_MOVE) % TURN
                        q = c // SUB % STEPS
                        at = (q % 2) * QS + c // NH0 % 2 * P
                        act.wait_ge(b_moved, i * (TURN // NH0) + k // NH0)
                        act.activation(Q2[q // 2][3 * GK:P, :, at:at + P],
                                       bank(2)[3 * GK:P].rearrange("p (n q) -> p n q", n=NH0),
                                       ACT.Copy).then_inc(b_guard, 1)
                    if k % SUB == 2 and in_range(i, k, L_SUM + SUB):
                        g = i * (2 * STEPS) + (k - L_SUM - SUB) // SUB
                        act.wait_ge(b_sum, g * SUB + SUB)
                        wait(act, b_rec, g)
                        act.activation(sums, bank(7)[:, 0:QS], ACT.Copy).then_inc(b_summed, 1)
                    if k % SUB == 3 and in_range(i, k, L_SUM + SUB + 1):
                        st = (k - L_SUM - SUB - 1) // SUB
                        act.wait_ge(b_rec, i * (2 * STEPS) + st + 1)
                        wait_moved(act, i, st - 1)
                        act.activation(rec_parts[:, 0, :], rec, ACT.Copy).then_inc(b_rhi, 1)
                    if k % SUB == 4 and in_range(i, k, L_SUM + SUB + 2):
                        g = i * (2 * STEPS) + (k - L_SUM - SUB - 2) // SUB
                        act.wait_ge(b_rrest, g + 1)
                        act.activation(rec_parts[:, 1, :], rec_rest, ACT.Copy).then_inc(b_rmid, 1)
                    if in_range(i, k, L_EXP):
                        c = (k - L_EXP) % TURN
                        for hp in range(2):
                            act.wait_ge(b_qk, K * 2 + (hp + 1 - 2 * L_EXP))
                            wait(act, b_pv, K + (1 - L_EXP - 2 * SUB))
                            act.activation(E0[c // SUB % 2][:, c % SUB, 2 * hp:2 * hp + 2, :].rearrange("p n q -> p (n q)"),
                                           bank(2 + hp), ACT.Exp, scale=SCALE0).then_inc(b_exp, 1)
                    if k % SUB == L_OUT % SUB and in_range(i, k, L_OUT):
                        g0 = (k - L_OUT) // SUB
                        act.wait_ge(b_pv, i * TURN + (g0 + 1) * SUB)
                        act.activation(Yall[:, ds(i * 2 + g0 // STEPS, 1), (g0 % STEPS) * QS:(g0 % STEPS + 1) * QS]
                                       .rearrange("p o t -> p (o t)"), bank(6)[:, 0:QS], ACT.Copy).then_inc(b_out, 1)
            turns(act, act_b)

            def act_c(i):
                for par in range(2):
                    n, m = i * 2 + par, i * 2 + (par - 2)
                    front, back = turn_parts(i)
                    pl = planes[par]
                    if back:
                        RP.after(act, m, "qk")
                        RD.after(act, m - 1, "guard")
                        for k in range(4):
                            act.activation((ss, sqa)[k % 2][k // 2], bank(4 + k), ACT.Square).then_inc(r_act, 1)
                    if front and par == 1:
                        CG.after(act, n - 1, "xn")
                        RP.after(act, m, "qk")
                        act.activation(xn_high, half(xn[0], 1), ACT.Copy).then_inc(c_kept, 1)
                    if front:
                        CD.after(act, n, "xc")
                        act.activation(sq[par], xc[par], ACT.Square).then_inc(c_act, 1)
                    if back:
                        for k in range(2):
                            RG.after(act, m, f"ss{k}")
                            act.activation(ss[k], ss[k], ACT.Sqrt, bias=eps_c[:, 1:2], scale=0.5).then_inc(r_act, 1)
                    if front:
                        CP.after(act, n, "var")
                        act.activation(sq[par], bank(0, 2), ACT.Sqrt, bias=eps_c[:, 0:1]).then_inc(c_act, 1)
                    if back:
                        for k in range(2):
                            RD.after(act, m, f"n{k}")
                            act.activation(tmp[k], nrm[k], ACT.Abs, scale=cv(c_ck + k)).then_inc(r_act, 1)
                        wait(act, c_stored[par], (i - 1) * (C_STORES * INC))
                        for k in range(4):
                            RD.after(act, m, f"n{k}")
                            act.activation(pl[:, hi_plane(k), :], nrm[k], ACT.Copy).then_inc(r_act, 1)
                        for k in range(4):
                            RD.after(act, m, f"rest{k}")
                            act.activation(pl[:, hi_plane(k) + 1, :], rst[k], ACT.Copy).then_inc(r_act, 1)
                        RD.after(act, m, "guard")
                        act.activation(pl[:, hi_plane(4), :], nrm[4], ACT.Copy).then_inc(r_act, 1)
                    if front:
                        CP.after(act, n, "val")
                        act.wait_ge(ones_set, 1)
                        dst = V1[:, :, ds(n * (3 * NH1), 3 * NH1)].rearrange("p s (h e) -> p s h e", e=3)
                        act.activation(dst[:, :, :, 0:2], bank(2, 2).rearrange("p (s h d) -> p s h d", s=NT, d=2),
                                       ACT.Copy).then_inc(c_act, 1)
                    if back:
                        RD.after(act, m, "rest4")
                        act.activation(pl[:, hi_plane(4) + 1, :], rst[4], ACT.Copy).then_inc(r_act, 1)
            turns_c(act, act_c)

            act.wait_ge(d_init, 4)
            act.activation(eps_c[:, 4:5], eps_c[:, 2:3], ACT.Exp)

            def act_d(i):
                for par in range(2):
                    for c in range(NC):
                        k = i * (2 * NC) + (par * NC + c)
                        s = (par * NC + c) % 2
                        act.wait_ge(d_qk, k + 1)
                        wait(act, d_pv, k - (PRING - 1))
                        act.activation(PR1[(par * NC + c) % PRING], bank(UPC * s, UPC), ACT.Exp).then_inc(d_exp, 1)
            peeled(act, NG // 2, act_d)

            with act.Fori(0, B // 2) as i:
                for par in range(2):
                    ED.after(act, i, f"xc{par}")
                    act.activation(esq[par], exc[par], ACT.Square).then_inc(e_act, 1)
                for par in range(2):
                    EP.after(act, i, f"var{par}")
                    act.activation(esq[par], bank(2 * par, 2), ACT.Sqrt, bias=eps_c[:, 0:1]).then_inc(e_act, 1)

            act.wait_ge(f_dve, 3)
            act.activation(lw, lg, ACT.Exp).then_inc(f_exp, 1)
            for e in range(0, NE, 2):
                act.wait_ge(f_wbps, e + 1)
                act.activation(wB[:, e, :], bank(4, 2), ACT.Copy).then_inc(f_wbA, 1)

            def act_f(i):
                def relu2(k):
                    n, e = i * (2 * NE) + k, k % NE
                    act.wait_ge(g_h2, n + 1)
                    wait(act, g_w, n - 1)
                    act.activation(h2[k % 2], bank(2 + k % 2), ACT.Relu, bias=cv(c_B2 + e),
                                   scale=cv(c_A2 + e)).then_inc(g_r2, 1)
                for k in range(2 * NE):
                    n, e = i * (2 * NE) + k, k % NE
                    act.wait_ge(g_h1, n + 1)
                    wait(act, g_h2, n - 1)
                    act.activation(h1[k % 2], bank(k % 2), ACT.Relu, bias=cv(c_B1 + e),
                                   scale=cv(c_A1 + e)).then_inc(g_r1, 1)
                    if k:
                        relu2(k - 1)
                relu2(2 * NE - 1)
            peeled(act, B, act_f)

        @block.tensor
        def _(pe):
            pe.wait_ge(ident_set, 4)
            pe.wait_ge(w_loaded, W_LOADS * INC)
            for k in range(8):
                mm = pe.transpose(ps[:, k * P:(k + 1) * P], WR[:, k, :], ident[:, :])
            mm.then_inc(w_turned, 1)
            pe.transpose(bank(2)[:, 0:NPR], PRr[0:NPR, :], ident[0:NPR, 0:NPR]).then_inc(w_turned, 1)

            pe.wait_ge(w_copied, 4)

            def pe_a(i):
                for par in range(2):
                    b = i * 2 + par
                    pe.wait_ge(a_bn, b + 1)
                    for k, w in enumerate(("q0", "k0")):
                        wait(pe, a_rest, b * 2 + (k - 1))
                        for th in range(2):
                            mm = pe.matmul(bank(2 * k + th), wt(w), half(xbn[par], th), start=True, stop=True)
                        mm.then_inc(a_mm, 1)
                    wait(pe, a_hi, b * 5 - 2)
                    for t in range(NT):
                        mm = pe.matmul(bank(4, 2)[:, t * P:(t + 1) * P], xbn[par][:, t * P:(t + 1) * P], wt("v0"),
                                       start=True, stop=True)
                    mm.then_inc(a_mm, 1)
            peeled(pe, B // 2, pe_a)

            pe.wait_ge(a_hi, B * 5)
            pe.wait_ge(a_rest, B * 2)

            pe.wait_ge(b_const, 14)

            def sums_of(i, k, K):
                if in_range(i, k, L_SUM):
                    c = (k - L_SUM) % TURN
                    kb, sl = c % SUB, c // SUB % 2
                    if kb == 0:
                        wait(pe, b_summed, i * (2 * STEPS) + (k - L_SUM) // SUB)
                    pe.wait_ge(b_exp, K * 2 + (2 - 2 * L_SUM))
                    for n in range(NH0):
                        mm = pe.matmul(bank(7)[GK * n:GK * (n + 1), 0:QS],
                                       window[:, GK - RB - RB * kb:2 * GK - RB - RB * kb], E0[sl][:, kb, n, :],
                                       start=kb == 0, stop=kb == SUB - 1, skip_group_check=True)
                    mm.then_inc(b_sum, 1)

            def pe_b(i, subs):
                for k in subs:
                    K = i * TURN + k
                    if k % NH0 == 0 and in_range(i, k, L_MOVE):
                        pe.wait_ge(b_max, K)
                        wait(pe, b_guard, i * (TURN // NH0) + (k // NH0 - 1))
                        wait(pe, b_exp, K * 2 + (-1 - 2 * L_EXP))
                        for n in range(NH0):
                            mm = pe.matmul(bank(2)[3 * GK:P, n * P:(n + 1) * P],
                                           maxima[:, (k + n - L_MOVE) % SUB, :], identb, start=True, stop=True)
                        mm.then_inc(b_moved, 1)
                    if in_range(i, k, 0):
                        par, q, qb, n = k // (TURN // 2), k // SUB % STEPS, k // NH0 % 2, k % NH0
                        if k % (TURN // 2) == 0:
                            pe.wait_ge(k_loaded[par], i * (K_LOADS * INC) + K_LOADS * INC)
                        if q % 2 == 0 and k % SUB == 0:
                            pe.wait_ge(q_loaded[q // 2], (i * 2 + (par + 1)) * (Q_LOADS * INC))
                        wait(pe, b_max, K)
                        at = (q % 2) * QS + qb * P
                        for th in range(2):
                            mm = pe.matmul(bank(th), Q1[q // 2][0:3 * D0, n, at:at + P],
                                           half(K1[par][0:3 * D0, n, :], th), start=True, stop=True)
                        mm.then_inc(b_raw, 1)
                    if k % NH0 == 0:
                        sums_of(i, k, K)
                    for hp in range(2):
                        if in_range(i, k, L_EXP):
                            c = (k - L_EXP) % TURN
                            par, q, kb = c // (TURN // 2), c // SUB % STEPS, c % SUB
                            at = (q % 2) * QS
                            if k % NH0 == 0 and hp == 0 and in_range(i, k, L_MOVE):
                                wait(pe, b_guard, i * (TURN // NH0) + k // NH0)
                            if kb == 0 and hp == 0:
                                pe.wait_ge(b_guard, (i * (TURN // SUB) + ((k - L_EXP) // SUB + 1)) * (SUB // NH0))
                            wait(pe, b_exp, K * 2 + (hp - 1 - 2 * L_EXP))
                            for n in (2 * hp, 2 * hp + 1):
                                o = bank(2 + hp)[:, (n % 2) * QS:(n % 2 + 1) * QS]
                                pe.matmul(o, K1[par][0:3 * D0, n, kb * P:(kb + 1) * P],
                                          Q1[q // 2][0:3 * D0, n, at:at + QS], start=True, stop=False)
                                mm = pe.matmul(o, K2[par][:, n, kb * P:(kb + 1) * P],
                                               Q2[q // 2][:, n, at:at + QS], start=False, stop=True)
                            mm.then_inc(b_qk, 1)
                        if in_range(i, k, L_NORM):
                            c = (k - L_NORM) % TURN
                            if c % SUB == 0 and hp == 0:
                                wait_moved(pe, i, (k - L_NORM) // SUB)
                            wait(pe, b_norm, K * 2 + (hp - 1 - 2 * L_NORM))
                            pe.matmul(bank(4 + hp), spread[0:3 * GK, c % SUB, :],
                                      RS[c // SUB % 2][0:3 * GK, 2 * hp:2 * hp + 2, :].rearrange("p n q -> p (n q)"),
                                      start=True, stop=True).then_inc(b_spread, 1)
                    if k % NH0:
                        sums_of(i, k, K)
                    if in_range(i, k, L_PV):
                        c = (k - L_PV) % TURN
                        par, kb, sl = c // (TURN // 2), c % SUB, c // SUB % 2
                        if c % (TURN // 2) == 0:
                            pe.wait_ge(v_loaded[par], (i + (k - L_PV) // TURN) * INC + INC)
                        if kb == 0:
                            wait(pe, b_out, i * (2 * STEPS) + (k - L_PV) // SUB)
                        pe.wait_ge(b_norm, K * 2 + (2 - 2 * L_PV))
                        for n in range(NH0):
                            v = kb * P + D0 * n
                            mm = pe.matmul(bank(6)[D0 * n:D0 * (n + 1), 0:QS], V0[par][:, v:v + D0], E0[sl][:, kb, n, :],
                                           start=kb == 0, stop=kb == SUB - 1, skip_group_check=True)
                        mm.then_inc(b_pv, 1)
            turns(pe, pe_b)

            def pe_c(i):
                def image(ap, n, th):
                    return ap[:, ds(n, 1), th * HALF:(th + 1) * HALF].rearrange("p o t -> p (o t)")
                for par in range(2):
                    n, m = i * 2 + par, i * 2 + (par - 2)
                    front, back = turn_parts(i)
                    if front:
                        CA.after(pe, n - 1, "sd")
                        for th in range(2):
                            mm = pe.matmul(bank(th), wt("out"), image(Yall, n, th), start=True, stop=True)
                        mm.then_inc(c_pe, 1)
                    if back:
                        RD.after(pe, m - 1, "n3")
                        CG.after(pe, i * 2 - 1, "xn")
                        pe.wait_ge(c_kept, i)
                        xns = [(half(xn[0], 0), xn_high)[par], half(xn[1], par)]
                        for k in range(4):
                            for im in range(2):
                                mm = pe.matmul(bank(4 + k)[NH1 * im:NH1 * (im + 1), :],
                                               wt("qk1")[:, NH1 * k:NH1 * (k + 1)], xns[im],
                                               start=True, stop=True)
                        mm.then_inc(r_pe, 1)
                    if front:
                        CD.after(pe, n, "x")
                        CA.after(pe, n - 1, "cv")
                        for th in range(2):
                            mm = pe.matmul(bank(2 + th), mean_w[:, :], image(X, n, th), start=True, stop=True)
                        mm.then_inc(c_pe, 1)
                        CA.after(pe, n, "sq")
                        for th in range(2):
                            mm = pe.matmul(bank(th), mean_w[:, :], half(sq[par], th), start=True, stop=True)
                        mm.then_inc(c_pe, 1)
                        CG.after(pe, n, "xn")
                        for t in range(NT):
                            mm = pe.matmul(bank(2, 2)[:, t * P:(t + 1) * P], xn[par][:, t * P:(t + 1) * P], wt("v1"),
                                           start=True, stop=True)
                        mm.then_inc(c_pe, 1)
            pe.wait_ge(b_out, NSTEP)
            turns_c(pe, pe_c)

            RD.after(pe, B - 1, "n3")

            def scores1(i, par, c):
                if c == 0:
                    pe.wait_ge(d_loaded[par], i * (2 * INC) + 2 * INC)
                wait(pe, d_exp, i * (2 * NC) + (par * NC + c - 1))
                at = UPC * ((par * NC + c) % 2)
                for h in range(HG - 1):
                    for s, j, t, n in runs(CHUNKS[c], False):
                        pe.matmul(bank(at + h)[:, s * P:(s + n) * P], Ks[par][:, h, j * P:(j + 1) * P],
                                  Qs[par][:, h, t * P:(t + n) * P], start=True, stop=True)
                h = HG - 1
                for s, (j, t) in enumerate(CHUNKS[c]):
                    mm = pe.matmul(bank(at + s)[:, UPC * P:HG * P], Ks[par][:, h, j * P:(j + 1) * P],
                                   Qs[par][:, h, t * P:(t + 1) * P], start=True, stop=True)
                mm.then_inc(d_qk, 1)

            def values1(i, par, c):
                g = i * 2 + par
                if MASKS[c]:
                    pe.wait_ge(d_mask, g * sum(MASKS) + sum(MASKS[:c + 1]))
                else:
                    pe.wait_ge(d_exp, g * NC + (c + 1))
                if c == 0:
                    pe.wait_ge(d_v, g + 1)
                    wait(pe, d_ev, g * 2 - 1)
                if c == 1:
                    wait(pe, d_ev, g * 2)
                pr = PR1[(par * NC + c) % PRING]
                for s, j, t, n in runs(CHUNKS[c], True):
                    high = t >= NT // 2
                    first = j == 0 and t in (0, NT // 2)
                    last = (j, t + n) in ((NT // 2 - 1, NT // 2), (NT - 1, NT))
                    o = bank(7 if high else 6)[:, (t - high * NT // 2) * P:(t + n - high * NT // 2) * P]
                    for h in range(HG):
                        if h < HG - 1:
                            rhs = pr[:, h * HALF + s * P:h * HALF + (s + n) * P]
                        else:
                            rhs = pr.rearrange("p (u c) -> p u c", u=UPC)[:, s:s + n, UPC * P:HG * P]
                        mm = pe.matmul(o[32 * h:32 * (h + 1), :], Vg[par][:, j, 3 * h:3 * h + 32], rhs,
                                       start=first, stop=last, skip_group_check=True)
                mm.then_inc(d_pv, 1)

            def pe_d(i, first=False, last=False):
                for k in range(2 * NC):
                    nk = k + 2
                    if nk < 2 * NC:
                        scores1(i, nk // NC, nk % NC)
                    elif not last:
                        scores1(i + 1, 0, nk - 2 * NC)
                    if k:
                        values1(i, (k - 1) // NC, (k - 1) % NC)
                    elif not first:
                        values1(i - 1, 1, NC - 1)

            scores1(0, 0, 0)
            scores1(0, 0, 1)
            pe_d(0, first=True)
            with pe.Fori(1, NG // 2 - 1) as i:
                pe_d(i)
            pe_d(NG // 2 - 1, last=True)
            values1(NG // 2 - 1, 1, NC - 1)

            pe.wait_ge(d_exp, NG * NC)
            pe.wait_ge(d_ev, 2 * NG)
            pe.wait_ge(e_set, 4)

            def pe_e(i):
                def image(ap, par, th):
                    return ap[:, ds(i * 2 + par, 1), th * HALF:(th + 1) * HALF].rearrange("p o t -> p (o t)")
                for par in range(2):
                    ED.after(pe, i, "rden")
                    ED.after(pe, i - 1, f"xc{par}")
                    for th in range(2):
                        mm = pe.matmul(bank(4 + 2 * par + th), expand[:, par, :], half(rden, th), start=True, stop=True)
                    mm.then_inc(e_pe, 1)
                for par in range(2):
                    ED.after(pe, i, f"y{par}")
                    EA.after(pe, i - 1, f"sd{par}")
                    for th in range(2):
                        mm = pe.matmul(bank(2 * par + th), wt("proj"), half(num[par], th), start=True, stop=True)
                    mm.then_inc(e_pe, 1)
                for par in range(2):
                    ED.after(pe, i, f"x{par}")
                    for th in range(2):
                        mm = pe.matmul(bank(4 + 2 * par + th), mean_w[:, :], image(X, par, th), start=True, stop=True)
                    mm.then_inc(e_pe, 1)
                for par in range(2):
                    EA.after(pe, i, f"sq{par}")
                    for th in range(2):
                        mm = pe.matmul(bank(2 * par + th), mean_w[:, :], half(esq[par], th), start=True, stop=True)
                    mm.then_inc(e_pe, 1)
            peeled(pe, B // 2, pe_e)

            pe.wait_ge(ffn_w_loaded, FFN_LOADS * INC)
            ED.after(pe, B // 2 - 1, "sum1")
            for t in range(NT):
                mm = pe.matmul(bank(0)[:, t * NE:(t + 1) * NE], xsum[:, t * P:(t + 1) * P], Wr[:, :],
                               start=True, stop=True)
            mm.then_inc(f_mm, 1)
            pe.wait_ge(f_dve, 6)
            for t in range(NT):
                mm = pe.transpose(bank(2, 2)[0:NE, t * P:(t + 1) * P], lw[:, t, :], ident[:, :])
            mm.then_inc(f_mm, 1)
            pe.wait_ge(f_dve, 7)
            pe.wait_ge(f_set, 2)
            for e in range(NE):
                wait(pe, f_wbA if e % 2 == 0 else f_wbV, e // 2)
                for th in range(2):
                    mm = pe.matmul(bank(4 + 2 * (e % 2) + th), sel[0:NE, e, :], wT[0:NE, th * HALF:(th + 1) * HALF],
                                   start=True, stop=True)
                mm.then_inc(f_wbps, 1)
            pe.wait_ge(f_wbA, NE // 2)
            pe.wait_ge(f_wbV, NE // 2)

            def pe_f(i):
                def second(k):
                    n = i * (2 * NE) + k
                    pe.wait_ge(g_r1, n + 1)
                    wait(pe, g_r2, n - 1)
                    pe.matmul(bank(2 + k % 2), W2[:, k % NE, :], h1[k % 2], start=True, stop=True).then_inc(g_h2, 1)

                def third(k):
                    n, th, e = i * (2 * NE) + k, k // NE, k % NE
                    pe.wait_ge(g_w, n + 1)
                    if e == 0:
                        wait(pe, g_res, i * 2 + (th - 1))
                    pe.matmul(bank(4 + th), Wo[:, e, :], h2w[k % 2], start=e == 0, stop=False).then_inc(g_y3, 1)
                    if e == NE - 1:
                        pe.matmul(bank(4 + th), bo[:, :], wT[0:NE, th * HALF:(th + 1) * HALF],
                                  start=False, stop=True).then_inc(g_y, 1)
                for k in range(2 * NE):
                    n = i * (2 * NE) + k
                    wait(pe, g_r1, n - 1)
                    th = k // NE
                    pe.matmul(bank(k % 2), W1[:, k % NE, :],
                              Yall[:, ds(i, 1), th * HALF:(th + 1) * HALF].rearrange("p o t -> p (o t)"),
                              start=True, stop=True).then_inc(g_h1, 1)
                    if k >= 1:
                        second(k - 1)
                    if k >= 2:
                        third(k - 2)
                second(2 * NE - 1)
                third(2 * NE - 2)
                third(2 * NE - 1)
            peeled(pe, B, pe_f)

        @block.vector
        def _(dve):
            dve.wait_ge(w_turned, 2)
            dve.tensor_copy(PT[:, :], bank(2)[:, 0:NPR]).then_inc(param_step, 1)
            dve.wait_ge(param_step, 1)
            dve.tensor_scalar(cv(c_sd, NE), param("L1_ffn_v1"), BN_EPS, None, ALU.add).then_inc(param_step, 1)
            dve.tensor_scalar(cv(c_sd + NE, NE), param("L1_ffn_v2"), BN_EPS, None, ALU.add)
            dve.tensor_scalar(cv(c_sd + 2 * NE), param("L0_conv_bn_var"), BN_EPS0, None, ALU.add)\
                .then_inc(param_step, 1)
            step = [3]

            def chain(ins):
                step[0] += 1
                ins.then_inc(param_step, 1)
                dve.wait_ge(param_step, step[0])

            dve.wait_ge(param_sd, 1)
            dve.wait_ge(param_step, 3)
            chain(dve.reciprocal(cv(c_sd, 17), cv(c_sd, 17)))
            for c_A, c_B, k in ((c_A1, c_B1, "1"), (c_A2, c_B2, "2")):
                at = c_sd + NE * (k == "2")
                chain(dve.tensor_tensor(cv(c_A, NE), param("L1_ffn_g" + k), cv(at, NE), ALU.mult))
                chain(dve.tensor_tensor(cv(c_B, NE), param("L1_ffn_b" + k), param("L1_ffn_m" + k), ALU.subtract))
                chain(dve.tensor_tensor(cv(c_B, NE), cv(c_B, NE), cv(c_A, NE), ALU.mult))
                chain(dve.tensor_tensor(cv(c_B, NE), cv(c_B, NE), param("L1_ffn_be" + k), ALU.add))
            chain(dve.tensor_tensor(cv(c_scale0), param("L0_conv_bn_gamma"), cv(c_sd + 2 * NE), ALU.mult))
            chain(dve.tensor_tensor(cv(c_scale0), cv(c_scale0), param("L0_conv_dw_w"), ALU.mult))
            chain(dve.tensor_tensor(cv(c_bias0), param("L0_conv_bn_beta"), param("L0_conv_dw_w"), ALU.mult))
            chain(dve.tensor_tensor(cv(c_t), param("L0_conv_bn_mean"), cv(c_scale0), ALU.mult))
            chain(dve.tensor_tensor(cv(c_bias0), cv(c_bias0), cv(c_t), ALU.subtract))
            chain(dve.tensor_scalar(cv(c_wq, 2), qkw[:, 0:2], SCALE1, None, ALU.mult))
            chain(dve.scalar_tensor_tensor(cv(c_ck, 2), qkw[:, 2:4], -1.0, qkw[:, 2:4], ALU.mult, ALU.max))
            chain(dve.tensor_scalar(cv(c_ck, 2), cv(c_ck, 2), 2.0 ** 0.5, None, ALU.mult))

            def dve_a(i):
                for par in range(2):
                    b = i * 2 + par
                    wait(dve, a_mm, b * 3 - 3)
                    dve.tensor_scalar(xbn[par], X[:, ds(b, 1), :].rearrange("p o t -> p (o t)"), cv(c_scale0),
                                      cv(c_bias0), ALU.mult, ALU.add).then_inc(a_bn, 1)
                    for k in range(2):
                        dve.wait_ge(a_hi, b * 5 + (k + 1))
                        wait(dve, a_lo, b * 2 + (k - 1))
                        dve.tensor_tensor(rest0[k], bank(2 * k, 2), parts[par][:, 3 * k, :],
                                          ALU.subtract).then_inc(a_rest, 1)
            dve.wait_ge(x_loaded_first, INC)
            dve_a(0)
            dve.wait_ge(x_loaded_rest, INC)
            with dve.Fori(1, B // 2) as i:
                dve_a(i)

            def dve_b(i, subs):
                for k in subs:
                    K = i * TURN + k
                    if in_range(i, k, 0):
                        dve.wait_ge(b_raw, K + 1)
                        wait(dve, b_moved, i * (TURN // NH0) + (k // NH0 - 1))
                        dve.reduce_max(maxima[:, k % SUB, :], bank(0, 2).rearrange("p (y x) -> p y x", x=GK), AX_X)\
                            .then_inc(b_max, 1)
                    if in_range(i, k, L_NORM):
                        c = (k - L_NORM) % TURN
                        for hp in range(2):
                            e = E0[c // SUB % 2][:, c % SUB, 2 * hp:2 * hp + 2, :].rearrange("p n q -> p (n q)")
                            dve.wait_ge(b_spread, K * 2 + (hp + 1 - 2 * L_NORM))
                            dve.tensor_tensor(e, e, bank(4 + hp), ALU.mult).then_inc(b_norm, 1)
                    if k % SUB == 2 and in_range(i, k, L_SUM + SUB):
                        g = i * (2 * STEPS) + (k - L_SUM - SUB) // SUB
                        dve.wait_ge(b_summed, g + 1)
                        wait(dve, b_rrest, g)
                        dve.reciprocal(rec, sums).then_inc(b_rec, 1)
                    if k % SUB == 3 and in_range(i, k, L_SUM + SUB + 1):
                        g = i * (2 * STEPS) + (k - L_SUM - SUB - 1) // SUB
                        dve.wait_ge(b_rhi, g + 1)
                        wait(dve, b_rlo, g)
                        dve.tensor_tensor(rec_rest, rec, rec_parts[:, 0, :], ALU.subtract).then_inc(b_rrest, 1)
            turns(dve, dve_b)

            dve.wait_ge(b_out, NSTEP)

            def dve_c(i):
                for par in range(2):
                    n, m = i * 2 + par, i * 2 + (par - 2)
                    front, back = turn_parts(i)
                    q0, q1, k0, k1, guard = nrm
                    if front:
                        xi = X[:, ds(n, 1), :].rearrange("p o t -> p (o t)")
                        CP.after(dve, n, "z")
                        dve.scalar_tensor_tensor(xi, bank(0, 2), param("L0_conv_out_b"), xi,
                                                 ALU.add, ALU.add).then_inc(c_dve, 1)
                        CP.after(dve, n, "mean")
                        CG.after(dve, n - 2, "xn")
                        dve.tensor_tensor(xc[par], xi, bank(2, 2), ALU.subtract).then_inc(c_dve, 1)
                    if back:
                        for k in range(2):
                            RA.after(dve, m, f"sd{k}")
                            dve.reciprocal(ss[k], ss[k]).then_inc(r_dve, 1)
                        RA.after(dve, m - 1, "hi4")
                        RD.after(dve, m - 1, "rest4")
                        for k in range(4):
                            RD.after(dve, m, ("rq", "rk")[k // 2])
                            w = cv(c_wq + k) if k < 2 else qkw[:, k:k + 1]
                            dve.scalar_tensor_tensor(nrm[k], bank(4 + k), w, ss[k // 2], ALU.mult, ALU.mult)\
                                .then_inc(r_dve, 1)
                    if front:
                        CA.after(dve, n, "sd")
                        dve.reciprocal(sq[par], sq[par]).then_inc(c_dve, 1)
                    if back:
                        def rest(k):
                            RA.after(dve, m, f"hi{k}")
                            RG.after(dve, m - 1, f"lo{k}")
                            dve.tensor_tensor(rst[k], nrm[k], planes[par][:, hi_plane(k), :], ALU.subtract)\
                                .then_inc(r_dve, 1)
                        for k in range(4):
                            rest(k)
                        RG.after(dve, m, "own")
                        dve.scalar_tensor_tensor(guard, tmp[2], GUARD, tmp[0], ALU.add, ALU.min).then_inc(r_dve, 1)
                        rest(4)
            turns_c(dve, dve_c)

            def copy_out(i, par, hh):
                g = i * 2 + par
                if hh == 0:
                    wait(dve, d_stored[par], i * (HG * INC))
                    dve.wait_ge(d_pv, g * NC + (CHUNK_A + 1))
                else:
                    dve.wait_ge(d_pv, g * NC + NC)
                dve.tensor_copy(half(Oe[par], hh), bank(6 + hh)).then_inc(d_ev, 1)

            def dve_d(i):
                for par in range(2):
                    for c in range(NC):
                        if MASKS[c]:
                            dve.wait_ge(d_exp, i * (2 * NC) + (par * NC + c + 1))
                            pr = PR1[(par * NC + c) % PRING]
                            for s, (j, t) in enumerate(CHUNKS[c]):
                                if j == t:
                                    v = pr.rearrange("p (h c) -> p h c", h=UPC)[:, :, s * P:(s + 1) * P]
                                    m3 = causal[:, :].rearrange("p (o t) -> p o t", o=1).to_broadcast([P, UPC, P])
                                    dve.tensor_tensor(v, v, m3, ALU.min).then_inc(d_mask, 1)
                                    v = pr[:, s * HALF + UPC * P:(s + 1) * HALF]
                                    dve.tensor_tensor(v, v, causal[:, :], ALU.min).then_inc(d_mask, 1)
                        if c == 0:
                            if par == 1:
                                copy_out(i, 0, 1)
                            elif not (isinstance(i, int) and i == 0):
                                copy_out(i - 1, 1, 1)
                        if c == CHUNK_A + 2:
                            copy_out(i, par, 0)
            dve.wait_ge(d_init, 4)
            peeled(dve, NG // 2, dve_d)
            copy_out(NG // 2 - 1, 1, 1)

            def dve_e(i):
                dve.wait_ge(e_loaded, i * (5 * INC) + 5 * INC)
                EP.after(dve, i - 1, "den1")
                dve.reciprocal(rden, den).then_inc(e_dve, 1)
                for par in range(2):
                    EP.after(dve, i, f"den{par}")
                    dve.tensor_tensor(num[par], num[par], bank(4 + 2 * par, 2), ALU.mult).then_inc(e_dve, 1)
                for par in range(2):
                    xi = X[:, ds(i * 2 + par, 1), :].rearrange("p o t -> p (o t)")
                    EP.after(dve, i, f"z{par}")
                    dve.tensor_tensor(xi, xi, bank(2 * par, 2), ALU.add).then_inc(e_dve, 1)
                for par in range(2):
                    xi = X[:, ds(i * 2 + par, 1), :].rearrange("p o t -> p (o t)")
                    EP.after(dve, i, f"mean{par}")
                    EG.after(dve, i - 1, f"xn{par}")
                    dve.tensor_tensor(exc[par], xi, bank(4 + 2 * par, 2), ALU.subtract).then_inc(e_dve, 1)
                for par in range(2):
                    EA.after(dve, i, f"sd{par}")
                    dve.reciprocal(esq[par], esq[par]).then_inc(e_dve, 1)
                for par in range(2):
                    EG.after(dve, i, f"xn{par}")
                    if par:
                        ED.after(dve, i, "sum0")
                    else:
                        ED.after(dve, i - 1, "sum1")
                    dve.tensor_tensor(xsum, xsum, Yall[:, ds(i * 2 + par, 1), :].rearrange("p o t -> p (o t)"),
                                      ALU.add).then_inc(e_dve, 1)
            dve.wait_ge(e_set, 2)
            peeled(dve, B // 2, dve_e)

            def per_token(ap):
                return ap.rearrange("p (t o) -> p t o", o=1).to_broadcast([P, NT, NE])
            dve.wait_ge(f_mm, 1)
            dve.scalar_tensor_tensor(lg, bank(0)[:, 0:NT * NE].rearrange("p (t e) -> p t e", e=NE), 1.0 / B,
                                     br_b[:, :].rearrange("p (o e) -> p o e", o=1).to_broadcast([P, NT, NE]),
                                     ALU.mult, ALU.add).then_inc(f_dve, 1)
            dve.wait_ge(f_dve, 1)
            dve.reduce_max(lm, lg, AX_X).then_inc(f_dve, 1)
            dve.wait_ge(f_dve, 2)
            dve.tensor_tensor(lg, lg, per_token(lm), ALU.subtract).then_inc(f_dve, 1)
            dve.wait_ge(f_exp, 1)
            dve.reduce_sum(lm, lw, AX_X).then_inc(f_dve, 1)
            dve.wait_ge(f_dve, 4)
            dve.reciprocal(lm, lm).then_inc(f_dve, 1)
            dve.wait_ge(f_dve, 5)
            dve.tensor_tensor(lw, lw, per_token(lm), ALU.mult).then_inc(f_dve, 1)
            dve.wait_ge(f_mm, 2)
            dve.tensor_copy(wT[0:NE, :], bank(2, 2)[0:NE, :]).then_inc(f_dve, 1)
            for e in range(1, NE, 2):
                dve.wait_ge(f_wbps, e + 1)
                dve.tensor_copy(wB[:, e, :], bank(6, 2)).then_inc(f_wbV, 1)

            def dve_f(i):
                def result(th):
                    dve.wait_ge(g_y, i * 2 + (th + 1))
                    wait(dve, out_stored[th], i * INC)
                    dve.tensor_tensor(res[th], bank(4 + th),
                                      X[:, ds(i, 1), th * HALF:(th + 1) * HALF].rearrange("p o t -> p (o t)"),
                                      ALU.add).then_inc(g_res, 1)
                for k in range(2 * NE):
                    n, th, e = i * (2 * NE) + k, k // NE, k % NE
                    dve.wait_ge(g_r2, n + 1)
                    wait(dve, g_y3, n - 1)
                    dve.tensor_tensor(h2w[k % 2], h2[k % 2], half(wB[:, e, :], th), ALU.mult).then_inc(g_w, 1)
                    if k == NE + 2:
                        result(0)
                result(1)
            dve.wait_ge(f_wbA, NE // 2)
            dve.wait_ge(f_wbV, NE // 2)
            peeled(dve, B, dve_f)


_INS = ["x"] + VECTORS[:5] + ["L0_conv_pw_w", "L0_conv_out_w", "L0_conv_out_b", "L1_attn_w_qkv", "L1_attn_w_proj",
        "L1_attn_qn_w", "L1_attn_kn_w", "L1_ffn_Wr", "L1_ffn_br", "L1_ffn_W1", "L1_ffn_W2", "L1_ffn_Wo",
        "L1_ffn_bo"] + PARAMS


def kernel(**inputs):
    import numpy as _np
    import concourse.bacc as _bacc
    from concourse import mybir as _mybir
    from concourse.bass_utils import run_bass_kernel_spmd as _run

    nc = _bacc.Bacc("TRN2", target_bir_lowering=False, num_devices=1)
    arrays, aps = {}, {}
    for name in _INS:
        a = _np.ascontiguousarray(inputs[name])
        arrays[f"in_{name}"] = a
        aps[name] = nc.dram_tensor(f"in_{name}", a.shape, _mybir.dt.from_np(a.dtype), kind="ExternalInput").ap()
    out = nc.dram_tensor("out_0", (B, P, H, W), _mybir.dt.float32, kind="ExternalOutput").ap()
    hybrid_kernel(nc, aps, out)
    r = _run(nc, [arrays], core_ids=[0])
    return r.results[0]["out_0"]
```

```python
from contextlib import ExitStack

import concourse.bass as bass
from concourse import mybir

F32 = mybir.dt.float32
BF16 = mybir.dt.bfloat16
ACT = mybir.ActivationFunctionType
ALU = mybir.AluOpType
AX_X = mybir.AxisListType.X
ds = bass.ds

P = 128
B = 8
H = W = 32
T = H * W
HALF = T // 2
NT = T // P
NH0 = 4
D0 = P // NH0
NH1 = P // 2
NHB = B * NH1
NE = 8
HG = 4
NG = NHB // HG
BN_EPS0 = 1e-5
LN_EPS = 1e-5
RMS_EPS = 1e-6
BN_EPS = 1e-3
SCALE0 = D0 ** -0.5
SCALE1 = 2 ** -0.5
GUARD = 60.0
BIG = 3.0e38

INC = 16

QS = 256
STEPS = T // QS
SUB = 8
TURN = 2 * STEPS * SUB
GK = W
RB = P // GK
L_MOVE = NH0
L_EXP = 9
L_SUM = 10
L_NORM = 23
L_PV = 24
L_OUT = L_PV + SUB
TAIL = L_OUT

STACK = 12
QROWS, KROWS = STACK + 3, STACK

UNITS = [(j, t) for j in range(NT) for t in range(j, NT)]
UPC = 3
CHUNKS = [UNITS[i:i + UPC] for i in range(0, len(UNITS), UPC)]
NC = len(CHUNKS)
CW = UPC * HG * P
PRING = 6
VW = 44


def runs(chunk, split_half):
    out = []
    for i, (j, t) in enumerate(chunk):
        if out and out[-1][1] == j and out[-1][2] + out[-1][3] == t and not (
                split_half and t == NT // 2):
            out[-1][3] += 1
        else:
            out.append([i, j, t, 1])
    return out


CHUNK_A = max(c for c, ch in enumerate(CHUNKS) if any(t < NT // 2 for _, t in ch))

PARAMS = ["L1_ffn_b1", "L1_ffn_g1", "L1_ffn_be1", "L1_ffn_m1", "L1_ffn_v1",
          "L1_ffn_b2", "L1_ffn_g2", "L1_ffn_be2", "L1_ffn_m2", "L1_ffn_v2"]
VECTORS = ["L0_conv_bn_gamma", "L0_conv_bn_beta", "L0_conv_bn_mean", "L0_conv_bn_var",
           "L0_conv_dw_w", "L0_conv_out_b"]
NPR = NE * len(PARAMS) + len(VECTORS)


def hybrid_kernel(nc, a, out):
    x_v = a["x"].rearrange("b c h w -> c b (h w)")
    out_v = out.rearrange("b c h w -> c b (h w)")

    parts0 = nc.dram_tensor("parts0", (B, 6, P, T), BF16, kind="Internal").ap()
    values0 = nc.dram_tensor("values0", (B, P, T), F32, kind="Internal").ap()
    qstack = nc.dram_tensor("qstack", (QROWS, NHB, T), BF16, kind="Internal").ap()
    kstack = nc.dram_tensor("kstack", (KROWS, NHB, T), BF16, kind="Internal").ap()
    attn1 = nc.dram_tensor("attn1", (NHB, 3, T), F32, kind="Internal").ap()

    with ExitStack() as ctx:
        def sb(name, shape, dt=F32):
            return ctx.enter_context(nc.sbuf_tensor(name, shape, dt))

        def sem(name):
            return ctx.enter_context(nc.semaphore(name))

        X = sb("X", [P, B, T])
        WT = sb("WT", [P, 8 * P])
        ident = sb("ident", [P, P])
        mean_w = sb("mean_w", [P, P])
        causal = sb("causal", [P, P])
        PT = sb("PT", [P, NPR])
        CV = sb("CV", [P, 64])
        qkw = sb("qkw", [P, 4])
        br_b = sb("br_b", [P, NE])
        Wr = sb("Wr", [P, NE])
        bo = sb("bo", [NE, P])
        eps_c = sb("eps_c", [P, 5])
        sel = sb("sel", [P, NE, P])
        Yall = sb("Yall", [P, B, T])
        arena_bytes = 133 * 1024
        arena = sb("arena", [P, arena_bytes // 4])

        class Cut:
            def __init__(self, at=0):
                self.at = at

            def __call__(self, shape, dt=F32):
                n = 1
                for s in shape:
                    n *= s
                size = 2 if dt == BF16 else 4
                words = (n * size + 3) // 4
                start = self.at // 4
                self.at += words * 4
                assert self.at <= arena_bytes, self.at
                ap = arena[:, start:start + words]
                if dt != F32:
                    ap = ap.bitcast(dt)
                names = [f"d{i}" for i in range(len(shape))]
                if len(shape) > 1:
                    ap = ap.rearrange("p (" + " ".join(names) + ") -> p " + " ".join(names),
                                      **dict(zip(names[1:], shape[1:])))
                return ap

        cut = Cut()
        WR = cut([8, P])
        PRr = cut([P])
        cut = Cut(8 * 1024)
        xbn = [cut([T]) for _ in range(2)]
        parts = [cut([6, T], BF16) for _ in range(2)]
        rest0 = [cut([T]) for _ in range(2)]
        v_out = [cut([T]) for _ in range(2)]
        cut = Cut()
        E0 = [cut([NT, NH0, QS]) for _ in range(2)]
        K1, K2 = [[cut([NH0, T], BF16) for _ in range(2)] for _ in range(2)]
        Q1, Q2 = [[cut([NH0, HALF], BF16) for _ in range(2)] for _ in range(2)]
        V0 = [cut([T]) for _ in range(2)]
        RS = [cut([NH0, QS], BF16) for _ in range(2)]
        sums = cut([QS])
        rec = cut([QS])
        rec_rest = cut([QS])
        rec_parts = cut([3, QS], BF16)
        maxima = cut([2 * NH0, GK], BF16)
        spread = cut([NT, P], BF16)
        window = cut([2 * GK - RB])
        identb = cut([P], BF16)
        cut = Cut()
        V1 = cut([NT, NHB * 3])
        in_c = cut.at
        xc = [cut([T]) for _ in range(2)]
        sq = cut([T])
        dev = cut([NT])
        dev_t = cut([P])
        xn = [cut([T]) for _ in range(2)]
        xn_high = cut([HALF])
        ss = [cut([HALF]) for _ in range(2)]
        nrm = [cut([HALF]) for _ in range(5)]
        rst = [cut([HALF]) for _ in range(5)]
        tmp = [cut([HALF]) for _ in range(4)]
        sqa = tmp[2:4]
        planes = [cut([15, HALF], BF16) for _ in range(2)]
        cut = Cut(in_c)
        Qs = [Yall[:, 2 + 2 * k:4 + 2 * k, :].rearrange("p b t -> p (b t)").bitcast(BF16)
              .rearrange("p (h t) -> p h t", h=HG) for k in range(2)]
        Ks = [Yall[:, 6:8, :].rearrange("p b t -> p (b t)").bitcast(BF16).rearrange("p (h t) -> p h t", h=HG),
              cut([HG, T], BF16)]
        Vg = [cut([NT, VW]) for _ in range(2)]
        PR1 = [cut([CW]) for _ in range(PRING)]
        Oe = [Yall[:, 0, :], Yall[:, 1, :]]
        num = [[cut([T]) for _ in range(2)] for _ in range(2)]
        den = [cut([T]) for _ in range(2)]
        expand = cut([2, P])
        W1, W2, Wo = [cut([NE, P]) for _ in range(3)]
        cut = Cut()
        exc = [cut([T]) for _ in range(2)]
        esq = cut([T])
        edev = cut([NT])
        edev_t = cut([P])
        rden = [cut([T]) for _ in range(2)]
        xsum = cut([T])
        cut = Cut(cut.at)
        bias_w = cut([T])
        wB = cut([NE, T])
        wT = cut([T])
        lg = cut([NT, NE])
        lw = cut([NT, NE])
        lm = cut([NT])
        h1 = [cut([HALF]) for _ in range(2)]
        h2 = [cut([HALF]) for _ in range(2)]
        h2w = [cut([HALF]) for _ in range(2)]
        res = [cut([HALF]) for _ in range(2)]

        ps = ctx.enter_context(nc.psum_tensor("ps", [P, 8 * HALF], F32))

        def bank(k, n=1):
            return ps[:, k * HALF:(k + n) * HALF]

        c_scale0, c_bias0, c_wq, c_ck, c_t = 0, 1, 2, 4, 6
        c_A1, c_B1, c_A2, c_B2, c_sd = 8, 16, 24, 32, 40

        def cv(c, n=1):
            return CV[:, c:c + n]

        def param(name):
            if name in PARAMS:
                k = NE * PARAMS.index(name)
                return PT[:, k:k + NE]
            k = NE * len(PARAMS) + VECTORS.index(name)
            return PT[:, k:k + 1]

        def wt(what):
            k, n = {"q0": (0, P), "k0": (P, P), "v0": (2 * P, P), "out": (3 * P, P),
                    "qk1": (4 * P, 2 * P), "v1": (6 * P, P), "proj": (7 * P, P)}[what]
            return WT[:, k:k + n]

        w_loaded, ffn_w_loaded = sem("w_loaded"), sem("ffn_w_loaded")
        x_loaded_first, x_loaded_rest = sem("x_loaded_first"), sem("x_loaded_rest")
        ident_set, eps_set = sem("ident_set"), sem("eps_set")
        w_turned, w_copied = sem("w_turned"), sem("w_copied")
        param_step, param_sd = sem("param_step"), sem("param_sd")
        a_bn, a_mm, a_hi, a_rest, a_lo = [sem(n) for n in ("a_bn", "a_mm", "a_hi", "a_rest", "a_lo")]
        a_stored = [sem("a_stored_even"), sem("a_stored_odd")]
        k_loaded = [sem("k_loaded_even"), sem("k_loaded_odd")]
        v_loaded = [sem("v_loaded_even"), sem("v_loaded_odd")]
        q_loaded = [sem("q_loaded_low"), sem("q_loaded_high")]
        b_const = sem("b_constants")
        b_raw, b_max, b_moved, b_guard = [sem(n) for n in ("b_raw_scores", "b_max", "b_max_turned", "b_guard")]
        b_qk, b_exp, b_sum, b_summed = [sem(n) for n in ("b_scores", "b_exp", "b_sum", "b_sum_copied")]
        b_rec, b_rhi, b_rrest, b_rmid, b_rlo = [sem(n) for n in (
            "b_rec", "b_rec_hi", "b_rec_rest", "b_rec_mid", "b_rec_lo")]
        rs_loaded = [sem("rs_loaded_even"), sem("rs_loaded_odd")]
        b_spread, b_norm, b_pv, b_out = [sem(n) for n in ("b_spread", "b_norm", "b_pv", "b_out")]
        c_pe, c_dve, c_act = [sem(n) for n in ("c_pe", "c_dve", "c_act")]
        c_pe_next, c_dve_next = sem("c_pe_next"), sem("c_dve_next")
        r_pe, r_dve, r_act, r_pool = [sem(n) for n in ("r_pe", "r_dve", "r_act", "r_pool")]
        c_stored = [sem("c_stored_low"), sem("c_stored_high")]
        ones_set, c_kept = sem("ones_set"), sem("c_kept")
        e_pe, e_dve, e_act = [sem(n) for n in ("e_pe", "e_dve", "e_act")]
        e_pe_next, e_dve_next, e_den = sem("e_pe_next"), sem("e_dve_next"), sem("e_den")
        e_sum = sem("e_sum")
        e_loaded, e_set = [sem("e_loaded_even"), sem("e_loaded_odd")], sem("e_set")
        d_init, d_init_k = sem("d_first_slot_set"), sem("d_more_slots_set")
        d_vinit = sem("d_value_slots_set")
        d_loaded = [sem("d_loaded_even"), sem("d_loaded_odd")]
        d_qk, d_exp, d_mask, d_pv = [sem(n) for n in ("d_scores", "d_exp", "d_mask", "d_pv")]
        d_v, d_ev = sem("d_values"), sem("d_copied_out")
        d_stored = [sem("d_stored_even"), sem("d_stored_odd")]
        f_mm, f_dve, f_exp, f_set = [sem(n) for n in ("f_mm", "f_dve", "f_exp", "f_set")]
        f_wbps, f_wbA, f_wbV = sem("f_wb_product"), sem("f_wb_copied_act"), sem("f_wb_copied_dve")
        f_biased = sem("f_biased")
        g_h1, g_r1, g_h2, g_r2 = [sem(n) for n in ("g_h1", "g_relu1", "g_h2", "g_relu2")]
        g_w, g_y3, g_res = [sem(n) for n in ("g_weighted", "g_third", "g_res")]
        out_stored = [sem("out_stored_low"), sem("out_stored_high")]

        W_LOADS = 4 + len(PARAMS) + len(VECTORS) + 3
        FFN_LOADS = 5
        K_LOADS, Q_LOADS = 6, 6
        RS_LOADS = 3 * NH0
        NSTEP = B * STEPS
        B_CONSTANTS = 5 + 3 + RB + 2
        C_STORES = 13
        MASKS = [2 * sum(j == t for j, t in ch) for ch in CHUNKS]

        def wait(eng, s, v):
            if isinstance(v, int) and v <= 0:
                return
            eng.wait_ge(s, v)

        def peeled(eng, n, body):
            body(0)
            with eng.Fori(1, n) as i:
                body(i)

        def turns(eng, body):
            body(0, range(TURN))
            with eng.Fori(1, B // 2) as i:
                body(i, range(TURN))
            body(B // 2, range(TAIL + 1))

        def in_range(i, k, lag):
            if not isinstance(i, int):
                return True
            return 0 <= i * TURN + k - lag < B // 2 * TURN

        def wait_moved(eng, i, st):
            if isinstance(i, int) and i * 2 * STEPS + st < 0:
                return
            eng.wait_ge(rs_loaded[st % 2], i * (STEPS * RS_LOADS * INC) + (st // 2 + 1) * (RS_LOADS * INC))

        class Steps:
            def __init__(self, s, names):
                self.s, self.names = s, names

            def after(self, eng, i, name):
                wait(eng, self.s, i * len(self.names) + self.names.index(name) + 1)

        def turn_parts(i):
            return i < B // 2, i > 0

        def turns_c(eng, body):
            for i in range(B // 2 + 1):
                body(i)

        two = (0, 1)
        five = range(5)
        CN = Steps(c_pe_next, ["z", "mean"])
        CX = Steps(c_dve_next, ["x"])
        CP = Steps(c_pe, ["var", "turn", "wide", "val"])
        CD = Steps(c_dve, ["xc", "rec", "xn"])
        CA = Steps(c_act, ["sq", "sd", "turned", "cv"])
        RP = Steps(r_pe, ["q", "k"])
        RD = Steps(r_dve, ["rq", "rk", "n0", "n1", "n2", "n3", "rest0", "rest1", "rest2", "rest3", "guard", "rest4"])
        RA = Steps(r_act, [f"s{k}" for k in range(4)] + ["sd0", "sd1", "abs0", "abs1"]
                   + [f"{n}{k}" for n in ("hi", "mid") for k in range(4)] + ["hi4", "mid4"])
        RG = Steps(r_pool, ["ss0", "ss1", "p0", "p1", "bound", "own"] + [f"lo{k}" for k in five])
        EN = Steps(e_pe_next, ["den", "z", "mean"])
        EX = Steps(e_dve_next, ["y", "x"])
        EP = Steps(e_pe, ["var", "turn", "wide"])
        ED = Steps(e_dve, ["xc", "rec", "xn"])
        ES = Steps(e_sum, ["sum"])
        EA = Steps(e_act, ["sq", "sd", "turned"])

        def hi_plane(k):
            return 3 * k

        def half(ap, th):
            return ap[:, th * HALF:(th + 1) * HALF]

        def flat(ap):
            return ap.rearrange("p n t -> p (n t)")

        block = ctx.enter_context(nc.Block())

        @block.sync
        def _(sp):
            sp.dma_start(X[:, 0:2, :], x_v[:, 0:2, :]).then_inc(x_loaded_first, INC)
            sp.dma_start(WR[:, 0:3, :], a["L0_conv_pw_w"].rearrange("(k p) c -> p k c", p=P)).then_inc(w_loaded, INC)
            sp.dma_start(WR[:, 3, :], a["L0_conv_out_w"]).then_inc(w_loaded, INC)
            sp.dma_start(WR[:, 4:7, :], a["L1_attn_w_qkv"].rearrange("(k p) c -> p k c", p=P)).then_inc(w_loaded, INC)
            sp.dma_start(WR[:, 7, :], a["L1_attn_w_proj"]).then_inc(w_loaded, INC)
            for k, name in enumerate(PARAMS):
                sp.dma_start(PRr[NE * k:NE * (k + 1), :], a[name]).then_inc(w_loaded, INC)
            for k, name in enumerate(VECTORS):
                r = NE * len(PARAMS) + k
                sp.dma_start(PRr[r:r + 1, :], a[name].rearrange("(o c) -> o c", o=1)).then_inc(w_loaded, INC)
            for k, name in enumerate(["L1_attn_qn_w", "L1_attn_kn_w"]):
                sp.dma_start(qkw[:, 2 * k:2 * k + 2],
                             a[name].rearrange("(o c) -> o c", o=1).to_broadcast([P, 2])).then_inc(w_loaded, INC)
            sp.dma_start(br_b[:, :],
                         a["L1_ffn_br"].rearrange("(o c) -> o c", o=1).to_broadcast([P, NE])).then_inc(w_loaded, INC)
            sp.dma_start(X[:, 2:B, :], x_v[:, 2:B, :]).then_inc(x_loaded_rest, INC)
            sp.dma_start(Wr[:, :], a["L1_ffn_Wr"]).then_inc(ffn_w_loaded, INC)
            sp.dma_start(bo[:, :], a["L1_ffn_bo"]).then_inc(ffn_w_loaded, INC)

            def store_parts(i):
                for par in range(2):
                    b = i * 2 + par
                    sp.wait_ge(a_lo, b * 2 + 2)
                    sp.dma_start(parts0[ds(b, 1)].rearrange("o k p t -> p (o k) t"), parts[par])\
                        .then_inc(a_stored[par], INC)
                    sp.dma_start(values0[ds(b, 1)].rearrange("o p t -> p (o t)"), v_out[par])\
                        .then_inc(a_stored[par], INC)

            with sp.Fori(0, B // 2 - 1) as i:
                store_parts(i)

            def load_k(b, par):
                for tile, kinds in ((K1, (3, 4, 3)), (K2, (5, 3, 4))):
                    for r, kind in enumerate(kinds):
                        src = parts0[ds(b, 1), kind].rearrange("o (n i) t -> i (o n) t", n=NH0)
                        sp.dma_start(tile[par][D0 * r:D0 * (r + 1), :, :], src).then_inc(k_loaded[par], INC)

            def load_q(b, th):
                for tile, kinds in ((Q1, (0, 0, 1)), (Q2, (0, 2, 1))):
                    for r, kind in reversed(list(enumerate(kinds))):
                        src = parts0[ds(b, 1), kind, :, th * HALF:(th + 1) * HALF]\
                            .rearrange("o (n i) t -> i (o n) t", n=NH0)
                        sp.dma_start(tile[th][D0 * r:D0 * (r + 1), :, :], src).then_inc(q_loaded[th], INC)

            def load_v(b, par):
                sp.dma_start(V0[par], values0[ds(b, 1)].rearrange("o p t -> p (o t)")).then_inc(v_loaded[par], INC)

            def feed(i, last=False):
                for st in range(2 * STEPS):
                    g = i * (2 * STEPS) + st
                    for r, part_made in enumerate((b_rhi, b_rmid, b_rlo)):
                        sp.wait_ge(part_made, g + 1)
                        for n in range(NH0):
                            sp.dma_start(RS[st % 2][GK * r:GK * (r + 1), n, :], rec_parts[GK * n:GK * (n + 1), r, :])\
                                .then_inc(rs_loaded[st % 2], INC)
                    par, q = st // STEPS, st % STEPS
                    b, sub = i * 2 + par, i * TURN + par * (TURN // 2)
                    if not (last and par == 1) and q in (1, 2):
                        sp.wait_ge(b_qk, sub * 2 + 2 * SUB * (STEPS // 2) * q)
                        load_q(b + 1, q - 1)
                    if not last and q == 3:
                        sp.wait_ge(b_qk, sub * 2 + TURN)
                        load_k(b + 2, par)
                    first_image = isinstance(i, int) and i == 0 and par == 0
                    if q == 0 and not first_image and not (last and par == 1):
                        sp.wait_ge(b_pv, sub)
                        load_v(b + 1, 1 - par)

            sp.wait_ge(a_stored[0], 2 * INC)
            load_k(0, 0)
            for th in range(2):
                load_q(0, th)
            load_v(0, 0)
            store_parts(B // 2 - 1)
            for par in range(2):
                sp.wait_ge(a_stored[par], B * INC)
            load_k(1, 1)
            load_v(1, 1)
            feed(0)
            with sp.Fori(1, B // 2 - 1) as i:
                feed(i)
            feed(B // 2 - 1, last=True)

            def store_stacks(i, th):
                RG.after(sp, i * 2 + th, "lo4")
                pl = planes[th]

                def rows(dram, r, k):
                    return dram[r:r + k, ds(i * P, P), th * HALF:(th + 1) * HALF].rearrange("r h t -> h r t")
                for d in range(2):
                    q, k, r = hi_plane(d), hi_plane(2 + d), 6 * d
                    sp.dma_start(rows(qstack, r, 3), pl[:, q:q + 1, :].to_broadcast([P, 3, HALF]))\
                        .then_inc(c_stored[th], INC)
                    sp.dma_start(rows(qstack, r + 3, 2), pl[:, q + 1:q + 2, :].to_broadcast([P, 2, HALF]))\
                        .then_inc(c_stored[th], INC)
                    sp.dma_start(rows(qstack, r + 5, 1), pl[:, q + 2:q + 3, :]).then_inc(c_stored[th], INC)
                    sp.dma_start(rows(kstack, r, 3), pl[:, k:k + 3, :]).then_inc(c_stored[th], INC)
                    sp.dma_start(rows(kstack, r + 3, 2), pl[:, k:k + 2, :]).then_inc(c_stored[th], INC)
                    sp.dma_start(rows(kstack, r + 5, 1), pl[:, k:k + 1, :]).then_inc(c_stored[th], INC)
                g = hi_plane(4)
                sp.dma_start(rows(qstack, STACK, 3), pl[:, g:g + 3, :]).then_inc(c_stored[th], INC)

            with sp.Fori(0, B // 2 - 1) as i:
                for th in range(2):
                    store_stacks(i, th)
            store_stacks(B // 2 - 1, 0)

            def load_group(g, par):
                sp.dma_start(Qs[par][0:QROWS, :, :], qstack[:, ds(g * HG, HG), :]).then_inc(d_loaded[par], INC)
                sp.dma_start(Ks[par][0:KROWS, :, :], kstack[:, ds(g * HG, HG), :]).then_inc(d_loaded[par], INC)

            def store_group(g, par):
                sp.wait_ge(d_ev, g * 2 + 2)
                for j in range(HG):
                    sp.dma_start(attn1[ds(g * HG + j, 1)].rearrange("o r t -> (o r) t"),
                                 Oe[par][32 * j:32 * j + 3, :]).then_inc(d_stored[par], INC)

            for th in range(2):
                sp.wait_ge(c_stored[th], (B // 2 - 1) * C_STORES * INC)
            sp.wait_ge(d_init, 1)
            sp.wait_ge(d_init_k, 1)
            load_group(0, 0)
            store_stacks(B // 2 - 1, 1)
            sp.wait_ge(d_init_k, 3)
            load_group(1, 1)
            for th in range(2):
                sp.wait_ge(c_stored[th], B // 2 * C_STORES * INC)
            with sp.Fori(0, NG // 2 - 1) as i:
                for par in range(2):
                    g = i * 2 + par
                    sp.wait_ge(d_qk, g * NC + NC)
                    load_group(g + 2, par)
                    store_group(g, par)


            def load_pair(i, slot):
                if i > 1:
                    EN.after(sp, 2 * i - 3, "z")
                for par in range(2):
                    for d in range(2):
                        sp.dma_start(num[slot][par][d:P:2, :], attn1[ds((i * 2 + par) * NH1, NH1), d, :])\
                            .then_inc(e_loaded[slot], INC)
                sp.dma_start(den[slot], attn1[ds(i * P, P), 2, :]).then_inc(e_loaded[slot], INC)
            for par in range(2):
                sp.wait_ge(d_stored[par], NG // 4 * HG * INC)
            RG.after(sp, B - 1, "lo4")
            for i in range(2):
                load_pair(i, i)
            for w, name in ((W1, "L1_ffn_W1"), (W2, "L1_ffn_W2"), (Wo, "L1_ffn_Wo")):
                sp.dma_start(w, a[name].rearrange("e d h -> d e h")).then_inc(ffn_w_loaded, INC)
            for par in range(2):
                store_group(NG - 2 + par, par)
            for par in range(2):
                sp.wait_ge(d_stored[par], NG // 2 * HG * INC)
            for i in range(2, B // 2):
                load_pair(i, i % 2)

            with sp.Fori(0, B) as i:
                for th in range(2):
                    sp.wait_ge(g_res, i * 2 + th + 1)
                    sp.dma_start(out_v[:, ds(i, 1), th * HALF:(th + 1) * HALF].rearrange("p o t -> p (o t)"),
                                 res[th]).then_inc(out_stored[th], INC)
            for th in range(2):
                sp.wait_ge(out_stored[th], B * INC)

        @block.gpsimd
        def _(pool):
            pool.memset(ident[:, :], 0.0).then_inc(ident_set, 1)
            pool.memset(causal[:, :], BIG).then_inc(ident_set, 1)
            pool.memset(mean_w[:, :], 1.0 / P).then_inc(eps_set, 1)
            pool.memset(eps_c[:, 0:1], LN_EPS).then_inc(eps_set, 1)
            pool.memset(eps_c[:, 1:2], RMS_EPS).then_inc(eps_set, 1)
            pool.memset(eps_c[:, 2:3], 0.0).then_inc(eps_set, 1)
            pool.wait_ge(ident_set, 2)
            pool.affine_select(out=ident[:, :], in_=ident[:, :], compare_op=ALU.not_equal, fill=1.0, base=0,
                               pattern=[[-1, P]], channel_multiplier=1).then_inc(ident_set, 1)
            pool.affine_select(out=causal[:, :], in_=causal[:, :], compare_op=ALU.is_ge, fill=0.0, base=0,
                               pattern=[[1, P]], channel_multiplier=-1).then_inc(ident_set, 1)

            pool.memset(sel[0:NE, :, :], 0.0).then_inc(f_set, 1)
            pool.wait_ge(f_set, 1)
            pool.affine_select(out=sel[0:NE, :, :], in_=sel[0:NE, :, :], compare_op=ALU.not_equal, fill=1.0,
                               base=0, pattern=[[-1, NE], [0, P]], channel_multiplier=1).then_inc(f_set, 1)
            pool.wait_ge(f_set, 2)

            pool.wait_ge(ident_set, 4)
            made = [0]

            def constant(ins):
                made[0] += 1
                ins.then_inc(b_const, 1)
                pool.wait_ge(b_const, made[0])
            constant(pool.tensor_copy(identb, ident[:, :]))
            constant(pool.memset(spread[0:3 * GK], 0.0))
            constant(pool.memset(window, 0.0))
            for par in range(2):
                constant(pool.memset(K2[par][3 * GK:P], 0.0))
            for r in range(3):
                v = flat(spread[GK * r:GK * (r + 1)]).rearrange("p (y x) -> p y x", x=GK)
                constant(pool.affine_select(out=v, in_=v, compare_op=ALU.not_equal, fill=1.0, base=0,
                                            pattern=[[-1, H], [0, GK]], channel_multiplier=1))
            for j in range(RB):
                at = GK - RB + j
                constant(pool.memset(window[GK * j:GK * (j + 1), at:at + 1], 1.0))
            for par in range(2):
                v = K2[par][3 * GK:P].rearrange("p n (y x) -> p n y x", x=GK)
                constant(pool.affine_select(out=v, in_=v, compare_op=ALU.not_equal, fill=-1.0, base=0,
                                            pattern=[[0, NH0], [-1, H], [0, GK]], channel_multiplier=1))

            with pool.Fori(0, B // 2) as i:
                for par in range(2):
                    b = i * 2 + par
                    for k in range(2):
                        pool.wait_ge(a_hi, b * 5 + 4 + k)
                        pool.tensor_tensor(parts[par][:, 3 * k + 2, :], rest0[k], parts[par][:, 3 * k + 1, :],
                                           ALU.subtract).then_inc(a_lo, 1)

            def pool_b(i):
                for par in range(2):
                    g = i * 2 + par
                    pool.wait_ge(b_rmid, g + 1)
                    if par:
                        pool.wait_ge(rs_loaded[0], i * (RS_LOADS * INC) + RS_LOADS * INC)
                    else:
                        wait(pool, rs_loaded[1], i * (RS_LOADS * INC))
                    pool.tensor_tensor(rec_parts[:, 2, :], rec_rest, rec_parts[:, 1, :], ALU.subtract).then_inc(b_rlo, 1)
            peeled(pool, NSTEP // 2, pool_b)

            pool.wait_ge(b_out, NSTEP)
            pool.memset(V1, 1.0).then_inc(ones_set, 1)

            def pool_c(i):
                for par in range(2):
                    n, m = i * 2 + par, i * 2 + (par - 2)
                    front, back = turn_parts(i)
                    q0, q1, k0, k1, _ = nrm
                    if back:
                        for k in range(2):
                            RA.after(pool, m, f"s{2 * k + 1}")
                            pool.tensor_tensor(ss[k], ss[k], sqa[k], ALU.add).then_inc(r_pool, 1)
                        RD.after(pool, m, "n3")
                        pool.tensor_tensor(tmp[2], q0, k0, ALU.mult).then_inc(r_pool, 1)
                        pool.tensor_tensor(tmp[3], q1, k1, ALU.mult).then_inc(r_pool, 1)
                        RA.after(pool, m, "abs1")
                        pool.tensor_tensor(tmp[0], tmp[0], tmp[1], ALU.add).then_inc(r_pool, 1)
                        RG.after(pool, m, "p1")
                        pool.tensor_tensor(tmp[2], tmp[2], tmp[3], ALU.add).then_inc(r_pool, 1)
                    if back:
                        for k in range(5):
                            RA.after(pool, m, f"mid{k}")
                            r = hi_plane(k)
                            pool.tensor_tensor(planes[par][:, r + 2, :], rst[k], planes[par][:, r + 1, :],
                                               ALU.subtract).then_inc(r_pool, 1)
                    if n == B - 1:
                        CN.after(pool, B - 1, "z")
                        pool.memset(Qs[0], 0.0).then_inc(d_init, 1)
            turns_c(pool, pool_c)

            for th in range(2):
                pool.wait_ge(c_stored[th], B // 2 * C_STORES * INC)
            pool.memset(expand, 0.0).then_inc(e_set, 1)
            pool.wait_ge(e_set, 1)
            for par in range(2):
                e_v = expand[:, par, :].rearrange("p (h d) -> p h d", d=2)
                pool.affine_select(out=e_v, in_=e_v, compare_op=ALU.not_equal, fill=1.0, base=-NH1 * par,
                                   pattern=[[-1, NH1], [0, 2]], channel_multiplier=1).then_inc(e_set, 1)

            pool.wait_ge(d_vinit, 2)
            CA.after(pool, B - 1, "cv")

            def group_values(g, par):
                pool.tensor_copy(Vg[par][:, :, 0:3 * HG], V1[:, :, ds(g * (3 * HG), 3 * HG)]).then_inc(d_v, 1)

            def pool_d(i):
                for par in range(2):
                    g = i * 2 + par
                    wait(pool, d_pv, g * NC - NC)
                    group_values(g, par)
            peeled(pool, NG // 2, pool_d)

            pool.wait_ge(f_dve, 8)
            with pool.Fori(0, B) as i:
                xi = X[:, ds(i, 1), :].rearrange("p o t -> p (o t)")
                pool.tensor_tensor(xi, xi, bias_w, ALU.add).then_inc(f_biased, 1)

        @block.scalar
        def _(act):
            act.wait_ge(w_turned, 1)
            w = bank(0, 2)
            act.activation(WT[:, 0:3 * P].rearrange("p (s n i) -> p n s i", s=3, n=NH0),
                           w[:, 0:3 * P].rearrange("p (n s i) -> p n s i", s=3, n=NH0), ACT.Copy).then_inc(w_copied, 1)
            act.activation(wt("out"), w[:, 3 * P:4 * P], ACT.Copy).then_inc(w_copied, 1)
            act.activation(wt("qk1").rearrange("p (s d h) -> p s h d", s=2, d=2),
                           w[:, 4 * P:6 * P].rearrange("p (s h d) -> p s h d", s=2, d=2), ACT.Copy).then_inc(w_copied, 1)
            act.activation(WT[:, 6 * P:8 * P], w[:, 6 * P:8 * P], ACT.Copy).then_inc(w_copied, 1)
            act.wait_ge(param_step, 3)
            act.activation(cv(c_sd, 17), cv(c_sd, 17), ACT.Sqrt).then_inc(param_sd, 1)

            def act_a(i):
                for par in range(2):
                    b = i * 2 + par
                    wait(act, a_stored[par], i * (2 * INC))
                    for k in range(2):
                        act.wait_ge(a_mm, b * 3 + k + 1)
                        act.activation(parts[par][:, 3 * k, :], bank(2 * k, 2), ACT.Copy).then_inc(a_hi, 1)
                    act.wait_ge(a_mm, b * 3 + 3)
                    act.activation(v_out[par], bank(4, 2), ACT.Copy).then_inc(a_hi, 1)
                    for k in range(2):
                        act.wait_ge(a_rest, b * 2 + k + 1)
                        act.activation(parts[par][:, 3 * k + 1, :], rest0[k], ACT.Copy).then_inc(a_hi, 1)
            peeled(act, B // 2, act_a)

            act.wait_ge(eps_set, 4)
            act.activation(eps_c[:, 3:4], eps_c[:, 2:3], ACT.Exp)
            for par in range(2):
                act.wait_ge(a_stored[par], B * INC)

            def act_b(i, subs):
                for k in subs:
                    K = i * TURN + k
                    if k % NH0 == 0 and in_range(i, k, L_MOVE):
                        c = (k - L_MOVE) % TURN
                        q = c // SUB % STEPS
                        at = (q % 2) * QS + c // NH0 % 2 * P
                        act.wait_ge(b_moved, i * (TURN // NH0) + k // NH0)
                        act.activation(Q2[q // 2][3 * GK:P, :, at:at + P],
                                       bank(2)[3 * GK:P].rearrange("p (n q) -> p n q", n=NH0),
                                       ACT.Copy).then_inc(b_guard, 1)
                    if k % SUB == 2 and in_range(i, k, L_SUM + SUB):
                        g = i * (2 * STEPS) + (k - L_SUM - SUB) // SUB
                        act.wait_ge(b_sum, g * SUB + SUB)
                        wait(act, b_rec, g)
                        act.activation(sums, bank(7)[:, 0:QS], ACT.Copy).then_inc(b_summed, 1)
                    if k % SUB == 3 and in_range(i, k, L_SUM + SUB + 1):
                        st = (k - L_SUM - SUB - 1) // SUB
                        act.wait_ge(b_rec, i * (2 * STEPS) + st + 1)
                        wait_moved(act, i, st - 1)
                        act.activation(rec_parts[:, 0, :], rec, ACT.Copy).then_inc(b_rhi, 1)
                    if k % SUB == 4 and in_range(i, k, L_SUM + SUB + 2):
                        g = i * (2 * STEPS) + (k - L_SUM - SUB - 2) // SUB
                        act.wait_ge(b_rrest, g + 1)
                        act.activation(rec_parts[:, 1, :], rec_rest, ACT.Copy).then_inc(b_rmid, 1)
                    if in_range(i, k, L_EXP):
                        c = (k - L_EXP) % TURN
                        for hp in range(2):
                            act.wait_ge(b_qk, K * 2 + (hp + 1 - 2 * L_EXP))
                            wait(act, b_pv, K + (1 - L_EXP - 2 * SUB))
                            act.activation(E0[c // SUB % 2][:, c % SUB, 2 * hp:2 * hp + 2, :].rearrange("p n q -> p (n q)"),
                                           bank(2 + hp), ACT.Exp, scale=SCALE0).then_inc(b_exp, 1)
                    if k % SUB == L_OUT % SUB and in_range(i, k, L_OUT):
                        g0 = (k - L_OUT) // SUB
                        act.wait_ge(b_pv, i * TURN + (g0 + 1) * SUB)
                        act.activation(Yall[:, ds(i * 2 + g0 // STEPS, 1), (g0 % STEPS) * QS:(g0 % STEPS + 1) * QS]
                                       .rearrange("p o t -> p (o t)"), bank(6)[:, 0:QS], ACT.Copy).then_inc(b_out, 1)
            turns(act, act_b)

            def act_c(i):
                for par in range(2):
                    n, m = i * 2 + par, i * 2 + (par - 2)
                    front, back = turn_parts(i)
                    pl = planes[par]
                    if back:
                        RD.after(act, m - 1, "guard")
                        for k in range(4):
                            RP.after(act, m, "qk"[k // 2])
                            act.activation((ss, sqa)[k % 2][k // 2], bank(4 + k), ACT.Square).then_inc(r_act, 1)
                        for k in range(2):
                            RG.after(act, m, f"ss{k}")
                            act.activation(ss[k], ss[k], ACT.Sqrt, bias=eps_c[:, 1:2], scale=0.5).then_inc(r_act, 1)
                    if 0 < n <= B:
                        CP.after(act, n - 1, "val")
                        act.wait_ge(ones_set, 1)
                        dst = V1[:, :, (n - 1) * (3 * NH1):n * (3 * NH1)].rearrange("p s (h e) -> p s h e", e=3)
                        act.activation(dst[:, :, :, 0:2], bank(2, 2).rearrange("p (s h d) -> p s h d", s=NT, d=2),
                                       ACT.Copy).then_inc(c_act, 1)
                    if front and par == 1:
                        CD.after(act, n - 1, "xn")
                        RP.after(act, m, "k")
                        act.activation(xn_high, half(xn[0], 1), ACT.Copy).then_inc(c_kept, 1)
                    if front:
                        CD.after(act, n, "xc")
                        CP.after(act, n - 1, "var")
                        act.activation(sq, xc[par], ACT.Square).then_inc(c_act, 1)
                    if front:
                        CP.after(act, n, "var")
                        CP.after(act, n - 1, "turn")
                        act.activation(dev, bank(2)[:, 0:NT], ACT.Sqrt, bias=eps_c[:, 0:1]).then_inc(c_act, 1)
                        CP.after(act, n, "turn")
                        CP.after(act, n - 1, "wide")
                        act.activation(dev_t[0:NT, :], bank(3)[0:NT, 0:P], ACT.Copy).then_inc(c_act, 1)
                    if back:
                        for k in range(2):
                            RD.after(act, m, f"n{k}")
                            act.activation(tmp[k], nrm[k], ACT.Abs, scale=cv(c_ck + k)).then_inc(r_act, 1)
                        wait(act, c_stored[par], (i - 1) * (C_STORES * INC))
                        for k in range(4):
                            RD.after(act, m, f"n{k}")
                            act.activation(pl[:, hi_plane(k), :], nrm[k], ACT.Copy).then_inc(r_act, 1)
                        for k in range(4):
                            RD.after(act, m, f"rest{k}")
                            act.activation(pl[:, hi_plane(k) + 1, :], rst[k], ACT.Copy).then_inc(r_act, 1)
                        RD.after(act, m, "guard")
                        act.activation(pl[:, hi_plane(4), :], nrm[4], ACT.Copy).then_inc(r_act, 1)
                    if back:
                        RD.after(act, m, "rest4")
                        act.activation(pl[:, hi_plane(4) + 1, :], rst[4], ACT.Copy).then_inc(r_act, 1)
            turns_c(act, act_c)

            RG.after(act, B - 1, "lo4")
            act.activation(eps_c[:, 4:5], eps_c[:, 2:3], ACT.Exp)

            def act_d(i):
                for par in range(2):
                    for c in range(NC):
                        k = i * (2 * NC) + (par * NC + c)
                        s = (par * NC + c) % 2
                        act.wait_ge(d_qk, k + 1)
                        wait(act, d_pv, k - (PRING - 1))
                        act.activation(PR1[(par * NC + c) % PRING], bank(UPC * s, UPC), ACT.Exp).then_inc(d_exp, 1)
            peeled(act, NG // 2, act_d)

            for n in range(B):
                ED.after(act, n, "xc")
                EP.after(act, n - 1, "var")
                act.activation(esq, exc[n % 2], ACT.Square).then_inc(e_act, 1)
                EP.after(act, n, "var")
                act.activation(edev, bank(6)[:, 0:NT], ACT.Sqrt, bias=eps_c[:, 0:1]).then_inc(e_act, 1)
                EP.after(act, n, "turn")
                act.activation(edev_t[0:NT, :], bank(7)[0:NT, 0:P], ACT.Copy).then_inc(e_act, 1)

            act.wait_ge(f_dve, 3)
            act.activation(lw, lg, ACT.Exp).then_inc(f_exp, 1)
            for e in range(0, NE, 2):
                act.wait_ge(f_wbps, e + 1)
                act.activation(wB[:, e, :], bank(4, 2), ACT.Copy).then_inc(f_wbA, 1)

            def act_f(i):
                def relu2(k):
                    n, e = i * (2 * NE) + k, k % NE
                    act.wait_ge(g_h2, n + 1)
                    wait(act, g_w, n - 1)
                    act.activation(h2[k % 2], bank(2 + k % 2), ACT.Relu, bias=cv(c_B2 + e),
                                   scale=cv(c_A2 + e)).then_inc(g_r2, 1)
                for k in range(2 * NE):
                    n, e = i * (2 * NE) + k, k % NE
                    act.wait_ge(g_h1, n + 1)
                    wait(act, g_h2, n - 1)
                    act.activation(h1[k % 2], bank(k % 2), ACT.Relu, bias=cv(c_B1 + e),
                                   scale=cv(c_A1 + e)).then_inc(g_r1, 1)
                    if k:
                        relu2(k - 1)
                relu2(2 * NE - 1)
            peeled(act, B, act_f)

        @block.tensor
        def _(pe):
            pe.wait_ge(ident_set, 4)
            pe.wait_ge(w_loaded, W_LOADS * INC)
            for k in range(8):
                mm = pe.transpose(ps[:, k * P:(k + 1) * P], WR[:, k, :], ident[:, :])
            mm.then_inc(w_turned, 1)
            pe.transpose(bank(2)[:, 0:NPR], PRr[0:NPR, :], ident[0:NPR, 0:NPR]).then_inc(w_turned, 1)

            pe.wait_ge(w_copied, 4)

            def pe_a(i):
                for par in range(2):
                    b = i * 2 + par
                    pe.wait_ge(a_bn, b + 1)
                    for k, w in enumerate(("q0", "k0")):
                        wait(pe, a_rest, b * 2 + (k - 1))
                        for th in range(2):
                            mm = pe.matmul(bank(2 * k + th), wt(w), half(xbn[par], th), start=True, stop=True)
                        mm.then_inc(a_mm, 1)
                    wait(pe, a_hi, b * 5 - 2)
                    for t in range(NT):
                        mm = pe.matmul(bank(4, 2)[:, t * P:(t + 1) * P], xbn[par][:, t * P:(t + 1) * P], wt("v0"),
                                       start=True, stop=True)
                    mm.then_inc(a_mm, 1)
            peeled(pe, B // 2, pe_a)

            pe.wait_ge(a_hi, B * 5)
            pe.wait_ge(a_rest, B * 2)

            pe.wait_ge(b_const, B_CONSTANTS)

            def sums_of(i, k, K):
                if in_range(i, k, L_SUM):
                    c = (k - L_SUM) % TURN
                    kb, sl = c % SUB, c // SUB % 2
                    if kb == 0:
                        wait(pe, b_summed, i * (2 * STEPS) + (k - L_SUM) // SUB)
                    pe.wait_ge(b_exp, K * 2 + (2 - 2 * L_SUM))
                    for n in range(NH0):
                        mm = pe.matmul(bank(7)[GK * n:GK * (n + 1), 0:QS],
                                       window[:, GK - RB - RB * kb:2 * GK - RB - RB * kb], E0[sl][:, kb, n, :],
                                       start=kb == 0, stop=kb == SUB - 1, skip_group_check=True)
                    mm.then_inc(b_sum, 1)

            def pe_b(i, subs):
                for k in subs:
                    K = i * TURN + k
                    if k % NH0 == 0 and in_range(i, k, L_MOVE):
                        pe.wait_ge(b_max, K)
                        wait(pe, b_guard, i * (TURN // NH0) + (k // NH0 - 1))
                        wait(pe, b_exp, K * 2 + (-1 - 2 * L_EXP))
                        for n in range(NH0):
                            mm = pe.matmul(bank(2)[3 * GK:P, n * P:(n + 1) * P],
                                           maxima[:, (k + n - L_MOVE) % SUB, :], identb, start=True, stop=True)
                        mm.then_inc(b_moved, 1)
                    if in_range(i, k, 0):
                        par, q, qb, n = k // (TURN // 2), k // SUB % STEPS, k // NH0 % 2, k % NH0
                        if k % (TURN // 2) == 0:
                            pe.wait_ge(k_loaded[par], i * (K_LOADS * INC) + K_LOADS * INC)
                        if q % 2 == 0 and k % SUB == 0:
                            pe.wait_ge(q_loaded[q // 2], (i * 2 + (par + 1)) * (Q_LOADS * INC))
                        wait(pe, b_max, K)
                        at = (q % 2) * QS + qb * P
                        for th in range(2):
                            mm = pe.matmul(bank(th), Q1[q // 2][0:3 * D0, n, at:at + P],
                                           half(K1[par][0:3 * D0, n, :], th), start=True, stop=True)
                        mm.then_inc(b_raw, 1)
                    if k % NH0 == 0:
                        sums_of(i, k, K)
                    for hp in range(2):
                        if in_range(i, k, L_EXP):
                            c = (k - L_EXP) % TURN
                            par, q, kb = c // (TURN // 2), c // SUB % STEPS, c % SUB
                            at = (q % 2) * QS
                            if k % NH0 == 0 and hp == 0 and in_range(i, k, L_MOVE):
                                wait(pe, b_guard, i * (TURN // NH0) + k // NH0)
                            if kb == 0 and hp == 0:
                                pe.wait_ge(b_guard, (i * (TURN // SUB) + ((k - L_EXP) // SUB + 1)) * (SUB // NH0))
                            wait(pe, b_exp, K * 2 + (hp - 1 - 2 * L_EXP))
                            for n in (2 * hp, 2 * hp + 1):
                                o = bank(2 + hp)[:, (n % 2) * QS:(n % 2 + 1) * QS]
                                pe.matmul(o, K1[par][0:3 * D0, n, kb * P:(kb + 1) * P],
                                          Q1[q // 2][0:3 * D0, n, at:at + QS], start=True, stop=False)
                                mm = pe.matmul(o, K2[par][:, n, kb * P:(kb + 1) * P],
                                               Q2[q // 2][:, n, at:at + QS], start=False, stop=True)
                            mm.then_inc(b_qk, 1)
                        if in_range(i, k, L_NORM):
                            c = (k - L_NORM) % TURN
                            if c % SUB == 0 and hp == 0:
                                wait_moved(pe, i, (k - L_NORM) // SUB)
                            wait(pe, b_norm, K * 2 + (hp - 1 - 2 * L_NORM))
                            pe.matmul(bank(4 + hp), spread[0:3 * GK, c % SUB, :],
                                      RS[c // SUB % 2][0:3 * GK, 2 * hp:2 * hp + 2, :].rearrange("p n q -> p (n q)"),
                                      start=True, stop=True).then_inc(b_spread, 1)
                    if k % NH0:
                        sums_of(i, k, K)
                    if in_range(i, k, L_PV):
                        c = (k - L_PV) % TURN
                        par, kb, sl = c // (TURN // 2), c % SUB, c // SUB % 2
                        if c % (TURN // 2) == 0:
                            pe.wait_ge(v_loaded[par], (i + (k - L_PV) // TURN) * INC + INC)
                        if kb == 0:
                            wait(pe, b_out, i * (2 * STEPS) + (k - L_PV) // SUB)
                        pe.wait_ge(b_norm, K * 2 + (2 - 2 * L_PV))
                        for n in range(NH0):
                            v = kb * P + D0 * n
                            mm = pe.matmul(bank(6)[D0 * n:D0 * (n + 1), 0:QS], V0[par][:, v:v + D0], E0[sl][:, kb, n, :],
                                           start=kb == 0, stop=kb == SUB - 1, skip_group_check=True)
                        mm.then_inc(b_pv, 1)
            turns(pe, pe_b)

            def image(ap, n, th):
                return ap[:, n, th * HALF:(th + 1) * HALF]

            def variance(squares, b, t_sem):
                for t in range(NT):
                    mm = pe.matmul(bank(b)[:, t:t + 1], squares[:, t * P:(t + 1) * P], mean_w[:, 0:1],
                                   start=True, stop=True)
                mm.then_inc(t_sem, 1)

            def widen(rows, b, t_sem):
                for t in range(NT):
                    mm = pe.matmul(bank(b, 2)[:, t * P:(t + 1) * P], sel[0:NT, t, :], rows[0:NT, :],
                                   start=True, stop=True)
                mm.then_inc(t_sem, 1)

            def project(n):
                CD.after(pe, n - 1, "xc")
                for th in range(2):
                    mm = pe.matmul(bank(th), wt("out"), image(Yall, n, th), start=True, stop=True)
                mm.then_inc(c_pe_next, 1)

            def mean_of(n):
                CX.after(pe, n, "x")
                for th in range(2):
                    mm = pe.matmul(bank(th), mean_w[:, :], image(X, n, th), start=True, stop=True)
                mm.then_inc(c_pe_next, 1)

            def queries_keys(m):
                RD.after(pe, m - 1, "n3")
                CD.after(pe, m // 2 * 2 + 1, "xn")
                pe.wait_ge(c_kept, m // 2 + 1)
                xns = [(half(xn[0], 0), xn_high)[m % 2], half(xn[1], m % 2)]
                for k in range(4):
                    for im in range(2):
                        mm = pe.matmul(bank(4 + k)[NH1 * im:NH1 * (im + 1), :],
                                       wt("qk1")[:, NH1 * k:NH1 * (k + 1)], xns[im], start=True, stop=True)
                    if k % 2:
                        mm.then_inc(r_pe, 1)

            def pe_c(i):
                for par in range(2):
                    n, m = i * 2 + par, i * 2 + (par - 2)
                    front, back = turn_parts(i)
                    if front:
                        CA.after(pe, n, "sq")
                        CA.after(pe, n - 1, "cv")
                        variance(sq, 2, c_pe)
                        if n + 1 < B:
                            project(n + 1)
                        CD.after(pe, n, "rec")
                        pe.transpose(bank(3)[0:NT, 0:P], dev, ident[:, :]).then_inc(c_pe, 1)
                        CA.after(pe, n, "turned")
                        widen(dev_t, 2, c_pe)
                        if n + 1 < B:
                            mean_of(n + 1)
                    if 0 <= m + 1 < B:
                        queries_keys(m + 1)
                    if front:
                        CD.after(pe, n, "xn")
                        for t in range(NT):
                            mm = pe.matmul(bank(2, 2)[:, t * P:(t + 1) * P], xn[par][:, t * P:(t + 1) * P], wt("v1"),
                                           start=True, stop=True)
                        mm.then_inc(c_pe, 1)
            pe.wait_ge(b_out, NSTEP)
            pe.wait_ge(f_set, 2)
            project(0)
            mean_of(0)
            turns_c(pe, pe_c)

            RD.after(pe, B - 1, "n3")

            def scores1(i, par, c):
                if c == 0:
                    pe.wait_ge(d_loaded[par], i * (2 * INC) + 2 * INC)
                wait(pe, d_exp, i * (2 * NC) + (par * NC + c - 1))
                at = UPC * ((par * NC + c) % 2)
                for h in range(HG - 1):
                    for s, j, t, n in runs(CHUNKS[c], False):
                        pe.matmul(bank(at + h)[:, s * P:(s + n) * P], Ks[par][:, h, j * P:(j + 1) * P],
                                  Qs[par][:, h, t * P:(t + n) * P], start=True, stop=True)
                h = HG - 1
                for s, (j, t) in enumerate(CHUNKS[c]):
                    mm = pe.matmul(bank(at + s)[:, UPC * P:HG * P], Ks[par][:, h, j * P:(j + 1) * P],
                                   Qs[par][:, h, t * P:(t + 1) * P], start=True, stop=True)
                mm.then_inc(d_qk, 1)

            def values1(i, par, c):
                g = i * 2 + par
                if MASKS[c]:
                    pe.wait_ge(d_mask, g * sum(MASKS) + sum(MASKS[:c + 1]))
                else:
                    pe.wait_ge(d_exp, g * NC + (c + 1))
                if c == 0:
                    pe.wait_ge(d_v, g + 1)
                    wait(pe, d_ev, g * 2 - 1)
                if c == 1:
                    wait(pe, d_ev, g * 2)
                pr = PR1[(par * NC + c) % PRING]
                for s, j, t, n in runs(CHUNKS[c], True):
                    high = t >= NT // 2
                    first = j == 0 and t in (0, NT // 2)
                    last = (j, t + n) in ((NT // 2 - 1, NT // 2), (NT - 1, NT))
                    o = bank(7 if high else 6)[:, (t - high * NT // 2) * P:(t + n - high * NT // 2) * P]
                    for h in range(HG):
                        if h < HG - 1:
                            rhs = pr[:, h * HALF + s * P:h * HALF + (s + n) * P]
                        else:
                            rhs = pr.rearrange("p (u c) -> p u c", u=UPC)[:, s:s + n, UPC * P:HG * P]
                        mm = pe.matmul(o[32 * h:32 * (h + 1), :], Vg[par][:, j, 3 * h:3 * h + 32], rhs,
                                       start=first, stop=last, skip_group_check=True)
                mm.then_inc(d_pv, 1)

            def pe_d(i, first=False, last=False):
                for k in range(2 * NC):
                    nk = k + 2
                    if nk < 2 * NC:
                        scores1(i, nk // NC, nk % NC)
                    elif not last:
                        scores1(i + 1, 0, nk - 2 * NC)
                    if k:
                        values1(i, (k - 1) // NC, (k - 1) % NC)
                    elif not first:
                        values1(i - 1, 1, NC - 1)

            scores1(0, 0, 0)
            scores1(0, 0, 1)
            pe_d(0, first=True)
            with pe.Fori(1, NG // 2 - 1) as i:
                pe_d(i)
            pe_d(NG // 2 - 1, last=True)
            values1(NG // 2 - 1, 1, NC - 1)

            pe.wait_ge(d_exp, NG * NC)
            pe.wait_ge(d_ev, 2 * NG)
            pe.wait_ge(e_set, 3)

            def divisors(n):
                par, slot = n % 2, n // 2 % 2
                pe.wait_ge(e_den, n // 2 + 1)
                EX.after(pe, n - 1, "y")
                for th in range(2):
                    mm = pe.matmul(bank(th), expand[:, par, :], half(rden[slot], th), start=True, stop=True)
                mm.then_inc(e_pe_next, 1)

            def attended(n):
                par, slot = n % 2, n // 2 % 2
                EX.after(pe, n, "y")
                EX.after(pe, n - 1, "x")
                for th in range(2):
                    mm = pe.matmul(bank(2 + th), wt("proj"), half(num[slot][par], th), start=True, stop=True)
                mm.then_inc(e_pe_next, 1)

            def attended_mean(n):
                EX.after(pe, n, "x")
                ED.after(pe, n - 1, "xc")
                for th in range(2):
                    mm = pe.matmul(bank(4 + th), mean_w[:, :], half(X[:, n, :], th), start=True, stop=True)
                mm.then_inc(e_pe_next, 1)

            divisors(0)
            attended(0)
            attended_mean(0)
            for n in range(B):
                if n + 1 < B:
                    divisors(n + 1)
                EA.after(pe, n, "sq")
                EA.after(pe, n - 1, "sd")
                ED.after(pe, n - 1, "xn")
                variance(esq, 6, e_pe)
                if n + 1 < B:
                    attended(n + 1)
                ED.after(pe, n, "rec")
                pe.transpose(bank(7)[0:NT, 0:P], edev, ident[:, :]).then_inc(e_pe, 1)
                EA.after(pe, n, "turned")
                widen(edev_t, 6, e_pe)
                if n + 1 < B:
                    attended_mean(n + 1)

            pe.wait_ge(ffn_w_loaded, FFN_LOADS * INC)
            ES.after(pe, B - 1, "sum")
            for t in range(NT):
                mm = pe.matmul(bank(0)[:, t * NE:(t + 1) * NE], xsum[:, t * P:(t + 1) * P], Wr[:, :],
                               start=True, stop=True)
            mm.then_inc(f_mm, 1)
            pe.wait_ge(f_dve, 6)
            for t in range(NT):
                mm = pe.transpose(bank(2, 2)[0:NE, t * P:(t + 1) * P], lw[:, t, :], ident[:, :])
            mm.then_inc(f_mm, 1)
            pe.wait_ge(f_dve, 7)
            for th in range(2):
                mm = pe.matmul(bank(2 + th), bo[:, :], wT[0:NE, th * HALF:(th + 1) * HALF], start=True, stop=True)
            mm.then_inc(f_mm, 1)
            for e in range(NE):
                wait(pe, f_wbA if e % 2 == 0 else f_wbV, e // 2)
                for th in range(2):
                    mm = pe.matmul(bank(4 + 2 * (e % 2) + th), sel[0:NE, e, :], wT[0:NE, th * HALF:(th + 1) * HALF],
                                   start=True, stop=True)
                mm.then_inc(f_wbps, 1)
            pe.wait_ge(f_wbA, NE // 2)
            pe.wait_ge(f_wbV, NE // 2)

            pe.wait_ge(f_dve, 8)

            def pe_f(i):
                def second(k):
                    n = i * (2 * NE) + k
                    pe.wait_ge(g_r1, n + 1)
                    wait(pe, g_r2, n - 1)
                    pe.matmul(bank(2 + k % 2), W2[:, k % NE, :], h1[k % 2], start=True, stop=True).then_inc(g_h2, 1)

                def third(k):
                    n, th, e = i * (2 * NE) + k, k // NE, k % NE
                    pe.wait_ge(g_w, n + 1)
                    if e == 0:
                        wait(pe, g_res, i * 2 + (th - 1))
                    pe.matmul(bank(4 + th), Wo[:, e, :], h2w[k % 2], start=e == 0, stop=e == NE - 1).then_inc(g_y3, 1)
                for k in range(2 * NE):
                    n = i * (2 * NE) + k
                    wait(pe, g_r1, n - 1)
                    th = k // NE
                    pe.matmul(bank(k % 2), W1[:, k % NE, :],
                              Yall[:, ds(i, 1), th * HALF:(th + 1) * HALF].rearrange("p o t -> p (o t)"),
                              start=True, stop=True).then_inc(g_h1, 1)
                    if k >= 1:
                        second(k - 1)
                    if k >= 2:
                        third(k - 2)
                second(2 * NE - 1)
                third(2 * NE - 2)
                third(2 * NE - 1)
            peeled(pe, B, pe_f)

        @block.vector
        def _(dve):
            dve.wait_ge(w_turned, 2)
            dve.tensor_copy(PT[:, :], bank(2)[:, 0:NPR]).then_inc(param_step, 1)
            dve.wait_ge(param_step, 1)
            dve.tensor_scalar(cv(c_sd, NE), param("L1_ffn_v1"), BN_EPS, None, ALU.add).then_inc(param_step, 1)
            dve.tensor_scalar(cv(c_sd + NE, NE), param("L1_ffn_v2"), BN_EPS, None, ALU.add)
            dve.tensor_scalar(cv(c_sd + 2 * NE), param("L0_conv_bn_var"), BN_EPS0, None, ALU.add)\
                .then_inc(param_step, 1)
            step = [3]

            def chain(ins):
                step[0] += 1
                ins.then_inc(param_step, 1)
                dve.wait_ge(param_step, step[0])

            dve.wait_ge(param_sd, 1)
            dve.wait_ge(param_step, 3)
            chain(dve.reciprocal(cv(c_sd, 17), cv(c_sd, 17)))
            for c_A, c_B, k in ((c_A1, c_B1, "1"), (c_A2, c_B2, "2")):
                at = c_sd + NE * (k == "2")
                chain(dve.tensor_tensor(cv(c_A, NE), param("L1_ffn_g" + k), cv(at, NE), ALU.mult))
                chain(dve.tensor_tensor(cv(c_B, NE), param("L1_ffn_b" + k), param("L1_ffn_m" + k), ALU.subtract))
                chain(dve.tensor_tensor(cv(c_B, NE), cv(c_B, NE), cv(c_A, NE), ALU.mult))
                chain(dve.tensor_tensor(cv(c_B, NE), cv(c_B, NE), param("L1_ffn_be" + k), ALU.add))
            chain(dve.tensor_tensor(cv(c_scale0), param("L0_conv_bn_gamma"), cv(c_sd + 2 * NE), ALU.mult))
            chain(dve.tensor_tensor(cv(c_scale0), cv(c_scale0), param("L0_conv_dw_w"), ALU.mult))
            chain(dve.tensor_tensor(cv(c_bias0), param("L0_conv_bn_beta"), param("L0_conv_dw_w"), ALU.mult))
            chain(dve.tensor_tensor(cv(c_t), param("L0_conv_bn_mean"), cv(c_scale0), ALU.mult))
            chain(dve.tensor_tensor(cv(c_bias0), cv(c_bias0), cv(c_t), ALU.subtract))
            chain(dve.tensor_scalar(cv(c_wq, 2), qkw[:, 0:2], SCALE1, None, ALU.mult))
            chain(dve.scalar_tensor_tensor(cv(c_ck, 2), qkw[:, 2:4], -1.0, qkw[:, 2:4], ALU.mult, ALU.max))
            chain(dve.tensor_scalar(cv(c_ck, 2), cv(c_ck, 2), 2.0 ** 0.5, None, ALU.mult))

            def dve_a(i):
                for par in range(2):
                    b = i * 2 + par
                    wait(dve, a_mm, b * 3 - 3)
                    dve.tensor_scalar(xbn[par], X[:, ds(b, 1), :].rearrange("p o t -> p (o t)"), cv(c_scale0),
                                      cv(c_bias0), ALU.mult, ALU.add).then_inc(a_bn, 1)
                    for k in range(2):
                        dve.wait_ge(a_hi, b * 5 + (k + 1))
                        wait(dve, a_lo, b * 2 + (k - 1))
                        dve.tensor_tensor(rest0[k], bank(2 * k, 2), parts[par][:, 3 * k, :],
                                          ALU.subtract).then_inc(a_rest, 1)
            dve.wait_ge(x_loaded_first, INC)
            dve_a(0)
            dve.wait_ge(x_loaded_rest, INC)
            with dve.Fori(1, B // 2) as i:
                dve_a(i)

            def dve_b(i, subs):
                for k in subs:
                    K = i * TURN + k
                    if in_range(i, k, 0):
                        dve.wait_ge(b_raw, K + 1)
                        wait(dve, b_moved, i * (TURN // NH0) + (k // NH0 - 1))
                        dve.reduce_max(maxima[:, k % SUB, :], bank(0, 2).rearrange("p (y x) -> p y x", x=GK), AX_X)\
                            .then_inc(b_max, 1)
                    if in_range(i, k, L_NORM):
                        c = (k - L_NORM) % TURN
                        for hp in range(2):
                            e = E0[c // SUB % 2][:, c % SUB, 2 * hp:2 * hp + 2, :].rearrange("p n q -> p (n q)")
                            dve.wait_ge(b_spread, K * 2 + (hp + 1 - 2 * L_NORM))
                            dve.tensor_tensor(e, e, bank(4 + hp), ALU.mult).then_inc(b_norm, 1)
                    if k % SUB == 2 and in_range(i, k, L_SUM + SUB):
                        g = i * (2 * STEPS) + (k - L_SUM - SUB) // SUB
                        dve.wait_ge(b_summed, g + 1)
                        wait(dve, b_rrest, g)
                        dve.reciprocal(rec, sums).then_inc(b_rec, 1)
                    if k % SUB == 3 and in_range(i, k, L_SUM + SUB + 1):
                        g = i * (2 * STEPS) + (k - L_SUM - SUB - 1) // SUB
                        dve.wait_ge(b_rhi, g + 1)
                        wait(dve, b_rlo, g)
                        dve.tensor_tensor(rec_rest, rec, rec_parts[:, 0, :], ALU.subtract).then_inc(b_rrest, 1)
            turns(dve, dve_b)

            dve.wait_ge(b_out, NSTEP)

            def residual(n):
                CN.after(dve, n, "z")
                dve.scalar_tensor_tensor(X[:, n, :], bank(0, 2), param("L0_conv_out_b"), X[:, n, :],
                                         ALU.add, ALU.add).then_inc(c_dve_next, 1)

            def dve_c(i):
                for par in range(2):
                    n, m = i * 2 + par, i * 2 + (par - 2)
                    front, back = turn_parts(i)
                    q0, q1, k0, k1, guard = nrm
                    if front:
                        CN.after(dve, n, "mean")
                        CD.after(dve, n - 2, "xn")
                        dve.tensor_tensor(xc[par], X[:, n, :], bank(0, 2), ALU.subtract).then_inc(c_dve, 1)
                    if n == B:
                        CN.after(dve, B - 1, "z")
                        dve.memset(Ks[0], -1.0).then_inc(d_init_k, 1)
                    if n == B + 1:
                        dve.memset(Qs[1], 0.0).then_inc(d_init_k, 1)
                    if back:
                        for k in range(2):
                            RA.after(dve, m, f"sd{k}")
                            dve.reciprocal(ss[k], ss[k]).then_inc(r_dve, 1)
                    if front:
                        CA.after(dve, n, "sd")
                        dve.reciprocal(dev, dev).then_inc(c_dve, 1)
                    if back:
                        RA.after(dve, m - 1, "hi4")
                        RD.after(dve, m - 1, "rest4")
                        for k in range(4):
                            RD.after(dve, m, ("rq", "rk")[k // 2])
                            w = cv(c_wq + k) if k < 2 else qkw[:, k:k + 1]
                            dve.scalar_tensor_tensor(nrm[k], bank(4 + k), w, ss[k // 2], ALU.mult, ALU.mult)\
                                .then_inc(r_dve, 1)
                    if front:
                        if n + 1 < B:
                            residual(n + 1)
                        CP.after(dve, n, "wide")
                        RP.after(dve, m, "k")
                        if par == 0:
                            wait(dve, c_kept, i)
                        dve.tensor_tensor(xn[par], xc[par], bank(2, 2), ALU.mult).then_inc(c_dve, 1)
                    if back:
                        def rest(k):
                            RA.after(dve, m, f"hi{k}")
                            RG.after(dve, m - 1, f"lo{k}")
                            dve.tensor_tensor(rst[k], nrm[k], planes[par][:, hi_plane(k), :], ALU.subtract)\
                                .then_inc(r_dve, 1)
                        for k in range(4):
                            rest(k)
                        RG.after(dve, m, "own")
                        dve.scalar_tensor_tensor(guard, tmp[2], GUARD, tmp[0], ALU.add, ALU.min).then_inc(r_dve, 1)
                        rest(4)
            residual(0)
            turns_c(dve, dve_c)

            CP.after(dve, B - 1, "val")
            RP.after(dve, B - 1, "k")
            dve.memset(Ks[1], -1.0).then_inc(d_init_k, 1)
            for s in range(2):
                dve.memset(Vg[s], 0.0).then_inc(d_vinit, 1)

            def copy_out(i, par, hh):
                g = i * 2 + par
                if hh == 0:
                    wait(dve, d_stored[par], i * (HG * INC))
                    dve.wait_ge(d_pv, g * NC + (CHUNK_A + 1))
                else:
                    dve.wait_ge(d_pv, g * NC + NC)
                dve.tensor_copy(half(Oe[par], hh), bank(6 + hh)).then_inc(d_ev, 1)

            def dve_d(i):
                for par in range(2):
                    for c in range(NC):
                        if MASKS[c]:
                            dve.wait_ge(d_exp, i * (2 * NC) + (par * NC + c + 1))
                            pr = PR1[(par * NC + c) % PRING]
                            for s, (j, t) in enumerate(CHUNKS[c]):
                                if j == t:
                                    v = pr.rearrange("p (h c) -> p h c", h=UPC)[:, :, s * P:(s + 1) * P]
                                    m3 = causal[:, :].rearrange("p (o t) -> p o t", o=1).to_broadcast([P, UPC, P])
                                    dve.tensor_tensor(v, v, m3, ALU.min).then_inc(d_mask, 1)
                                    v = pr[:, s * HALF + UPC * P:(s + 1) * HALF]
                                    dve.tensor_tensor(v, v, causal[:, :], ALU.min).then_inc(d_mask, 1)
                        if c == 0:
                            if par == 1:
                                copy_out(i, 0, 1)
                            elif not (isinstance(i, int) and i == 0):
                                copy_out(i - 1, 1, 1)
                        if c == CHUNK_A + 2:
                            copy_out(i, par, 0)
            peeled(dve, NG // 2, dve_d)
            copy_out(NG // 2 - 1, 1, 1)

            def summed(n):
                ED.after(dve, n, "xn")
                ES.after(dve, n - 1, "sum")
                if n == 0:
                    dve.tensor_copy(xsum, Yall[:, n, :]).then_inc(e_sum, 1)
                else:
                    dve.tensor_tensor(xsum, xsum, Yall[:, n, :], ALU.add).then_inc(e_sum, 1)

            def reciprocal_of(i):
                dve.wait_ge(e_loaded[i % 2], (i // 2 + 1) * 5 * INC)
                EN.after(dve, 2 * i - 3, "den")
                dve.reciprocal(rden[i % 2], den[i % 2]).then_inc(e_den, 1)

            def added(n):
                y = num[n // 2 % 2][n % 2]
                EN.after(dve, n, "den")
                dve.tensor_tensor(y, y, bank(0, 2), ALU.mult).then_inc(e_dve_next, 1)
                if n % 2 == 1 and n + 1 < B:
                    reciprocal_of(n // 2 + 1)

            def joined(n):
                EN.after(dve, n, "z")
                dve.tensor_tensor(X[:, n, :], X[:, n, :], bank(2, 2), ALU.add).then_inc(e_dve_next, 1)

            reciprocal_of(0)
            added(0)
            joined(0)
            for n in range(B):
                EN.after(dve, n, "mean")
                ED.after(dve, n - 2, "xn")
                dve.tensor_tensor(exc[n % 2], X[:, n, :], bank(4, 2), ALU.subtract).then_inc(e_dve, 1)
                if n + 1 < B:
                    added(n + 1)
                EA.after(dve, n, "sd")
                dve.reciprocal(edev, edev).then_inc(e_dve, 1)
                if n + 1 < B:
                    joined(n + 1)
                EP.after(dve, n, "wide")
                if n == 0:
                    for par in range(2):
                        dve.wait_ge(d_stored[par], NG // 2 * HG * INC)
                dve.tensor_tensor(Yall[:, n, :], exc[n % 2], bank(6, 2), ALU.mult).then_inc(e_dve, 1)
                if n:
                    summed(n - 1)
            summed(B - 1)

            def per_token(ap):
                return ap.rearrange("p (t o) -> p t o", o=1).to_broadcast([P, NT, NE])
            dve.wait_ge(f_mm, 1)
            dve.scalar_tensor_tensor(lg, bank(0)[:, 0:NT * NE].rearrange("p (t e) -> p t e", e=NE), 1.0 / B,
                                     br_b[:, :].rearrange("p (o e) -> p o e", o=1).to_broadcast([P, NT, NE]),
                                     ALU.mult, ALU.add).then_inc(f_dve, 1)
            dve.wait_ge(f_dve, 1)
            dve.reduce_max(lm, lg, AX_X).then_inc(f_dve, 1)
            dve.wait_ge(f_dve, 2)
            dve.tensor_tensor(lg, lg, per_token(lm), ALU.subtract).then_inc(f_dve, 1)
            dve.wait_ge(f_exp, 1)
            dve.reduce_sum(lm, lw, AX_X).then_inc(f_dve, 1)
            dve.wait_ge(f_dve, 4)
            dve.reciprocal(lm, lm).then_inc(f_dve, 1)
            dve.wait_ge(f_dve, 5)
            dve.tensor_tensor(lw, lw, per_token(lm), ALU.mult).then_inc(f_dve, 1)
            dve.wait_ge(f_mm, 2)
            dve.tensor_copy(wT[0:NE, :], bank(2, 2)[0:NE, :]).then_inc(f_dve, 1)
            dve.wait_ge(f_mm, 3)
            dve.tensor_copy(bias_w, bank(2, 2)).then_inc(f_dve, 1)
            for e in range(1, NE, 2):
                dve.wait_ge(f_wbps, e + 1)
                dve.tensor_copy(wB[:, e, :], bank(6, 2)).then_inc(f_wbV, 1)

            def dve_f(i):
                def result(th):
                    dve.wait_ge(g_y3, (i * 2 + (th + 1)) * NE)
                    dve.wait_ge(f_biased, i + 1)
                    wait(dve, out_stored[th], i * INC)
                    dve.tensor_tensor(res[th], bank(4 + th),
                                      X[:, ds(i, 1), th * HALF:(th + 1) * HALF].rearrange("p o t -> p (o t)"),
                                      ALU.add).then_inc(g_res, 1)
                for k in range(2 * NE):
                    n, th, e = i * (2 * NE) + k, k // NE, k % NE
                    dve.wait_ge(g_r2, n + 1)
                    wait(dve, g_y3, n - 1)
                    dve.tensor_tensor(h2w[k % 2], h2[k % 2], half(wB[:, e, :], th), ALU.mult).then_inc(g_w, 1)
                    if k == NE + 2:
                        result(0)
                result(1)
            dve.wait_ge(f_wbA, NE // 2)
            dve.wait_ge(f_wbV, NE // 2)
            peeled(dve, B, dve_f)


_INS = ["x"] + VECTORS[:5] + ["L0_conv_pw_w", "L0_conv_out_w", "L0_conv_out_b", "L1_attn_w_qkv", "L1_attn_w_proj",
        "L1_attn_qn_w", "L1_attn_kn_w", "L1_ffn_Wr", "L1_ffn_br", "L1_ffn_W1", "L1_ffn_W2", "L1_ffn_Wo",
        "L1_ffn_bo"] + PARAMS


def kernel(**inputs):
    import numpy as _np
    import concourse.bacc as _bacc
    from concourse import mybir as _mybir
    from concourse.bass_utils import run_bass_kernel_spmd as _run

    nc = _bacc.Bacc("TRN2", target_bir_lowering=False, num_devices=1)
    arrays, aps = {}, {}
    for name in _INS:
        a = _np.ascontiguousarray(inputs[name])
        arrays[f"in_{name}"] = a
        aps[name] = nc.dram_tensor(f"in_{name}", a.shape, _mybir.dt.from_np(a.dtype), kind="ExternalInput").ap()
    out = nc.dram_tensor("out_0", (B, P, H, W), _mybir.dt.float32, kind="ExternalOutput").ap()
    hybrid_kernel(nc, aps, out)
    r = _run(nc, [arrays], core_ids=[0])
    return r.results[0]["out_0"]
```
